# Optimizing a Trainium2 kernel written in Bass

```python
import numpy as np
import jax
import jax.numpy as jnp

def _softmax(x, axis=-1):
    return jax.nn.softmax(x, axis=axis)

def _gelu(x):
    return jax.nn.gelu(x, approximate=True)

def _silu(x):
    return jax.nn.silu(x)

def _sigmoid(x):
    return jax.nn.sigmoid(x)

def _layernorm(x, axis=-1, eps=1e-05):
    m = jnp.mean(x, axis=axis, keepdims=True)
    v = jnp.var(x, axis=axis, keepdims=True)
    return (x - m) / jnp.sqrt(v + eps)

def _scatter_add(tgt, idx, src, axis=0):
    return tgt.at[idx].add(src)

def _segment_sum(src, seg, n):
    return jax.ops.segment_sum(src, seg, n)
kernel_name = 'mk_prb_d2_jaxref_r8_0aa1d8'

def setup_inputs(seed: int=0):
    np.random.seed(seed)
    _w = jnp.asarray

    def _L0_attn_setup():
        import jax, jax.numpy as jnp
        import numpy as np
        B, S, D = (2, 512, 256)
        LN_EPS = 1e-05
        key = jax.random.key(seed)
        ks = jax.random.split(key, 4)
        s = 0.02
        return {'hidden_states': jax.random.normal(ks[0], (B, S, D), jnp.float32), 'attention_mask': jnp.ones((B, S), jnp.int32), 'ln_g': jnp.ones((D,), jnp.float32), 'ln_b': jnp.zeros((D,), jnp.float32), 'Wq': jax.random.normal(ks[1], (D, D), jnp.float32) * s, 'bq': jnp.zeros((D,), jnp.float32), 'Wqa': jnp.zeros((D, D), jnp.float32), 'bqa': jnp.ones((D,), jnp.float32), 'Wk': jax.random.normal(ks[2], (D, D), jnp.float32) * s, 'bk': jnp.zeros((D,), jnp.float32), 'Wka': jnp.zeros((D, D), jnp.float32), 'bka': jnp.ones((D,), jnp.float32), 'Wv': jax.random.normal(ks[3], (D, D), jnp.float32) * s, 'bv': jnp.zeros((D,), jnp.float32)}
    _L0_attn_in = _L0_attn_setup()

    def _L0_ffn_setup():
        import jax, jax.numpy as jnp
        import numpy as np
        HIDDEN = 256
        INTER = 688
        LUT_SIZE = 16

        def _ghost_linear(x, idx, lut):
            w = lut[idx]
            return jnp.einsum('bsh,oh->bso', x, w)
        key = jax.random.key(seed)
        k_x, k_lut, k_g, k_u, k_d = jax.random.split(key, 5)
        x = jax.random.normal(k_x, (2, 512, HIDDEN), dtype=jnp.float32)
        lut = jax.random.normal(k_lut, (LUT_SIZE,), dtype=jnp.float32) * 0.02
        gate_idx = jax.random.randint(k_g, (INTER, HIDDEN), 0, LUT_SIZE, dtype=jnp.int32)
        up_idx = jax.random.randint(k_u, (INTER, HIDDEN), 0, LUT_SIZE, dtype=jnp.int32)
        down_idx = jax.random.randint(k_d, (HIDDEN, INTER), 0, LUT_SIZE, dtype=jnp.int32)
        return {'x': x, 'lut': lut, 'gate_idx': gate_idx, 'up_idx': up_idx, 'down_idx': down_idx}
    _L0_ffn_in = _L0_ffn_setup()

    def _L1_attn_setup():
        import jax, jax.numpy as jnp
        import numpy as np
        import math
        EMBED_DIM = 256
        NUM_HEADS = 16
        HEAD_DIM = EMBED_DIM // NUM_HEADS
        BATCH = 4
        SEQ = 256
        key = jax.random.key(seed)
        ks = jax.random.split(key, 5)
        scale_qkv = 1.0 / math.sqrt(EMBED_DIM)
        x = jax.random.normal(ks[0], (BATCH, SEQ, EMBED_DIM), dtype=jnp.float32)
        w_qkv = jax.random.normal(ks[1], (3 * EMBED_DIM, EMBED_DIM), dtype=jnp.float32) * scale_qkv
        b_qkv = jnp.zeros((3 * EMBED_DIM,), dtype=jnp.float32)
        w_o = jax.random.normal(ks[2], (EMBED_DIM, EMBED_DIM), dtype=jnp.float32) * scale_qkv
        b_o = jnp.zeros((EMBED_DIM,), dtype=jnp.float32)
        return {'x': x, 'w_qkv': w_qkv, 'b_qkv': b_qkv, 'w_o': w_o, 'b_o': b_o}
    _L1_attn_in = _L1_attn_setup()

    def _L1_ffn_setup():
        import jax, jax.numpy as jnp
        import numpy as np
        N_EXPERTS = 8
        TOP_K = 2
        N_GROUP = 4
        TOPK_GROUP = 2
        ROUTED_SCALE = 1.0

        def _group_limited_topk(scores):
            T, N = scores.shape
            E = N // N_GROUP
            group_scores = scores.reshape(T, N_GROUP, E).max(axis=-1)
            _, gidx = jax.lax.top_k(group_scores, TOPK_GROUP)
            gmask = jax.nn.one_hot(gidx, N_GROUP, dtype=scores.dtype).sum(1)
            smask = jnp.repeat(gmask, E, axis=1)
            masked = jnp.where(smask > 0, scores, jnp.zeros((), scores.dtype))
            topk_w, topk_i = jax.lax.top_k(masked, TOP_K)
            return (topk_w, topk_i)
        key = jax.random.key(seed)
        ks = jax.random.split(key, 8)
        B, S, H, F, FS, N = (2, 128, 256, 176, 352, N_EXPERTS)
        std = jnp.float32(0.02)
        return {'hidden_states': jax.random.normal(ks[0], (B, S, H), jnp.float32), 'gate_weight': jax.random.normal(ks[1], (N, H), jnp.float32) * std, 'gate_w': jax.random.normal(ks[2], (N, F, H), jnp.float32) * std, 'up_w': jax.random.normal(ks[3], (N, F, H), jnp.float32) * std, 'down_w': jax.random.normal(ks[4], (N, H, F), jnp.float32) * std, 'sh_gate_w': jax.random.normal(ks[5], (FS, H), jnp.float32) * std, 'sh_up_w': jax.random.normal(ks[6], (FS, H), jnp.float32) * std, 'sh_down_w': jax.random.normal(ks[7], (H, FS), jnp.float32) * std}
    _L1_ffn_in = _L1_ffn_setup()
    _d = {'L0_attn_hidden_states': _L0_attn_in['hidden_states'], 'L0_attn_attention_mask': _L0_attn_in['attention_mask'], 'L0_attn_ln_g': _L0_attn_in['ln_g'], 'L0_attn_ln_b': _L0_attn_in['ln_b'], 'L0_attn_Wq': _L0_attn_in['Wq'], 'L0_attn_bq': _L0_attn_in['bq'], 'L0_attn_Wqa': _L0_attn_in['Wqa'], 'L0_attn_bqa': _L0_attn_in['bqa'], 'L0_attn_Wk': _L0_attn_in['Wk'], 'L0_attn_bk': _L0_attn_in['bk'], 'L0_attn_Wka': _L0_attn_in['Wka'], 'L0_attn_bka': _L0_attn_in['bka'], 'L0_attn_Wv': _L0_attn_in['Wv'], 'L0_attn_bv': _L0_attn_in['bv'], 'L0_ffn_lut': _L0_ffn_in['lut'], 'L0_ffn_gate_idx': _L0_ffn_in['gate_idx'], 'L0_ffn_up_idx': _L0_ffn_in['up_idx'], 'L0_ffn_down_idx': _L0_ffn_in['down_idx'], 'L1_attn_w_qkv': _L1_attn_in['w_qkv'], 'L1_attn_b_qkv': _L1_attn_in['b_qkv'], 'L1_attn_w_o': _L1_attn_in['w_o'], 'L1_attn_b_o': _L1_attn_in['b_o'], 'L1_ffn_gate_weight': _L1_ffn_in['gate_weight'], 'L1_ffn_gate_w': _L1_ffn_in['gate_w'], 'L1_ffn_up_w': _L1_ffn_in['up_w'], 'L1_ffn_down_w': _L1_ffn_in['down_w'], 'L1_ffn_sh_gate_w': _L1_ffn_in['sh_gate_w'], 'L1_ffn_sh_up_w': _L1_ffn_in['sh_up_w'], 'L1_ffn_sh_down_w': _L1_ffn_in['sh_down_w']}
    _x0 = _d['L0_attn_hidden_states']
    _d['L0_attn_hidden_states'] = jax.random.normal(jax.random.fold_in(jax.random.key(seed), 1), (4, 1024, 256), dtype=_x0.dtype)
    del _x0
    return _d

def reference(L0_attn_hidden_states, L0_attn_attention_mask, L0_attn_ln_g, L0_attn_ln_b, L0_attn_Wq, L0_attn_bq, L0_attn_Wqa, L0_attn_bqa, L0_attn_Wk, L0_attn_bk, L0_attn_Wka, L0_attn_bka, L0_attn_Wv, L0_attn_bv, L0_ffn_lut, L0_ffn_gate_idx, L0_ffn_up_idx, L0_ffn_down_idx, L1_attn_w_qkv, L1_attn_b_qkv, L1_attn_w_o, L1_attn_b_o, L1_ffn_gate_weight, L1_ffn_gate_w, L1_ffn_up_w, L1_ffn_down_w, L1_ffn_sh_gate_w, L1_ffn_sh_up_w, L1_ffn_sh_down_w):

    def _L0_attn_ref(hidden_states, attention_mask, ln_g, ln_b, Wq, bq, Wqa, bqa, Wk, bk, Wka, bka, Wv, bv):
        import jax, jax.numpy as jnp
        import numpy as np
        B, S, D = (2, 512, 256)
        LN_EPS = 1e-05
        mu = jnp.mean(hidden_states, axis=-1, keepdims=True)
        var = jnp.var(hidden_states, axis=-1, keepdims=True)
        h = (hidden_states - mu) * jax.lax.rsqrt(var + LN_EPS) * ln_g + ln_b
        lin = lambda x, W, b: x @ W.T + b
        scale = 1.0 / jnp.sqrt(jnp.float32(D))
        query = lin(h, Wq, bq)
        keys = lin(h, Wk, bk)
        values = lin(h, Wv, bv)
        qw = jnp.exp(lin(query, Wqa, bqa) * scale)
        qw = qw / jnp.cumsum(qw, axis=1)
        pooled_query = jnp.cumsum(qw * query, axis=1)
        mixed_keys = pooled_query * keys
        kw = jnp.exp(lin(mixed_keys, Wka, bka) * scale)
        kw = kw / jnp.cumsum(kw, axis=1)
        pooled_keys = jnp.cumsum(kw * mixed_keys, axis=1)
        return pooled_keys * values

    def _L0_ffn_ref(x, lut, gate_idx, up_idx, down_idx):
        import jax, jax.numpy as jnp
        import numpy as np
        HIDDEN = 256
        INTER = 688
        LUT_SIZE = 16

        def _ghost_linear(x, idx, lut):
            w = lut[idx]
            return jnp.einsum('bsh,oh->bso', x, w)
        gate = _ghost_linear(x, gate_idx, lut)
        up = _ghost_linear(x, up_idx, lut)
        h = jax.nn.silu(gate) * up
        return _ghost_linear(h, down_idx, lut)

    def _L1_attn_ref(x, w_qkv, b_qkv, w_o, b_o):
        import jax, jax.numpy as jnp
        import numpy as np
        import math
        EMBED_DIM = 256
        NUM_HEADS = 16
        HEAD_DIM = EMBED_DIM // NUM_HEADS
        BATCH = 4
        SEQ = 256
        B, S, D = x.shape
        qkv = jnp.einsum('bsd,ed->bse', x, w_qkv) + b_qkv
        qkv = qkv.reshape(B, S, 3, NUM_HEADS, HEAD_DIM)
        qkv = jnp.transpose(qkv, (2, 0, 3, 1, 4))
        q, k, v = (qkv[0], qkv[1], qkv[2])
        scores = jnp.einsum('bhqd,bhkd->bhqk', q, k) / math.sqrt(HEAD_DIM)
        probs = jax.nn.softmax(scores, axis=-1)
        out = jnp.einsum('bhqk,bhkd->bhqd', probs, v)
        out = jnp.transpose(out, (0, 2, 1, 3)).reshape(B, S, D)
        return jnp.einsum('bsd,ed->bse', out, w_o) + b_o

    def _L1_ffn_ref(hidden_states, gate_weight, gate_w, up_w, down_w, sh_gate_w, sh_up_w, sh_down_w):
        import jax, jax.numpy as jnp
        import numpy as np
        N_EXPERTS = 8
        TOP_K = 2
        N_GROUP = 4
        TOPK_GROUP = 2
        ROUTED_SCALE = 1.0

        def _group_limited_topk(scores):
            T, N = scores.shape
            E = N // N_GROUP
            group_scores = scores.reshape(T, N_GROUP, E).max(axis=-1)
            _, gidx = jax.lax.top_k(group_scores, TOPK_GROUP)
            gmask = jax.nn.one_hot(gidx, N_GROUP, dtype=scores.dtype).sum(1)
            smask = jnp.repeat(gmask, E, axis=1)
            masked = jnp.where(smask > 0, scores, jnp.zeros((), scores.dtype))
            topk_w, topk_i = jax.lax.top_k(masked, TOP_K)
            return (topk_w, topk_i)
        B, S, H = hidden_states.shape
        h = hidden_states.reshape(-1, H)
        logits = h.astype(jnp.float32) @ gate_weight.astype(jnp.float32).T
        scores = jax.nn.softmax(logits, axis=-1)
        topk_w, topk_i = _group_limited_topk(scores)
        topk_w = (topk_w * ROUTED_SCALE).astype(h.dtype)
        wmat = (jax.nn.one_hot(topk_i, N_EXPERTS, dtype=topk_w.dtype) * topk_w[..., None]).sum(axis=1)
        g = jnp.einsum('th,nfh->ntf', h, gate_w)
        u = jnp.einsum('th,nfh->ntf', h, up_w)
        e = jnp.einsum('ntf,nhf->nth', jax.nn.silu(g) * u, down_w)
        routed = jnp.einsum('nth,tn->th', e, wmat)
        sg = h @ sh_gate_w.T
        su = h @ sh_up_w.T
        shared = jax.nn.silu(sg) * su @ sh_down_w.T
        return (routed + shared).reshape(B, S, H)
    x = L0_attn_hidden_states
    xn = _layernorm(x, axis=-1)
    x = x + _L0_attn_ref(xn, L0_attn_attention_mask, L0_attn_ln_g, L0_attn_ln_b, L0_attn_Wq, L0_attn_bq, L0_attn_Wqa, L0_attn_bqa, L0_attn_Wk, L0_attn_bk, L0_attn_Wka, L0_attn_bka, L0_attn_Wv, L0_attn_bv) + _L0_ffn_ref(xn, L0_ffn_lut, L0_ffn_gate_idx, L0_ffn_up_idx, L0_ffn_down_idx)
    xn = _layernorm(x, axis=-1)
    x = x + _L1_attn_ref(xn, L1_attn_w_qkv, L1_attn_b_qkv, L1_attn_w_o, L1_attn_b_o) + _L1_ffn_ref(xn, L1_ffn_gate_weight, L1_ffn_gate_w, L1_ffn_up_w, L1_ffn_down_w, L1_ffn_sh_gate_w, L1_ffn_sh_up_w, L1_ffn_sh_down_w)
    return x

_drawn_inputs = setup_inputs


def setup_inputs(seed=0):
    import zlib

    import numpy as np

    out = dict(_drawn_inputs(seed))
    spreads = {'L0_attn_ln_g': (1.0, 0.2),
     'L0_attn_ln_b': (0.0, 0.1),
     'L0_attn_bq': (0.0, 0.1),
     'L0_attn_Wqa': (0.0, 0.8),
     'L0_attn_bqa': (1.0, 0.6),
     'L0_attn_bk': (0.0, 0.1),
     'L0_attn_Wka': (0.0, 0.8),
     'L0_attn_bka': (1.0, 0.6),
     'L0_attn_bv': (0.0, 0.1),
     'L1_attn_b_qkv': (0.0, 0.516),
     'L1_attn_b_o': (0.0, 0.556)}
    factors = {'L1_ffn_gate_weight': 8.0,
     'L1_ffn_gate_w': 8.0,
     'L1_ffn_up_w': 8.0,
     'L1_ffn_down_w': 8.0,
     'L1_ffn_sh_gate_w': 3.041,
     'L1_ffn_sh_up_w': 3.006,
     'L1_ffn_sh_down_w': 3.008}
    for name, (base, spread) in spreads.items():
        noise = np.random.default_rng([zlib.crc32(name.encode()), seed]).standard_normal(out[name].shape)
        drawn = base * np.exp(spread * noise) if base else spread * noise
        out[name] = jnp.asarray(drawn.astype(out[name].dtype))
    for name, factor in factors.items():
        out[name] = (out[name] * factor).astype(out[name].dtype)
    return out
```

```python
from contextlib import ExitStack

import concourse.bass as bass
from concourse import mybir

F32 = mybir.dt.float32
F32R = mybir.dt.float32r
BF16 = mybir.dt.bfloat16
I32 = mybir.dt.int32
ALU = mybir.AluOpType
ACT = mybir.ActivationFunctionType
AX = mybir.AxisListType

P = 128
B, S, D = 4, 1024, 256
KD = D // P
BLK = 512
NB = B * S // BLK
TT = BLK // P
NT = B * S // P
EPS = 1e-5
SCALE0 = 1.0 / D ** 0.5

F0 = 688
C0 = 6
F0C = [116] * 5 + [F0 - 5 * 116]
LUT = 16
FLAT0 = 4 * F0 + C0 * D
LC = 480
NLC = -(-FLAT0 // LC)

WQ, WK, WV, WQA, WKA = range(5)

H, HD = 16, D // 16
NX, FX, FS = 8, 176, 352
F1 = NX * FX + FS
CX = NX * FX // P
F1C = [P] * CX + [120, 120, 112]
C1 = len(F1C)
PART = 3
VW = 32
LANE = 32


def wait(eng, sem, value):
    if not isinstance(value, int) or value > 0:
        eng.wait_ge(sem, value)


def split3(pe, out, w_hi, w_lo, x_hi, x_lo, first, last):
    pe.matmul(out, w_hi, x_hi, start=first, stop=False, skip_group_check=True)
    pe.matmul(out, w_lo, x_hi, start=False, stop=False, skip_group_check=True)
    return pe.matmul(out, w_hi, x_lo, start=False, stop=last, skip_group_check=True)


def layer_norm_stats(nc, sem, x_sb, mean, var, raw, name):
    rows_done, done = sem(f"{name}_rows_done"), sem(f"{name}_stats_done")
    stats, work = raw
    steps = 6

    def run(dve):
        with dve.Fori(0, NB) as n:
            for j in range(TT):
                t = bass.ds(n * TT + j, 1)
                dve.bn_stats(stats[:, t, :], x_sb[:, t, :]).then_inc(rows_done, 1)
        mean_e, mean_o = stats[:, :, 1], stats[:, :, 4]
        dve.wait_ge(rows_done, NT)
        dve.tensor_tensor(work[:, 0, :], mean_e, mean_o, ALU.add).then_inc(done, 1)
        dve.tensor_tensor(work[:, 1, :], mean_e, mean_o, ALU.subtract).then_inc(done, 1)
        dve.tensor_tensor(work[:, 2, :], stats[:, :, 2], stats[:, :, 5], ALU.add).then_inc(done, 1)
        dve.wait_ge(done, 1)
        dve.tensor_scalar(mean[:], work[:, 0, :], 0.5, None, ALU.mult).then_inc(done, 1)
        dve.wait_ge(done, 2)
        dve.scalar_tensor_tensor(work[:, 3, :], work[:, 1, :], 0.25, work[:, 1, :], ALU.mult, ALU.mult).then_inc(done, 1)
        dve.wait_ge(done, 5)
        dve.scalar_tensor_tensor(var[:], work[:, 2, :], 1.0 / D, work[:, 3, :], ALU.mult, ALU.add).then_inc(done, 1)
        dve.wait_ge(done, steps)
    return run, (done, steps)


def build(nc, a, out, stop_after=None):
    with ExitStack() as whole:
        def persistent(name, shape, dt, ctx=whole):
            return ctx.enter_context(nc.sbuf_tensor(name, shape, dt))

        def sem(name):
            return whole.enter_context(nc.semaphore(name))

        x_sb = persistent("x_sb", [P, NT, D], F32)
        ident = persistent("ident", [P, P], F32)
        mean = persistent("mean", [P, NT], F32)
        var = persistent("var", [P, NT], F32)
        rstd = persistent("rstd", [P, NT], F32)
        shift = persistent("shift", [P, NT], F32)
        stats = persistent("stats", [P, NT, 6], F32)
        pair = persistent("stat_work", [P, 4, NT], F32)
        eps_col = persistent("eps_col", [P, 1], F32)
        x_loaded = sem("x_loaded")
        stored = sem("stored")

        with ExitStack() as layer0:
            prepare_and_run_layer0(nc, a, layer0, sem, x_sb, ident, mean, var, rstd, shift, (stats, pair),
                                   eps_col, x_loaded)
        if stop_after != 0:
            scratch = {n: nc.dram_tensor(n, [B, PART, D, S], BF16) for n in ("q_parts", "k_parts")}
            scratch["v"] = nc.dram_tensor("v_scratch", [NT, P, H * VW], F32)
            run_layer1_ffn(nc, a, whole, sem, x_sb, ident, mean, var, rstd, shift, (stats, pair), eps_col, scratch)
        if stop_after is None:
            run_layer1_attention(nc, a, whole, sem, x_sb, ident, scratch, out)
        if stop_after in (0, 1):
            block = whole.enter_context(nc.Block())

            @block.sync
            def _(sp):
                sp.dma_start(out.rearrange("b (n p) d -> p (b n) d", p=P), x_sb[:]).then_inc(stored, 16)
                sp.wait_ge(stored, 16)


def prepare_and_run_layer0(nc, a, scope, sem, x_sb, ident, mean, var, rstd, shift, stat_raw, eps_col, x_loaded):
    def sb(name, shape, dt, ctx=scope):
        return ctx.enter_context(nc.sbuf_tensor(name, shape, dt))

    w_hi = sb("w_hi", [P, 5, KD, D], F32R)
    w_lo = sb("w_lo", [P, 5, KD, D], F32R)
    f_hi = sb("f_hi", [P, NLC * LC], F32R)
    f_lo = sb("f_lo", [P, NLC * LC], F32R)
    bias = sb("bias", [P, 5, KD], F32)
    rstd_h = sb("rstd_h", [P, NT], F32)
    shift_h = sb("shift_h", [P, NT], F32)
    ones = sb("ones", [P, BLK], F32)

    def gate_up(t, w, k, c):
        lo = (2 * w + k) * F0 + sum(F0C[:c])
        return t[:, lo:lo + F0C[c]]

    def down(t, c):
        return t[0:F0C[c], 4 * F0 + c * D:4 * F0 + (c + 1) * D]

    with ExitStack() as ctx:
        def st(name, shape, dt):
            return sb(name, shape, dt, ctx)

        def pb(name, shape):
            return ctx.enter_context(nc.psum_tensor(name, shape, F32))

        w_raw = st("w_raw", [P, 5, KD, D], F32)
        b_raw = st("b_raw", [P, 5, KD], F32)
        ln_g, ln_b = st("ln_g", [P, KD], F32), st("ln_b", [P, KD], F32)
        idx = st("idx", [P, NLC * LC], I32)
        lut, lut_lo = st("lut", [P, LUT], F32), st("lut_lo", [P, LUT], F32R)
        lut_hi = st("lut_hi", [P, LUT], F32R)
        d_hi, d_lo = st("d_hi", [P, LUT, P], F32R), st("d_lo", [P, LUT, P], F32R)
        mask = st("mask", [P, 4, LC], F32R)
        small = st("small", [P, 4, NT], F32)
        pb_bias, pb_hi, pb_lo = pb("pb_bias", [P, 512]), pb("pb_hi", [P, 2, 512]), pb("pb_lo", [P, 2, 512])

        w_loaded, small_loaded, idx_loaded = sem("w_loaded"), sem("small_loaded"), sem("idx_loaded")
        idx_zero, ident_ready, ident_zero = sem("idx_zero"), sem("ident_ready"), sem("ident_zero")
        lut_split, diag_ready, mask_ready, mask_used = (sem("lut_split"), sem("diag_ready"), sem("mask_ready"),
                                                        sem("mask_used"))
        weights_kept = sem("weights_kept")
        bias_ps, bias_ready, w_scaled, w_hi_ready, w_lo_ready = (sem("bias_ps"), sem("bias_ready"), sem("w_scaled"),
                                                                 sem("w_hi_ready"), sem("w_lo_ready"))
        stat_step, root_ready = sem("stat_step"), sem("root_ready")
        constants = sem("constants")
        stats_of, stats_kept = layer_norm_stats(nc, sem, x_sb, mean, var, stat_raw, "ln0")
        block = ctx.enter_context(nc.Block())

        @block.sync
        def _(sp):
            sp.wait_ge(idx_zero, 1)
            for w, name in enumerate(("gate_idx", "up_idx")):
                sp.dma_start(idx[:, 2 * w * F0:2 * (w + 1) * F0].rearrange("p (k f) -> p k f", k=KD),
                             a[name].rearrange("(k p) f -> p k f", p=P)).then_inc(idx_loaded, 16)
            for c in range(C0):
                f = sum(F0C[:c])
                sp.dma_start(down(idx, c), a["down_idx"][f:f + F0C[c], :]).then_inc(idx_loaded, 16)
            sp.dma_start(x_sb[:], a["x"].rearrange("(n p) d -> p n d", p=P)).then_inc(x_loaded, 16)

        @block.scalar
        def _(act):
            act.dma_start(lut[:], a["lut"].rearrange("(o n) -> o n", o=1).broadcast_to([P, LUT])).then_inc(small_loaded, 16)
            act.dma_start(ln_g[:], a["ln_g"]).then_inc(small_loaded, 16)
            act.dma_start(ln_b[:], a["ln_b"]).then_inc(small_loaded, 16)
            for i, name in enumerate(("q", "k", "v", "qa", "ka")):
                act.dma_start(w_raw[:, i, :, :], a["W" + name].rearrange("(k p) o -> p k o", p=P)).then_inc(w_loaded, 16)
                act.dma_start(b_raw[:, i, :], a["b" + name]).then_inc(small_loaded, 16)
            with act.Fori(0, NLC) as i:
                act.wait_ge(mask_used, i * LUT + 4 + LUT)
                act.activation(f_hi[:, bass.ds(i * LC, LC)], pb_hi[:, 0, 0:LC], ACT.Copy).then_inc(weights_kept, 1)
                act.activation(f_lo[:, bass.ds(i * LC, LC)], pb_lo[:, 0, 0:LC], ACT.Copy).then_inc(weights_kept, 1)
            act.wait_ge(w_scaled, 3 * KD)
            for i in range(5):
                act.activation(w_hi[:, i, :, :], w_raw[:, i, :, :], ACT.Copy).then_inc(w_hi_ready, 1)
            act.wait_ge(*stats_kept)
            act.wait_ge(constants, 2)
            act.activation(small[:, 0, :], var[:], ACT.Sqrt, bias=eps_col[:]).then_inc(root_ready, 1)
            act.wait_ge(stat_step, 3)
            act.activation(small[:, 2, :], small[:, 1, :], ACT.Sqrt, bias=eps_col[:]).then_inc(root_ready, 1)

        @block.gpsimd
        def _(pool):
            pool.memset(idx[:], 0).then_inc(idx_zero, 1)
            pool.memset(ident[:], 0.0).then_inc(ident_zero, 1)
            pool.wait_ge(ident_zero, 1)
            pool.affine_select(out=ident[:], in_=ident[:], compare_op=ALU.not_equal, fill=1.0, base=0,
                               pattern=[[-1, P]], channel_multiplier=1).then_inc(ident_ready, 1)

        @block.vector
        def _(dve):
            dve.memset(ones[:], 1.0).then_inc(constants, 1)
            dve.memset(eps_col[:], EPS).then_inc(constants, 1)
            dve.wait_ge(small_loaded, 8 * 16)
            dve.tensor_copy(lut_hi[:], lut[:]).then_inc(lut_split, 1)
            dve.wait_ge(lut_split, 1)
            dve.tensor_tensor(lut_lo[:], lut[:], lut_hi[:], ALU.subtract).then_inc(lut_split, 1)
            dve.wait_ge(ident_ready, 1)
            dve.wait_ge(lut_split, 2)
            for j in range(LUT):
                dve.tensor_scalar(d_hi[:, j, :], ident[:], lut_hi[:, j:j + 1].bitcast(F32), None,
                                  ALU.mult).then_inc(diag_ready, 1)
                dve.tensor_scalar(d_lo[:, j, :], ident[:], lut_lo[:, j:j + 1].bitcast(F32), None,
                                  ALU.mult).then_inc(diag_ready, 1)
            dve.wait_ge(idx_loaded, (2 + C0) * 16)
            with dve.Fori(0, NLC) as i:
                for j in range(LUT):
                    dve.wait_ge(mask_used, i * LUT + j + 1)
                    dve.tensor_scalar(mask[:, j % 4, :], idx[:, bass.ds(i * LC, LC)], float(j), None,
                                      ALU.is_equal).then_inc(mask_ready, 1)
            dve.wait_ge(bias_ps, 3 * KD)
            for i in (WQ, WK, WV):
                dve.tensor_tensor(bias[:, i, :], pb_bias[:, i * KD:(i + 1) * KD], b_raw[:, i, :],
                                  ALU.add).then_inc(bias_ready, 1)
            for i in (WQA, WKA):
                dve.tensor_scalar(bias[:, i, :], b_raw[:, i, :], SCALE0, None, ALU.mult).then_inc(bias_ready, 1)
            for i in (WQ, WK, WV):
                for k in range(KD):
                    dve.tensor_scalar(w_raw[:, i, k, :], w_raw[:, i, k, :], ln_g[:, k:k + 1], None,
                                      ALU.mult).then_inc(w_scaled, 1)
            for i in range(5):
                dve.wait_ge(w_hi_ready, i + 1)
                dve.tensor_tensor(w_lo[:, i, :, :], w_raw[:, i, :, :], w_hi[:, i, :, :],
                                  ALU.subtract).then_inc(w_lo_ready, 1)
            dve.wait_ge(x_loaded, 16)
            stats_of(dve)
            dve.wait_ge(root_ready, 1)
            dve.reciprocal(rstd[:], small[:, 0, :]).then_inc(stat_step, 1)
            dve.wait_ge(stat_step, 1)
            dve.tensor_tensor(small[:, 3, :], rstd[:], rstd[:], ALU.mult).then_inc(stat_step, 1)
            dve.wait_ge(stat_step, 2)
            dve.tensor_tensor(small[:, 1, :], var[:], small[:, 3, :], ALU.mult).then_inc(stat_step, 1)
            dve.scalar_tensor_tensor(shift[:], mean[:], -1.0, rstd[:], ALU.mult, ALU.mult).then_inc(stat_step, 1)
            dve.wait_ge(root_ready, 2)
            dve.reciprocal(small[:, 0, :], small[:, 2, :]).then_inc(stat_step, 1)
            dve.wait_ge(stat_step, 5)
            dve.tensor_tensor(rstd_h[:], rstd[:], small[:, 0, :], ALU.mult).then_inc(stat_step, 1)
            dve.tensor_tensor(shift_h[:], shift[:], small[:, 0, :], ALU.mult).then_inc(stat_step, 1)

        @block.tensor
        def _(pe):
            pe.wait_ge(w_loaded, 5 * 16)
            pe.wait_ge(small_loaded, 8 * 16)
            for i in (WQ, WK, WV):
                for c in range(KD):
                    for k in range(KD):
                        ins = pe.matmul(pb_bias[:, i * KD + c:i * KD + c + 1], w_raw[:, i, k, c * P:(c + 1) * P],
                                        ln_b[:, k:k + 1], start=(k == 0), stop=(k == KD - 1), skip_group_check=True)
                    ins.then_inc(bias_ps, 1)
            pe.wait_ge(diag_ready, 2 * LUT)
            pe.sem_inc(mask_used, 4)
            pe.sem_inc(weights_kept, 2)
            with pe.Fori(0, NLC) as i:
                pe.wait_ge(weights_kept, i * 2 + 2)
                for j in range(LUT):
                    pe.wait_ge(mask_ready, i * LUT + j + 1)
                    pe.matmul(pb_hi[:, 0, 0:LC], d_hi[:, j, :], mask[:, j % 4, :], start=(j == 0),
                                   stop=(j == LUT - 1))
                    lo = pe.matmul(pb_lo[:, 0, 0:LC], d_lo[:, j, :], mask[:, j % 4, :], start=(j == 0),
                                   stop=(j == LUT - 1))
                    lo.then_inc(mask_used, 1)

    run_layer0(nc, scope, sem, x_sb, ident, rstd, shift, rstd_h, shift_h, ones, bias, w_hi, w_lo, f_hi, f_lo,
               gate_up, down)


def run_layer0(nc, scope, sem, x_sb, ident, rstd, shift, rstd_h, shift_h, ones, bias, w_hi, w_lo, f_hi, f_lo,
               gate_up, down):
    def sb(name, shape, dt=F32):
        return scope.enter_context(nc.sbuf_tensor(name, shape, dt))

    x_tok, h_tok = sb("x_tok", [P, TT, D]), sb("h_tok", [P, TT, D])
    xt_hi, xt_lo = sb("xt_hi", [P, 2 * KD, BLK], F32R), sb("xt_lo", [P, 2 * KD, BLK], F32R)
    q_sb, e_sb, sum_sb, rc_sb = (sb(n, [P, KD, BLK]) for n in ("q_sb", "e_sb", "sum_sb", "rc_sb"))
    pool1, sum2, pool2, mixed = (sb(n, [P, KD, BLK]) for n in ("pool1", "sum2", "pool2", "mixed"))
    c_hi, c_lo = sb("c_hi", [P, KD, BLK], F32R), sb("c_lo", [P, KD, BLK], F32R)
    silu, hid = sb("silu", [P, 2, BLK]), sb("hid", [P, 2, BLK])
    hid_hi, hid_lo = sb("hid_hi", [P, 2, BLK], F32R), sb("hid_lo", [P, 2, BLK], F32R)
    ps = scope.enter_context(nc.psum_tensor("ps0", [P, 8, 512], F32))
    proj = ps[:, 0:2, :]
    ring = ps[:, 2:6, :]
    acc = ps[:, 6:8, :].rearrange("p h (j d) -> p (h j) d", d=D)

    names = ("l0_xtok l0_htok l0_xt_ps l0_xt_hi l0_xt_lo l0_proj_ps l0_q l0_chi l0_clo l0_exp l0_times l0_sum "
             "l0_recip l0_weight l0_pooled l0_mixed l0_attn l0_gu_ps l0_silu l0_hid l0_hid_hi l0_hid_lo l0_down "
             "l0_acc_ps l0_x1").split()
    (xtok, htok, xt_ps, xt_hi_ok, xt_lo_ok, proj_ps, q_ok, chi_ok, clo_ok, exp_ok, times_ok, sum_ok,
     recip_ok, weight_ok, pooled_ok, mixed_ok, attn_ok, gu_ps, silu_ok, hid_ok, hid_hi_ok, hid_lo_ok, down_ok,
     acc_ps, x1_ok) = (sem(n) for n in names)
    block = scope.enter_context(nc.Block())

    def steps(eng, body):
        for u in range(2):
            body(u, u, False)
        with eng.Fori(1, B - 1) as b:
            for u in range(2):
                body(b * 2 + u, u, False)
        for u in range(2):
            body((B - 1) * 2 + u, u, u == 1)

    @block.tensor
    def _(pe):
        def transposes(m, first=False):
            for t in range(2 * KD):
                wait(pe, xtok if t < KD else htok, m * TT + TT)
                if not first:
                    wait(pe, hid_ok if t % 2 else silu_ok, m * C0 - 1 + t // 2)
                tok, k = (x_tok, t) if t < KD else (h_tok, t - KD)
                for j in range(TT):
                    ins = pe.transpose(ring[:, t, j * P:(j + 1) * P], tok[:, j, k * P:(k + 1) * P], ident[:])
                ins.then_inc(xt_ps, 1)

        def projection(i, first, hi, lo):
            for c in range(KD):
                for k in range(KD):
                    o = slice(c * P, (c + 1) * P)
                    ins = split3(pe, proj[:, c, :], w_hi[:, i, k, o], w_lo[:, i, k, o], hi[:, first + k, :],
                                 lo[:, first + k, :], k == 0, k == KD - 1)
                ins.then_inc(proj_ps, 1)

        def gate_and_up(n, c):
            r = 2 * (c % 2)
            if c >= 2:
                wait(pe, silu_ok, n * C0 + c - 1)
                wait(pe, hid_ok, n * C0 + c - 1)
            for w in range(2):
                for k in range(KD):
                    ins = split3(pe, ring[0:F0C[c], r + w, :], gate_up(f_hi, w, k, c), gate_up(f_lo, w, k, c),
                                 xt_hi[:, k, :], xt_lo[:, k, :], k == 0, k == KD - 1)
                ins.then_inc(gu_ps, 1)

        def down_chunk(n, c):
            wait(pe, hid_hi_ok, n * C0 + c + 1)
            wait(pe, hid_lo_ok, n * C0 + c + 1)
            if c == 0:
                wait(pe, x1_ok, n * 2)
            for j in range(TT):
                t = slice(j * P, (j + 1) * P)
                f = slice(0, F0C[c])
                pe.matmul(acc[:, j, :], hid_hi[f, c % 2, t], down(f_hi, c), start=(c == 0 and j % 2 == 0),
                          stop=False, skip_group_check=True)
                pe.matmul(acc[:, j, :], hid_lo[f, c % 2, t], down(f_hi, c), start=False, stop=False,
                          skip_group_check=True)
                ins = pe.matmul(acc[:, j, :], hid_hi[f, c % 2, t], down(f_lo, c), start=False, stop=False,
                                skip_group_check=True)
            ins.then_inc(down_ok, 1)

        transposes(0, first=True)

        def body(n, u, last):
            wait(pe, xt_hi_ok, n * 4 + 4)
            wait(pe, xt_lo_ok, n * 4 + 4)
            wait(pe, attn_ok, n * KD)
            projection(WQ, KD, xt_hi, xt_lo)
            gate_and_up(n, 0)
            gate_and_up(n, 1)
            wait(pe, chi_ok, n * 2 * KD + KD)
            wait(pe, clo_ok, n * 2 * KD + KD)
            projection(WQA, 0, c_hi, c_lo)
            gate_and_up(n, 2)
            wait(pe, exp_ok, n * 2 * KD + KD)
            projection(WK, KD, xt_hi, xt_lo)
            down_chunk(n, 0)
            gate_and_up(n, 3)
            down_chunk(n, 1)
            gate_and_up(n, 4)
            down_chunk(n, 2)
            wait(pe, chi_ok, n * 2 * KD + 2 * KD)
            wait(pe, clo_ok, n * 2 * KD + 2 * KD)
            projection(WKA, 0, c_hi, c_lo)
            gate_and_up(n, 5)
            down_chunk(n, 3)
            wait(pe, exp_ok, n * 2 * KD + 2 * KD)
            projection(WV, KD, xt_hi, xt_lo)
            if not last:
                transposes(n + 1)
            down_chunk(n, 4)
            down_chunk(n, 5)
            wait(pe, attn_ok, n * KD + KD)
            for j in range(TT):
                for k in range(KD):
                    ins = pe.matmul(acc[:, j, k * P:(k + 1) * P], mixed[:, k, j * P:(j + 1) * P], ident[:],
                                    start=False, stop=(k == KD - 1 and j % 2 == 1), skip_group_check=True)
                if j % 2:
                    ins.then_inc(acc_ps, 1)

        steps(pe, body)

    @block.scalar
    def _(act):
        def twice_normalised(m):
            wait(act, xt_ps, m * 4)
            for j in range(TT):
                t = bass.ds(m * TT + j, 1)
                act.activation(h_tok[:, j, :], x_sb[:, t, :], ACT.Identity, scale=rstd_h[:, t],
                               bias=shift_h[:, t]).then_inc(htok, 1)

        def transposed(m):
            for t in range(2 * KD):
                wait(act, xt_ps, m * 4 + t + 1)
                act.activation(xt_hi[:, t, :], ring[:, t, :], ACT.Copy).then_inc(xt_hi_ok, 1)

        def silu_of(n, c):
            wait(act, gu_ps, n * 2 * C0 + 2 * c + 1)
            if c >= 2:
                wait(act, hid_ok, n * C0 + c - 1)
            f = slice(0, F0C[c])
            act.activation(silu[f, c % 2, :], ring[f, 2 * (c % 2), :], ACT.Silu).then_inc(silu_ok, 1)

        def hidden_high(n, c):
            wait(act, hid_ok, n * C0 + c + 1)
            if c >= 2:
                wait(act, down_ok, n * C0 + c - 1)
            f = slice(0, F0C[c])
            act.activation(hid_hi[f, c % 2, :], hid[f, c % 2, :], ACT.Copy).then_inc(hid_hi_ok, 1)

        def exponentials(n, which, i):
            for c in range(KD):
                wait(act, proj_ps, n * 5 * KD + (3 * KD if which else KD) + c + 1)
                act.activation(e_sb[:, c, :], proj[:, c, :], ACT.Exp, scale=SCALE0,
                               bias=bias[:, i, c:c + 1]).then_inc(exp_ok, 1)

        twice_normalised(0)
        transposed(0)

        def body(n, u, last):
            for c in range(KD):
                wait(act, proj_ps, n * 5 * KD + c + 1)
                act.activation(q_sb[:, c, :], proj[:, c, :], ACT.Identity, bias=bias[:, WQ, c:c + 1]).then_inc(q_ok, 1)
            if not last:
                twice_normalised(n + 1)
            silu_of(n, 0)
            silu_of(n, 1)
            hidden_high(n, 0)
            hidden_high(n, 1)
            exponentials(n, 0, WQA)
            silu_of(n, 2)
            hidden_high(n, 2)
            silu_of(n, 3)
            silu_of(n, 4)
            hidden_high(n, 3)
            for c in range(KD):
                wait(act, mixed_ok, n * KD + c + 1)
                act.activation(c_hi[:, c, :], mixed[:, c, :], ACT.Copy).then_inc(chi_ok, 1)
            hidden_high(n, 4)
            exponentials(n, 1, WKA)
            silu_of(n, 5)
            hidden_high(n, 5)
            if not last:
                transposed(n + 1)

        steps(act, body)

    @block.gpsimd
    def _(pool):
        def hidden_low(n, c):
            wait(pool, hid_hi_ok, n * C0 + c + 1)
            f = slice(0, F0C[c])
            pool.tensor_tensor(hid_lo[f, c % 2, :], hid[f, c % 2, :], hid_hi[f, c % 2, :],
                               ALU.subtract).then_inc(hid_lo_ok, 1)

        def body(n, u, last):
            hidden_low(n, 0)
            hidden_low(n, 1)
            for c in range(KD):
                wait(pool, exp_ok, n * 2 * KD + c + 1)
                pool.tensor_tensor(q_sb[:, c, :], q_sb[:, c, :], e_sb[:, c, :], ALU.mult).then_inc(times_ok, 1)
            hidden_low(n, 2)
            hidden_low(n, 3)
            hidden_low(n, 4)
            for c in range(KD):
                wait(pool, exp_ok, n * 2 * KD + KD + c + 1)
                pool.tensor_tensor(q_sb[:, c, :], mixed[:, c, :], e_sb[:, c, :], ALU.mult).then_inc(times_ok, 1)
            hidden_low(n, 5)

        steps(pool, body)

    @block.vector
    def _(dve):
        def once_normalised(m):
            wait(dve, xt_ps, m * 4)
            for j in range(TT):
                t = bass.ds(m * TT + j, 1)
                dve.tensor_scalar(x_tok[:, j, :], x_sb[:, t, :], rstd[:, t], shift[:, t], ALU.mult,
                                  ALU.add).then_inc(xtok, 1)

        def transposed_low(m):
            for t in range(2 * KD):
                wait(dve, xt_hi_ok, m * 4 + t + 1)
                dve.tensor_tensor(xt_lo[:, t, :], ring[:, t, :], xt_hi[:, t, :], ALU.subtract).then_inc(xt_lo_ok, 1)

        def hidden(n, c):
            wait(dve, silu_ok, n * C0 + c + 1)
            wait(dve, gu_ps, n * 2 * C0 + 2 * c + 2)
            if c >= 2:
                wait(dve, hid_lo_ok, n * C0 + c - 1)
            f = slice(0, F0C[c])
            dve.tensor_tensor(hid[f, c % 2, :], silu[f, c % 2, :], ring[f, 2 * (c % 2) + 1, :],
                              ALU.mult).then_inc(hid_ok, 1)

        def running_sum(sem_out, dst, src, waits, u):
            for c in range(KD):
                for s, v in waits:
                    wait(dve, s, v + c + 1)
                carry = dst[:, c, BLK - 1:BLK] if u else 0.0
                dve.tensor_tensor_scan(dst[:, c, :], ones[:], src[:, c, :], carry, ALU.mult, ALU.add).then_inc(sem_out, 1)

        def reciprocal(n, which, c):
            k = 2 * KD * n + KD * which + c
            wait(dve, sum_ok, k + 1)
            src = sum2 if which else sum_sb
            dve.reciprocal(rc_sb[:, c, :], src[:, c, :]).then_inc(recip_ok, 1)

        def weighted(n, which):
            for c in range(KD):
                k = 2 * KD * n + KD * which + c
                wait(dve, recip_ok, k + 1)
                wait(dve, times_ok, k + 1)
                dve.tensor_tensor(rc_sb[:, c, :], rc_sb[:, c, :], q_sb[:, c, :], ALU.mult).then_inc(weight_ok, 1)

        once_normalised(0)
        transposed_low(0)

        def body(n, u, last):
            for c in range(KD):
                wait(dve, q_ok, n * KD + c + 1)
                dve.tensor_copy(c_hi[:, c, :], q_sb[:, c, :]).then_inc(chi_ok, 1)
            for c in range(KD):
                wait(dve, chi_ok, n * 2 * KD + c + 1)
                dve.tensor_tensor(c_lo[:, c, :], q_sb[:, c, :], c_hi[:, c, :], ALU.subtract).then_inc(clo_ok, 1)
            if not last:
                once_normalised(n + 1)
            hidden(n, 0)
            hidden(n, 1)
            running_sum(sum_ok, sum_sb, e_sb, [(exp_ok, n * 2 * KD)], u)
            reciprocal(n, 0, 0)
            hidden(n, 2)
            reciprocal(n, 0, 1)
            weighted(n, 0)
            hidden(n, 3)
            running_sum(pooled_ok, pool1, rc_sb, [(weight_ok, n * 2 * KD)], u)
            for c in range(KD):
                wait(dve, proj_ps, n * 5 * KD + 2 * KD + c + 1)
                wait(dve, pooled_ok, n * 2 * KD + c + 1)
                dve.scalar_tensor_tensor(mixed[:, c, :], proj[:, c, :], bias[:, WK, c:c + 1], pool1[:, c, :],
                                         ALU.add, ALU.mult).then_inc(mixed_ok, 1)
            for c in range(KD):
                wait(dve, chi_ok, n * 2 * KD + KD + c + 1)
                dve.tensor_tensor(c_lo[:, c, :], mixed[:, c, :], c_hi[:, c, :], ALU.subtract).then_inc(clo_ok, 1)
            hidden(n, 4)
            running_sum(sum_ok, sum2, e_sb, [(exp_ok, n * 2 * KD + KD)], u)
            reciprocal(n, 1, 0)
            hidden(n, 5)
            reciprocal(n, 1, 1)
            if not last:
                transposed_low(n + 1)
            weighted(n, 1)
            running_sum(pooled_ok, pool2, rc_sb, [(weight_ok, n * 2 * KD + KD)], u)
            for c in range(KD):
                wait(dve, proj_ps, n * 5 * KD + 4 * KD + c + 1)
                wait(dve, pooled_ok, n * 2 * KD + KD + c + 1)
                dve.scalar_tensor_tensor(mixed[:, c, :], proj[:, c, :], bias[:, WV, c:c + 1], pool2[:, c, :],
                                         ALU.add, ALU.mult).then_inc(attn_ok, 1)
            for h in range(TT // 2):
                wait(dve, acc_ps, n * 2 + h + 1)
                t = bass.ds(n * TT + 2 * h, 2)
                dve.tensor_tensor(x_sb[:, t, :], x_sb[:, t, :], acc[:, 2 * h:2 * h + 2, :], ALU.add).then_inc(x1_ok, 1)

        steps(dve, body)


def run_layer1_ffn(nc, a, whole, sem, x_sb, ident, mean, var, rstd, shift, stat_raw, eps_col, scratch):
    with ExitStack() as scope:
        def right(name, shape, dt, ctx=scope):
            return ctx.enter_context(nc.sbuf_tensor(name, shape, dt, side="right"))

        gu_hi, gu_lo = (right(n, [P, 2, KD, F1], F32R) for n in ("gu_hi", "gu_lo"))
        dn_hi, dn_lo = (right(n, [P, C1, D], F32R) for n in ("dn_hi", "dn_lo"))
        qkv_hi, qkv_lo = (right(n, [P, KD, 3 * D], F32R) for n in ("qkv_hi", "qkv_lo"))
        rt_hi, rt_lo = (right(n, [P, KD, NX], F32R) for n in ("rt_hi", "rt_lo"))
        expert_of = right("expert_of", [3 * LANE, CX * P], BF16)
        before8 = right("before8", [P, TT, NX, NX], BF16)
        before4 = right("before4", [P, TT, NX // 2, NX // 2], BF16)
        w_parts = right("w_parts", [P, TT, 3 * LANE], BF16)
        bv_row, bo_row = right("bv_row", [P, D], F32), right("bo_row", [P, D], F32)
        qk_bias = right("qk_bias", [P, 3 * KD], F32)

        with ExitStack() as ctx:
            load_layer1(nc, a, ctx, sem, x_sb, mean, var, rstd, shift, stat_raw, eps_col, gu_hi, gu_lo, dn_hi, dn_lo,
                        qkv_hi, qkv_lo, rt_hi, rt_lo, expert_of, before8, before4, w_parts, bv_row, bo_row, qk_bias)
        layer1_steps(nc, scope, sem, x_sb, ident, rstd, shift, scratch, gu_hi, gu_lo, dn_hi, dn_lo, qkv_hi,
                     qkv_lo, rt_hi, rt_lo, expert_of, before8, before4, w_parts, bv_row, bo_row, qk_bias)


def load_layer1(nc, a, ctx, sem, x_sb, mean, var, rstd, shift, stat_raw, eps_col, gu_hi, gu_lo, dn_hi, dn_lo, qkv_hi,
                qkv_lo, rt_hi, rt_lo, expert_of, before8, before4, w_parts, bv_row, bo_row, qk_bias):
    def st(name, shape, dt=F32):
        return ctx.enter_context(nc.sbuf_tensor(name, shape, dt))

    gu, dn, qkv, rt = (st("gu_raw", [P, 2, KD, F1]), st("dn_raw", [P, C1, D]), st("qkv_raw", [P, KD, 3 * D]),
                       st("rt_raw", [P, KD, NX]))
    small = st("small1", [P, NT])
    names = "l1_qkv_loaded l1_gu_loaded l1_dn_loaded l1_rows_loaded l1_hi l1_lo_dve l1_lo_pool l1_masks l1_root l1_rstd"
    qkv_loaded, gu_loaded, dn_loaded, rows_loaded, hi_ok, lo_dve, lo_pool, masks, root, rstd_ok = (
        sem(n) for n in names.split())
    dn_zero = sem("l1_dn_zero")
    stats_of, stats_kept = layer_norm_stats(nc, sem, x_sb, mean, var, stat_raw, "ln1")
    routed, shared = NX * FX, slice(NX * FX, F1)
    block = ctx.enter_context(nc.Block())
    pieces = [(qkv, qkv_hi, qkv_lo, qkv_loaded, 2), (rt, rt_hi, rt_lo, qkv_loaded, 2)]

    @block.sync
    def _(sp):
        sp.dma_start(qkv[:], a["w_qkv"].rearrange("(k p) o -> p k o", p=P)).then_inc(qkv_loaded, 16)
        sp.dma_start(rt[:], a["router"].rearrange("(k p) o -> p k o", p=P)).then_inc(qkv_loaded, 16)
        for w, (routed_w, shared_w) in enumerate((("gate_w", "sh_gate"), ("up_w", "sh_up"))):
            for k in range(KD):
                rows = slice(k * P, (k + 1) * P)
                sp.dma_start(gu[:, w, k, 0:routed].rearrange("p (n f) -> p n f", n=NX),
                             a[routed_w][:, rows, :].rearrange("n p f -> p n f")).then_inc(gu_loaded, 16)
                sp.dma_start(gu[:, w, k, shared], a[shared_w][rows, :]).then_inc(gu_loaded, 16)

    @block.scalar
    def _(act):
        act.dma_start(bv_row[:], a["b_qkv_row"][2 * D:3 * D].rearrange("(o n) -> o n", o=1)
                      .broadcast_to([P, D])).then_inc(rows_loaded, 16)
        act.dma_start(bo_row[:], a["b_o"].rearrange("(o n) -> o n", o=1).broadcast_to([P, D])).then_inc(rows_loaded, 16)
        act.dma_start(qk_bias[:], a["b_qkv"]).then_inc(rows_loaded, 16)
        act.dma_start(dn[:, 0:CX, :], a["down_w"].rearrange("n f d -> (n f) d").rearrange("(c p) d -> p c d", p=P)
                      ).then_inc(dn_loaded, 16)
        wait(act, dn_zero, 1)
        for c in range(CX, C1):
            f = sum(F1C[CX:c])
            act.dma_start(dn[0:F1C[c], c, :], a["sh_down"][f:f + F1C[c], :]).then_inc(dn_loaded, 16)
        wait(act, qkv_loaded, 32)
        act.activation(qkv_hi[:], qkv[:], ACT.Copy).then_inc(hi_ok, 1)
        act.activation(rt_hi[:], rt[:], ACT.Copy).then_inc(hi_ok, 1)
        wait(act, gu_loaded, 8 * 16)
        for w in range(2):
            for k in range(KD):
                act.activation(gu_hi[:, w, k, :], gu[:, w, k, :], ACT.Copy).then_inc(hi_ok, 1)
        wait(act, dn_loaded, (1 + C1 - CX) * 16)
        for h in range(2):
            c = slice(h * C1 // 2, (h + 1) * C1 // 2)
            act.activation(dn_hi[:, c, :], dn[:, c, :], ACT.Copy).then_inc(hi_ok, 1)
        wait(act, *stats_kept)
        act.activation(small[:], var[:], ACT.Sqrt, bias=eps_col[:]).then_inc(root, 1)
        wait(act, rows_loaded, 48)

    @block.gpsimd
    def _(pool):
        pool.memset(dn[:, CX:C1, :], 0.0).then_inc(dn_zero, 1)
        pool.memset(expert_of[:], 1.0).then_inc(masks, 1)
        pool.memset(before8[:], 1.0).then_inc(masks, 1)
        pool.memset(before4[:], 1.0).then_inc(masks, 1)
        pool.memset(w_parts[:], 0.0).then_inc(masks, 1)
        wait(pool, masks, 4)
        for t, n in ((before8, NX), (before4, NX // 2)):
            pool.affine_select(out=t[:], in_=t[:], compare_op=ALU.is_gt, fill=0.0, base=0,
                               pattern=[[0, TT], [1, n], [-1, n]], channel_multiplier=0).then_inc(masks, 1)
        for r in range(PART):
            rows = expert_of[r * LANE:(r + 1) * LANE, :]
            pool.affine_select(out=rows, in_=rows, compare_op=ALU.is_ge, fill=0.0, base=0,
                               pattern=[[1, CX * P]], channel_multiplier=-FX).then_inc(masks, 1)
            wait(pool, masks, 7 + 2 * r)
            pool.affine_select(out=rows, in_=rows, compare_op=ALU.is_ge, fill=0.0, base=FX - 1,
                               pattern=[[-1, CX * P]], channel_multiplier=FX).then_inc(masks, 1)
        wait(pool, masks, 12)
        wait(pool, hi_ok, 6)
        pool.tensor_tensor(gu_lo[:, 1, 1, :], gu[:, 1, 1, :], gu_hi[:, 1, 1, :], ALU.subtract).then_inc(lo_pool, 1)
        wait(pool, hi_ok, 8)
        c = slice(C1 // 2, C1)
        pool.tensor_tensor(dn_lo[:, c, :], dn[:, c, :], dn_hi[:, c, :], ALU.subtract).then_inc(lo_pool, 1)
        wait(pool, lo_pool, 2)

    @block.vector
    def _(dve):
        stats_of(dve)
        wait(dve, hi_ok, 1)
        dve.tensor_tensor(qkv_lo[:], qkv[:], qkv_hi[:], ALU.subtract).then_inc(lo_dve, 1)
        wait(dve, hi_ok, 2)
        dve.tensor_tensor(rt_lo[:], rt[:], rt_hi[:], ALU.subtract).then_inc(lo_dve, 1)
        for i, (w, k) in enumerate(((0, 0), (0, 1), (1, 0))):
            wait(dve, hi_ok, 3 + i)
            dve.tensor_tensor(gu_lo[:, w, k, :], gu[:, w, k, :], gu_hi[:, w, k, :], ALU.subtract).then_inc(lo_dve, 1)
        wait(dve, hi_ok, 7)
        c = slice(0, C1 // 2)
        dve.tensor_tensor(dn_lo[:, c, :], dn[:, c, :], dn_hi[:, c, :], ALU.subtract).then_inc(lo_dve, 1)
        wait(dve, root, 1)
        dve.reciprocal(rstd[:], small[:]).then_inc(rstd_ok, 1)
        wait(dve, rstd_ok, 1)
        dve.scalar_tensor_tensor(shift[:], mean[:], -1.0, rstd[:], ALU.mult, ALU.mult).then_inc(rstd_ok, 1)
        wait(dve, lo_dve, 6)
        wait(dve, rstd_ok, 2)


ORDER1 = list(range(CX, C1)) + list(range(CX))


def layer1_steps(nc, scope, sem, x_sb, ident, rstd, shift, scratch, gu_hi, gu_lo, dn_hi, dn_lo, qkv_hi, qkv_lo,
                 rt_hi, rt_lo, expert_of, before8, before4, w_parts, bv_row, bo_row, qk_bias):
    def sb(name, shape, dt=F32):
        return scope.enter_context(nc.sbuf_tensor(name, shape, dt, side="right"))

    x_tok = sb("x_tok1", [P, TT, D])
    xt_hi, xt_lo = sb("xt_hi1", [P, 2, KD, BLK], F32R), sb("xt_lo1", [P, 2, KD, BLK], F32R)
    parts = sb("parts", [P, 2 * KD, PART, BLK], BF16)
    rest = sb("rest", [P, 2 * KD, BLK])
    v_sb = sb("v_sb", [P, TT, H, VW])
    hid = sb("hid1", [P, 2, BLK])
    hid_hi, hid_lo = sb("hid_hi1", [P, 2, BLK], F32R), sb("hid_lo1", [P, 2, BLK], F32R)
    w_turned = sb("w_turned", [3 * LANE, BLK], BF16)
    ident_bf = sb("ident_bf", [P, P], BF16)
    top, total = sb("top", [P, TT]), sb("total", [P, TT])
    logit, score, kept = sb("logit", [P, TT, NX]), sb("score", [P, TT, NX]), sb("kept_score", [P, TT, NX])
    group, g_rank = sb("group", [P, TT, NX // 2]), sb("g_rank", [P, TT, NX // 2])
    rank, w_rest = sb("rank", [P, TT, NX]), sb("w_rest", [P, TT, NX])
    above, equal = sb("above", [P, TT, NX, NX], BF16), sb("equal", [P, TT, NX, NX], BF16)
    ps = scope.enter_context(nc.psum_tensor("ps1", [P, 8, 512], F32))
    ring, spread, misc = ps[:, 0:4, :], ps[:, 4, :], ps[:, 5, :]
    acc = ps[:, 6:8, :].rearrange("p h (j d) -> p (h j) d", d=D)
    logits = misc[:, 0:TT * NX].rearrange("p (t e) -> p t e", t=TT)
    turned = misc[0:3 * LANE, 128:128 + BLK // 2].bitcast(BF16)

    names = ("l1_xtok l1_xt_ps l1_xt_hi l1_xt_lo l1_logits l1_route l1_exp l1_w_ready l1_turned_ps l1_w_turned l1_qk_ps l1_part1 "
             "l1_rest l1_part2 l1_part3 l1_v_ps l1_v l1_gu_ps l1_silu l1_prod l1_spread_ps l1_weighted "
             "l1_hid_hi l1_hid_lo l1_down l1_x2 l1_out l1_ones l1_ident_bf").split()
    (xtok, xt_ps, xt_hi_ok, xt_lo_ok, logits_ok, route, exp_ok, w_ready, turned_ps, w_turned_ok, qk_ps, part1, rest_ok, part2,
     part3, v_ps, v_ok, gu_ps, silu_ok, prod_ok, spread_ps, weighted_ok, hid_hi_ok, hid_lo_ok, down_ok,
     x2_ok, out_ok, ones_ok, ident_bf_ok) = (sem(n) for n in names)
    v_out = sem("l1_v_out")
    NQK = 2 * KD
    parts_out = [sem(f"l1_parts_out{c}") for c in range(NQK)]
    TURN_AT = (6, 9)
    block = scope.enter_context(nc.Block())

    def steps(eng, body):
        body(0, 0, False)
        with eng.Fori(0, NB // 2 - 1) as m:
            body(2 * m + 1, 1, False)
            body(2 * m + 2, 0, False)
        body(NB - 1, (NB - 1) % 2, True)

    def banks(i):
        return 2 * ((i + 1) % 2)

    def finished(n, i):
        if i < C1 - CX:
            return prod_ok, n * C1 + i + 1
        return weighted_ok, n * CX + i - (C1 - CX) + 1

    @block.tensor
    def _(pe):
        def transposes(m, k):
            if k == 0:
                wait(pe, xtok, m * TT + TT)
                wait(pe, w_turned_ok, m)
            else:
                wait(pe, xt_hi_ok, m * KD + k)
                wait(pe, xt_lo_ok, m * KD + k)
            for j in range(TT):
                ins = pe.transpose(misc[:, j * P:(j + 1) * P], x_tok[:, j, k * P:(k + 1) * P], ident[:])
            ins.then_inc(xt_ps, 1)

        def router(m, par):
            wait(pe, xt_hi_ok, m * KD + KD)
            wait(pe, xt_lo_ok, m * KD + KD)
            for j in range(TT):
                t = slice(j * P, (j + 1) * P)
                for k in range(KD):
                    pe.matmul(logits[:, j, :], xt_hi[:, par, k, t], rt_hi[:, k, :], start=(j == 0 and k == 0),
                              stop=False, skip_group_check=True)
                    pe.matmul(logits[:, j, :], xt_lo[:, par, k, t], rt_hi[:, k, :], start=False, stop=False,
                              skip_group_check=True)
                    ins = pe.matmul(logits[:, j, :], xt_hi[:, par, k, t], rt_lo[:, k, :], start=False,
                                    stop=(k == KD - 1), skip_group_check=True)
            ins.then_inc(logits_ok, 1)

        def gate_and_up(n, par, i):
            c, r = ORDER1[i], banks(i)
            f = slice(sum(F1C[:c]), sum(F1C[:c + 1]))
            if i == 0:
                wait(pe, rest_ok, n * NQK + NQK)
            elif i == 1:
                wait(pe, v_ok, n * 2 + 2)
            else:
                wait(pe, silu_ok, n * C1 + i - 1)
                wait(pe, prod_ok, n * C1 + i - 1)
            for w in range(2):
                for k in range(KD):
                    ins = split3(pe, ring[0:F1C[c], r + w, :], gu_hi[:, w, k, f], gu_lo[:, w, k, f],
                                 xt_hi[:, par, k, :], xt_lo[:, par, k, :], k == 0, k == KD - 1)
                ins.then_inc(gu_ps, 1)

        def spread_weights(n, c):
            wait(pe, w_turned_ok, n + 1)
            wait(pe, weighted_ok, n * CX + c)
            pe.matmul(spread[:, :], expert_of[:, c * P:(c + 1) * P], w_turned[:], start=True,
                      stop=True).then_inc(spread_ps, 1)

        def down_chunk(n, i):
            c = ORDER1[i]
            wait(pe, hid_hi_ok, n * C1 + i + 1)
            wait(pe, hid_lo_ok, n * C1 + i + 1)
            if i == 0:
                wait(pe, x2_ok, n * 2)
            f = slice(0, F1C[c])
            for j in range(TT):
                t = slice(j * P, (j + 1) * P)
                pe.matmul(acc[:, j, :], hid_hi[f, i % 2, t], dn_hi[f, c, :], start=(i == 0 and j % 2 == 0), stop=False,
                          skip_group_check=True)
                pe.matmul(acc[:, j, :], hid_lo[f, i % 2, t], dn_hi[f, c, :], start=False, stop=False,
                          skip_group_check=True)
                ins = pe.matmul(acc[:, j, :], hid_hi[f, i % 2, t], dn_lo[f, c, :], start=False, stop=(i == C1 - 1),
                                skip_group_check=True)
            ins.then_inc(down_ok, 1)

        wait(pe, ident_bf_ok, 1)
        for k in range(KD):
            transposes(0, k)
        router(0, 0)

        def body(n, par, last):
            wait(pe, silu_ok, n * C1)
            wait(pe, prod_ok, n * C1)
            for c in range(NQK):
                o = slice(c * P, (c + 1) * P)
                for k in range(KD):
                    ins = split3(pe, ring[:, c, :], qkv_hi[:, k, o], qkv_lo[:, k, o], xt_hi[:, par, k, :],
                                 xt_lo[:, par, k, :], k == 0, k == KD - 1)
                ins.then_inc(qk_ps, 1)
            for h in range(2):
                wait(pe, rest_ok, n * NQK + h + 1)
                o = slice(2 * D, 3 * D)
                for jj in range(2):
                    j = 2 * h + jj
                    t, dst = slice(j * P, (j + 1) * P), ring[:, h, jj * D:(jj + 1) * D]
                    for k in range(KD):
                        pe.matmul(dst, xt_hi[:, par, k, t], qkv_hi[:, k, o], start=(jj == 0 and k == 0), stop=False,
                                  skip_group_check=True)
                        pe.matmul(dst, xt_lo[:, par, k, t], qkv_hi[:, k, o], start=False, stop=False,
                                  skip_group_check=True)
                        ins = pe.matmul(dst, xt_hi[:, par, k, t], qkv_lo[:, k, o], start=False, stop=(k == KD - 1),
                                        skip_group_check=True)
                ins.then_inc(v_ps, 1)
            for i in range(C1):
                gate_and_up(n, par, i)
                if i == C1 - CX:
                    wait(pe, w_ready, n + 1)
                    for j in range(TT):
                        ins = pe.transpose(turned[:, j * P:(j + 1) * P], w_parts[:, j, :], ident_bf[:])
                    ins.then_inc(turned_ps, 1)
                if i >= 2:
                    down_chunk(n, i - 2)
                if ORDER1[i] < CX:
                    spread_weights(n, ORDER1[i])
                if i in TURN_AT and not last:
                    transposes(n + 1, TURN_AT.index(i))
            down_chunk(n, C1 - 2)
            if not last:
                router(n + 1, 1 - par)
            down_chunk(n, C1 - 1)

        steps(pe, body)

    @block.scalar
    def _(act):
        def transposed(m, par, k):
            wait(act, xt_ps, m * KD + k + 1)
            act.activation(xt_hi[:, par, k, :], misc, ACT.Copy).then_inc(xt_hi_ok, 1)

        def first_part(n, c):
            wait(act, qk_ps, n * NQK + c + 1)
            wait(act, parts_out[c], n * 16)
            act.activation(parts[:, c, 0, :], ring[:, c, :], ACT.Identity, bias=qk_bias[:, c:c + 1]).then_inc(part1, 1)

        def second_part(n, c):
            wait(act, rest_ok, n * NQK + c + 1)
            act.activation(parts[:, c, 1, :], rest[:, c, :], ACT.Copy).then_inc(part2, 1)

        def silu_of(n, i):
            wait(act, gu_ps, n * 2 * C1 + 2 * i + 1)
            if i >= 2:
                wait(act, hid_hi_ok, n * C1 + i - 1)
                wait(act, hid_lo_ok, n * C1 + i - 1)
            else:
                wait(act, hid_hi_ok, n * C1)
                wait(act, hid_lo_ok, n * C1)
            f = slice(0, F1C[ORDER1[i]])
            act.activation(hid[f, i % 2, :], ring[f, banks(i), :], ACT.Silu).then_inc(silu_ok, 1)

        def hidden_high(n, i):
            wait(act, *finished(n, i))
            if i >= 2:
                wait(act, down_ok, n * C1 + i - 1)
            else:
                wait(act, down_ok, n * C1)
            f = slice(0, F1C[ORDER1[i]])
            act.activation(hid_hi[f, i % 2, :], hid[f, i % 2, :], ACT.Copy).then_inc(hid_hi_ok, 1)

        for k in range(KD):
            transposed(0, 0, k)

        def body(n, par, last):
            first_part(n, 0)
            first_part(n, 1)
            for c in range(2, NQK):
                second_part(n, c - 2)
                first_part(n, c)
            second_part(n, NQK - 2)
            second_part(n, NQK - 1)
            wait(act, route, n + 1)
            act.activation(score[:], logit[:], ACT.Exp).then_inc(exp_ok, 1)
            silu_of(n, 0)
            for i in range(1, C1):
                silu_of(n, i)
                hidden_high(n, i - 1)
                if i - 1 in TURN_AT and not last:
                    transposed(n + 1, 1 - par, TURN_AT.index(i - 1))
            hidden_high(n, C1 - 1)

        steps(act, body)

    @block.gpsimd
    def _(pool):
        pool.memset(v_sb[:], 0.0).then_inc(ones_ok, 1)
        wait(pool, ones_ok, 1)
        pool.memset(v_sb[:, :, :, HD:HD + 1], 1.0).then_inc(ones_ok, 1)
        wait(pool, ones_ok, 2)

        def hidden_low(n, i):
            wait(pool, hid_hi_ok, n * C1 + i + 1)
            f = slice(0, F1C[ORDER1[i]])
            pool.tensor_tensor(hid_lo[f, i % 2, :], hid[f, i % 2, :], hid_hi[f, i % 2, :],
                               ALU.subtract).then_inc(hid_lo_ok, 1)

        def body(n, par, last):
            for c in range(NQK):
                wait(pool, part2, n * NQK + c + 1)
                pool.tensor_tensor(parts[:, c, 2, :], rest[:, c, :], parts[:, c, 1, :],
                                   ALU.subtract).then_inc(part3, 1)
            for i in range(C1):
                hidden_low(n, i)
            for h in range(TT // 2):
                wait(pool, x2_ok, n * 2 + h + 1)
                t = bass.ds(n * TT + 2 * h, 2)
                pool.tensor_tensor(x_sb[:, t, :], x_sb[:, t, :],
                                   bo_row[:].rearrange("p (o d) -> p o d", o=1).broadcast_to([P, 2, D]),
                                   ALU.add).then_inc(out_ok, 1)

        steps(pool, body)
        wait(pool, out_ok, 2 * NB)

    @block.sync
    def _(sp):
        def store(b, u, base):
            for c in range(NQK):
                wait(sp, part3, base * NQK + c + 1)
                dram = scratch["q_parts" if c < KD else "k_parts"]
                rows = slice((c % KD) * P, (c % KD + 1) * P)
                dst = dram[bass.ds(b, 1), :, rows, u * BLK:(u + 1) * BLK]
                sp.dma_start(dst.rearrange("b r p t -> p (b r) t"), parts[:, c, :, :]).then_inc(parts_out[c], 16)
            wait(sp, v_ok, base * 2 + 2)
            sp.dma_start(scratch["v"][bass.ds(base * TT, TT), :, :].rearrange("n p f -> p n f"),
                         v_sb[:].rearrange("p n h w -> p n (h w)")).then_inc(v_out, 16)

        with sp.Fori(0, B) as b:
            for u in range(S // BLK):
                store(b, u, b * (S // BLK) + u)
        wait(sp, v_out, NB * 16)
        for p in parts_out:
            wait(sp, p, NB * 16)

    @block.vector
    def _(dve):
        wait(dve, ones_ok, 2)
        dve.tensor_copy(ident_bf[:], ident[:]).then_inc(ident_bf_ok, 1)

        def normalised(m):
            wait(dve, xt_ps, m * KD)
            for j in range(TT):
                t = bass.ds(m * TT + j, 1)
                dve.tensor_scalar(x_tok[:, j, :], x_sb[:, t, :], rstd[:, t], shift[:, t], ALU.mult,
                                  ALU.add).then_inc(xtok, 1)

        def transposed_low(m, par, k):
            wait(dve, xt_hi_ok, m * KD + k + 1)
            dve.tensor_tensor(xt_lo[:, par, k, :], misc, xt_hi[:, par, k, :], ALU.subtract).then_inc(xt_lo_ok, 1)

        def product(n, i):
            wait(dve, silu_ok, n * C1 + i + 1)
            wait(dve, gu_ps, n * 2 * C1 + 2 * i + 2)
            f = slice(0, F1C[ORDER1[i]])
            dve.tensor_tensor(hid[f, i % 2, :], hid[f, i % 2, :], ring[f, banks(i) + 1, :],
                              ALU.mult).then_inc(prod_ok, 1)

        def weigh(n, i):
            wait(dve, prod_ok, n * C1 + i + 1)
            wait(dve, spread_ps, n * CX + ORDER1[i] + 1)
            dve.tensor_tensor(hid[:, i % 2, :], hid[:, i % 2, :], spread[:, :], ALU.mult).then_inc(weighted_ok, 1)

        def ranks(chain, out_rank, values, before, n, g):
            shape = [P, TT, g, g]
            other = values[:].rearrange("p t (a j) -> p t a j", a=1).broadcast_to(shape)
            own = values[:].rearrange("p t (i a) -> p t i a", a=1).broadcast_to(shape)
            ab, eq = above[:, :, 0:g, 0:g], equal[:, :, 0:g, 0:g]
            chain(dve.tensor_tensor(ab, other, own, ALU.is_gt), needed=False)
            chain(dve.tensor_tensor(eq, other, own, ALU.is_equal))
            chain(dve.tensor_tensor(eq, eq, before[:], ALU.mult))
            chain(dve.tensor_tensor(ab, ab, eq, ALU.add))
            chain(dve.tensor_reduce(out_rank[:], ab, AX.X, ALU.add))

        ROUTE_STEPS = 22
        chained = sem("l1_route_chain")

        done = [0]

        def chain_of(n):
            def chain(ins, needed=True):
                ins.then_inc(chained, 1)
                done[0] += 1
                if needed:
                    wait(dve, chained, n * ROUTE_STEPS + done[0])
            return chain

        def wide(t):
            return t[:].rearrange("p (t a) -> p t a", a=1).broadcast_to([P, TT, NX])

        def route_groups(n):
            chain = chain_of(n)
            wait(dve, exp_ok, n + 1)
            chain(dve.tensor_reduce(total[:], score[:], AX.X, ALU.add))
            chain(dve.reciprocal(total[:], total[:]))
            chain(dve.tensor_tensor(score[:], score[:], wide(total), ALU.mult))
            pairs = score[:].rearrange("p t (g e) -> p t g e", e=2)
            chain(dve.tensor_tensor(group[:], pairs[:, :, :, 0], pairs[:, :, :, 1], ALU.max))
            ranks(chain, g_rank, group, before4, n, NX // 2)

        def route_experts(n):
            chain = chain_of(n)
            chain(dve.tensor_scalar(g_rank[:], g_rank[:], 2.0, None, ALU.is_lt))
            chain(dve.tensor_tensor(kept[:].rearrange("p t (g e) -> p t g e", e=2),
                                    score[:].rearrange("p t (g e) -> p t g e", e=2),
                                    g_rank[:].rearrange("p t (g a) -> p t g a", a=1).broadcast_to([P, TT, NX // 2, 2]),
                                    ALU.mult))
            ranks(chain, rank, kept, before8, n, NX)

        def route_weights(n):
            chain = chain_of(n)
            chain(dve.scalar_tensor_tensor(w_rest[:], rank[:], 2.0, kept[:], ALU.is_lt, ALU.mult))
            wait(dve, turned_ps, n)
            for r in range(PART):
                part = w_parts[:, :, r * LANE:r * LANE + NX]
                if r < PART - 1:
                    chain(dve.tensor_copy(part, w_rest[:]))
                    chain(dve.tensor_tensor(w_rest[:], w_rest[:], part, ALU.subtract))
                else:
                    dve.tensor_copy(part, w_rest[:]).then_inc(w_ready, 1)
            assert done[0] == ROUTE_STEPS, done[0]

        normalised(0)
        for k in range(KD):
            transposed_low(0, 0, k)

        def body(n, par, last):
            done[0] = 1
            wait(dve, logits_ok, n + 1)
            dve.tensor_reduce(top[:], logits, AX.X, ALU.max).then_inc(chained, 1)
            wait(dve, chained, n * ROUTE_STEPS + 1)
            dve.tensor_tensor(logit[:], logits, top[:].rearrange("p (t a) -> p t a", a=1).broadcast_to([P, TT, NX]),
                              ALU.subtract).then_inc(route, 1)
            for c in range(NQK):
                wait(dve, part1, n * NQK + c + 1)
                wait(dve, part3, (n - 1) * NQK + c + 1)
                dve.scalar_tensor_tensor(rest[:, c, :], ring[:, c, :], qk_bias[:, c:c + 1], parts[:, c, 0, :],
                                         ALU.add, ALU.subtract).then_inc(rest_ok, 1)
            for h in range(2):
                wait(dve, v_ps, n * 2 + h + 1)
                src = ring[:, h, :].rearrange("p (t h d) -> p t h d", t=2, h=H)
                if h == 0:
                    wait(dve, v_out, n * 16)
                dve.tensor_tensor(v_sb[:, 2 * h:2 * h + 2, :, 0:HD], src,
                                  bv_row[:].rearrange("p (o h d) -> p o h d", o=1, h=H).broadcast_to([P, 2, H, HD]),
                                  ALU.add).then_inc(v_ok, 1)
            route_groups(n)
            for i in range(C1):
                product(n, i)
                if i == 0:
                    route_experts(n)
                if i == 1:
                    route_weights(n)
                if i == C1 - CX:
                    wait(dve, turned_ps, n + 1)
                    wait(dve, spread_ps, n * CX)
                    dve.tensor_copy(w_turned[:], turned).then_inc(w_turned_ok, 1)
                if ORDER1[i] < CX:
                    weigh(n, i)
                if i == TURN_AT[0] - 2 and not last:
                    normalised(n + 1)
                if i in TURN_AT and not last:
                    transposed_low(n + 1, 1 - par, TURN_AT.index(i))
            for h in range(TT // 2):
                wait(dve, down_ok, n * C1 + C1)
                t = bass.ds(n * TT + 2 * h, 2)
                dve.tensor_tensor(x_sb[:, t, :], x_sb[:, t, :], acc[:, 2 * h:2 * h + 2, :], ALU.add).then_inc(x2_ok, 1)

        steps(dve, body)
        wait(dve, x2_ok, 2 * NB)


HG = 4
NHG = H // HG
NG = B * NHG
KT = S // P
HALF = S // 2
STEPS = 2 * KT * 2
UNITS = HG * KT * 2
LEAD = 8
ROWS = 6 * HD
SLOTS = ((0, 0), (1, 0), (2, 0), (0, 1), (1, 1), (0, 2))
TASKS = {hg: [(2, "turn", 1), (18, "turn", 0), (26, "maxima", 0)] for hg in range(NHG)}
TASKS[0] += [(5, "features", (1, 0)), (7, "features", (1, 1)), (10, "project", (1, 0)), (12, "project", (1, 1))]
TASKS[NHG - 1] += [(20, "features", (0, 0)), (21, "features", (0, 1)), (22, "project", (0, 0)), (24, "project", (0, 1))]
for tasks in TASKS.values():
    tasks.sort()
CARRIED = 5
PER_BATCH = sum(len(t) for t in TASKS.values())


def task_number(b, hg, task, arg):
    before = sum(len(TASKS[g]) for g in range(hg)) + [t[1:] for t in TASKS[hg]].index((task, arg))
    return b * PER_BATCH + before + 1 - CARRIED - (1 if isinstance(b, int) and b == B else 0)


def run_layer1_attention(nc, a, scope, sem, x_sb, ident, scratch, out):
    def sb(name, shape, dt=F32):
        return scope.enter_context(nc.sbuf_tensor(name, shape, dt))

    q_stack, k_stack = (sb(n, [P, NHG, HG, S], BF16) for n in ("q_stack", "k_stack"))
    v_cur = sb("v_cur", [P, NHG, KT, HG * VW])
    probs = sb("probs", [P, 2, 2, HALF])
    o_sb = sb("o_sb", [P, HALF])
    att = sb("att", [P, KT, D])
    at_hi, at_lo = sb("at_hi", [P, KD, HALF], F32R), sb("at_lo", [P, KD, HALF], F32R)
    wo, wo_hi, wo_lo = sb("wo", [P, KD, D]), sb("wo_hi", [P, KD, D], F32R), sb("wo_lo", [P, KD, D], F32R)
    inv = sb("inv", [P, 4, HG])
    half_max, neg_max, m_rest = sb("half_max", [P, UNITS]), sb("neg_max", [P, UNITS // 2]), sb("m_rest", [P, UNITS // 2])
    m_parts = sb("m_parts", [P, PART, UNITS // 2], BF16)
    m_rows = sb("m_rows", [PART * UNITS // 2, P], BF16)
    ident_b = sb("ident_b", [P, P], BF16)
    ps = scope.enter_context(nc.psum_tensor("ps2", [P, 8, 512], F32))
    scores = ps[:, 0:4, :].rearrange("p (u j) n -> p u j n", u=2)
    maxima, o_ps, spare = ps[:, 4:6, :], ps[:, 6, :], ps[:, 7, :]

    qk_in = [sem(f"at_qk_in{i}") for i in range(NHG)]
    v_in = [sem(f"at_v_in{i}") for i in range(NHG)]
    names = ("at_wo_in at_wo_hi at_wo_lo at_ones at_ident at_scores_ps at_exp at_pv at_max_ps at_reduced at_o_out "
             "at_spare_ps at_spare_done at_split at_m_in at_inv at_high at_out").split()
    (wo_in, wo_hi_ok, wo_lo_ok, ones_ok, ident_ok, scores_ps, exp_ok, pv_ok, max_ps, reduced, o_out, spare_ps,
     spare_done, split_ok, m_in, inv_ok, high_ok, out_done) = (sem(n) for n in names)
    TAIL = [(task, arg) for _, task, arg in TASKS[0][:CARRIED]]
    block = scope.enter_context(nc.Block())

    def batches(eng, body):
        body(0, False)
        with eng.Fori(1, B - 1) as b:
            body(b, False)
        body(B - 1, True)

    def tasks_at(b, hg, s):
        for i, (at, task, arg) in enumerate(TASKS[hg]):
            carried = isinstance(b, int) and b == 0 and hg == 0 and i < CARRIED
            ended = isinstance(b, int) and b == B - 1 and hg == NHG - 1 and task == "maxima"
            if at == s and not carried and not ended:
                yield task, arg

    def max_units(b, hg, s, last):
        ahead, u = (1, s + LEAD) if s < STEPS - LEAD else (2, s + LEAD - STEPS)
        if last and hg + ahead >= NHG:
            return []
        return [(b * NHG + hg + ahead, (hg + ahead) % NHG, 2 * u + i) for i in range(2)]

    def unit(u):
        return u // (2 * KT), u // 2 % KT, u % 2

    @block.sync
    def _(sp):
        sp.dma_start(wo[:], a["w_o"].rearrange("(k p) o -> p k o", p=P)).then_inc(wo_in, 16)

        def load_qk(b, hg):
            for i, parts in enumerate(SLOTS):
                for name, stack, part in zip(("q_parts", "k_parts"), (q_stack, k_stack), parts):
                    src = scratch[name][bass.ds(b, 1), part, hg * HG * HD:(hg + 1) * HG * HD, :]
                    sp.dma_start(stack[i * HD:(i + 1) * HD, hg, :, :],
                                 src.rearrange("b (h d) t -> d (b h) t", h=HG)).then_inc(qk_in[hg], 16)

        def load_v(b, hg):
            src = scratch["v"][bass.ds(b * KT, KT), :, hg * HG * VW:(hg + 1) * HG * VW]
            sp.dma_start(v_cur[:, hg, :, :], src.rearrange("n p f -> p n f")).then_inc(v_in[hg], 16)

        def turn_maxima(number, hg):
            sp.wait_ge(spare_done, number + 1)
            for r in range(PART):
                n = UNITS // 2
                sp.dma_start(q_stack[ROWS + r:ROWS + r + 1, hg, :, :].rearrange("o j (q t) -> o (j q) t", t=P),
                             m_rows[r * n:(r + 1) * n, :]).then_inc(m_in, 16)

        load_qk(0, 0)
        load_v(0, 0)
        load_qk(0, 1)
        turn_maxima(0, 0)

        def store(b, hg, half, o):
            sp.wait_ge(spare_done, task_number(b, hg, "project", (half, o)) + 1)
            t = bass.ds(b * KT + (2 * o if half == 0 else 2 * o - 4), 2)
            sp.dma_start(out.rearrange("b (n p) d -> p (b n) d", p=P)[:, t, :], x_sb[:, t, :]).then_inc(out_done, 16)

        def body(b, last):
            for hg in range(NHG):
                g = b * NHG + hg
                if not (last and hg >= NHG - 2):
                    wait(sp, scores_ps, (g - 1) * STEPS)
                    load_qk(b + (hg + 2) // NHG, (hg + 2) % NHG)
                if not (last and hg == NHG - 1):
                    wait(sp, pv_ok, (g - 2) * STEPS)
                    load_v(b + (hg + 1) // NHG, (hg + 1) % NHG)
                for s in range(STEPS):
                    for task, arg in tasks_at(b, hg, s):
                        if task == "project":
                            store(b, hg, *arg)
                        if task == "maxima":
                            turn_maxima(task_number(b, hg, task, arg), (hg + 1) % NHG)

        batches(sp, body)
        for o in range(2):
            store(B, 0, 1, o)
        sp.wait_ge(out_done, 4 * B * 16)

    @block.gpsimd
    def _(pool):
        pool.memset(k_stack[ROWS:P, :, :, :], 1.0).then_inc(ones_ok, 1)
        pool.wait_ge(ones_ok, 1)

    @block.tensor
    def _(pe):
        def score_block(b, hg, t, s):
            if s == 0:
                pe.wait_ge(qk_in[hg], (b + 1) * 2 * len(SLOTS) * 16)
                pe.wait_ge(m_in, (b * NHG + hg + 1) * PART * 16)
            wait(pe, exp_ok, t - 1)
            half, kt, pair = s // (2 * KT), s // 2 % KT, s % 2
            for jj in range(2):
                j = 2 * pair + jj
                ins = pe.matmul(scores[:, s % 2, jj, :], k_stack[0:ROWS + PART, hg, j, kt * P:(kt + 1) * P],
                                q_stack[0:ROWS + PART, hg, j, half * HALF:(half + 1) * HALF], start=True, stop=True)
            ins.then_inc(scores_ps, 1)

        def max_block(g, hg, u):
            j, qt, kh = unit(u)
            wait(pe, reduced, g * UNITS + u - 1)
            pe.matmul(maxima[:, u % 2, :], q_stack[0:ROWS, hg, j, qt * P:(qt + 1) * P],
                      k_stack[0:ROWS, hg, j, kh * HALF:(kh + 1) * HALF], start=True, stop=True).then_inc(max_ps, 1)

        def weighted_values(b, hg, t, s):
            half, kt, pair = s // (2 * KT), s // 2 % KT, s % 2
            if s == 0:
                pe.wait_ge(v_in[hg], (b + 1) * 16)
            if kt == 0 and pair == 0:
                wait(pe, o_out, (b * NHG + hg) * 2 + half)
            pe.wait_ge(exp_ok, t + 1)
            for jj in range(2):
                j = 2 * pair + jj
                ins = pe.matmul(o_ps[32 * j:32 * j + VW, :], v_cur[:, hg, kt, j * VW:(j + 1) * VW],
                                probs[:, s % 2, jj, :], start=(kt == 0), stop=(kt == KT - 1))
            ins.then_inc(pv_ok, 1)

        def spare_task(n, b, hg, task, arg):
            wait(pe, spare_done, n)
            if task == "turn":
                done = (b * NHG + hg) * 2 + (1 if arg == 0 else 0)
                pe.wait_ge(o_out, done)
                for t in range(4):
                    ins = pe.transpose(spare[:, t * P:(t + 1) * P], o_sb[:, t * P:(t + 1) * P], ident[:])
            elif task == "maxima":
                pe.wait_ge(split_ok, b * NHG + hg + 2)
                ins = pe.transpose(spare[0:PART * UNITS // 2, 0:P // 2].bitcast(BF16),
                                   m_parts[:].rearrange("p r n -> p (r n)"), ident_b[:])
            elif task == "features":
                half, k = arg
                for t in range(4):
                    ins = pe.transpose(spare[:, t * P:(t + 1) * P], att[:, 4 * half + t, k * P:(k + 1) * P], ident[:])
            else:
                half, o = arg
                for tt in range(2):
                    t, dst = slice((2 * o + tt) * P, (2 * o + tt + 1) * P), spare[:, tt * D:(tt + 1) * D]
                    for k in range(KD):
                        pe.matmul(dst, at_hi[:, k, t], wo_hi[:, k, :], start=(tt == 0 and k == 0), stop=False,
                                  skip_group_check=True)
                        pe.matmul(dst, at_lo[:, k, t], wo_hi[:, k, :], start=False, stop=False, skip_group_check=True)
                        ins = pe.matmul(dst, at_hi[:, k, t], wo_lo[:, k, :], start=False, stop=(k == KD - 1),
                                        skip_group_check=True)
            ins.then_inc(spare_ps, 1)

        pe.wait_ge(ones_ok, 1)
        pe.wait_ge(ident_ok, 1)
        pe.wait_ge(wo_lo_ok, 1)
        pe.wait_ge(qk_in[0], 2 * len(SLOTS) * 16)
        for u in range(UNITS):
            max_block(0, 0, u)
        pe.wait_ge(split_ok, 1)
        pe.transpose(spare[0:PART * UNITS // 2, 0:P // 2].bitcast(BF16), m_parts[:].rearrange("p r n -> p (r n)"),
                     ident_b[:]).then_inc(spare_ps, 1)
        pe.wait_ge(qk_in[1], 2 * len(SLOTS) * 16)
        for u in range(2 * LEAD):
            max_block(1, 1, u)
        score_block(0, 0, 0, 0)

        def body(b, last):
            for hg in range(NHG):
                g = b * NHG + hg
                for s in range(STEPS):
                    t = g * STEPS + s
                    if s < STEPS - 1:
                        score_block(b, hg, t + 1, s + 1)
                    elif not (last and hg == NHG - 1):
                        score_block(b + (hg + 1) // NHG, (hg + 1) % NHG, t + 1, 0)
                    for mg, mh, u in max_units(b, hg, s, last):
                        if u == 0:
                            pe.wait_ge(qk_in[mh], (b + (hg + 2) // NHG + 1) * 2 * len(SLOTS) * 16)
                        max_block(mg, mh, u)
                    weighted_values(b, hg, t, s)
                    for task, arg in tasks_at(b, hg, s):
                        spare_task(task_number(b, hg, task, arg), b, hg, task, arg)

        batches(pe, body)
        for task, arg in TAIL:
            spare_task(task_number(B, 0, task, arg), B, 0, task, arg)

    @block.scalar
    def _(act):
        act.wait_ge(wo_in, 16)
        act.activation(wo_hi[:], wo[:], ACT.Copy).then_inc(wo_hi_ok, 1)

        def exponentials(t, s):
            act.wait_ge(scores_ps, t + 1)
            wait(act, pv_ok, t - 1)
            act.activation(probs[:, s % 2, :, :], scores[:, s % 2, :, :], ACT.Exp,
                           scale=1.0 / HD ** 0.5).then_inc(exp_ok, 1)

        def take_out(b, hg, half):
            h = (b * NHG + hg) * 2 + (0 if half == 0 else -1)
            act.wait_ge(pv_ok, (h + 1) * (STEPS // 2))
            if half == 0:
                if not (isinstance(b, int) and b == 0 and hg == 0):
                    act.wait_ge(spare_ps, task_number(b, hg, "turn", 1) + 1)
            else:
                before = (b, hg - 1) if hg else (b - 1, NHG - 1)
                act.wait_ge(spare_ps, task_number(*before, "turn", 0) + 1)
            act.activation(o_sb[:], o_ps[:], ACT.Copy).then_inc(o_out, 1)

        def high(n, arg):
            act.wait_ge(spare_ps, n + 1)
            act.activation(at_hi[:, arg[1], :], spare[:, :], ACT.Copy).then_inc(high_ok, 1)

        def body(b, last):
            for hg in range(NHG):
                g = b * NHG + hg
                for s in range(STEPS):
                    exponentials(g * STEPS + s, s)
                    if s == STEPS // 2:
                        take_out(b, hg, 0)
                    if s == 0 and not (isinstance(b, int) and b == 0 and hg == 0):
                        take_out(b, hg, 1)
                    for task, arg in tasks_at(b, hg, s):
                        if task == "features":
                            high(task_number(b, hg, task, arg), arg)

        batches(act, body)
        take_out(B, 0, 1)
        for task, arg in TAIL:
            if task == "features":
                high(task_number(B, 0, task, arg), arg)

    @block.vector
    def _(dve):
        dve.tensor_copy(ident_b[:], ident[:]).then_inc(ident_ok, 1)
        dve.wait_ge(wo_hi_ok, 1)
        dve.tensor_tensor(wo_lo[:], wo[:], wo_hi[:], ALU.subtract).then_inc(wo_lo_ok, 1)
        in_split = sem("at_in_split")

        def reduce_block(g, u):
            dve.wait_ge(max_ps, g * UNITS + u + 1)
            dve.tensor_reduce(half_max[:, u:u + 1], maxima[:, u % 2, :], AX.X, ALU.max, negate=True).then_inc(reduced, 1)

        def split_maxima(g):
            halves = half_max[:].rearrange("p (n k) -> p n k", k=2)
            dve.wait_ge(reduced, g * UNITS + UNITS)
            dve.tensor_tensor(neg_max[:], halves[:, :, 0], halves[:, :, 1], ALU.min).then_inc(in_split, 1)
            dve.wait_ge(in_split, g * 5 + 1)
            dve.tensor_copy(m_parts[:, 0, :], neg_max[:]).then_inc(in_split, 1)
            dve.wait_ge(in_split, g * 5 + 2)
            dve.tensor_tensor(m_rest[:], neg_max[:], m_parts[:, 0, :], ALU.subtract).then_inc(in_split, 1)
            dve.wait_ge(in_split, g * 5 + 3)
            dve.tensor_copy(m_parts[:, 1, :], m_rest[:]).then_inc(in_split, 1)
            dve.wait_ge(in_split, g * 5 + 4)
            dve.tensor_tensor(neg_max[:], m_rest[:], m_parts[:, 1, :], ALU.subtract).then_inc(in_split, 1)
            dve.wait_ge(in_split, g * 5 + 5)
            dve.tensor_copy(m_parts[:, 2, :], neg_max[:]).then_inc(split_ok, 1)

        def spare_task(n, b, hg, task, arg):
            dve.wait_ge(spare_ps, n + 1)
            if task == "turn":
                h = (b * NHG + hg) * 2 + (0 if arg == 0 else -1)
                src = spare[:, :].rearrange("p (t j w) -> p t j w", t=4, j=HG)
                dve.reciprocal(inv[:], src[:, :, :, HD]).then_inc(inv_ok, 1)
                dve.wait_ge(inv_ok, h + 1)
                g = hg if arg == 0 else (hg - 1) % NHG
                half = arg
                dst = att[:, 4 * half:4 * half + 4, g * HG * HD:(g + 1) * HG * HD]
                dve.tensor_tensor(dst.rearrange("p t (j d) -> p t j d", j=HG), src[:, :, :, 0:HD],
                                  inv[:].rearrange("p t (j o) -> p t j o", o=1).broadcast_to([P, 4, HG, HD]),
                                  ALU.mult).then_inc(spare_done, 1)
            elif task == "maxima":
                dve.wait_ge(m_in, (b * NHG + hg + 1) * PART * 16)
                dve.tensor_copy(m_rows[:], spare[0:PART * UNITS // 2, 0:P // 2].bitcast(BF16)).then_inc(spare_done, 1)
            elif task == "features":
                half, k = arg
                dve.wait_ge(high_ok, 4 * b + 2 * half + k + 1 - (4 if half else 0))
                dve.tensor_tensor(at_lo[:, k, :], spare[:, :], at_hi[:, k, :], ALU.subtract).then_inc(spare_done, 1)
            else:
                half, o = arg
                tile = bass.ds(b * KT + 4 * half - (KT if half else 0) + 2 * o, 2)
                dve.tensor_tensor(x_sb[:, tile, :], x_sb[:, tile, :],
                                  spare[:, :].rearrange("p (t d) -> p t d", t=2), ALU.add).then_inc(spare_done, 1)

        for u in range(UNITS):
            reduce_block(0, u)
        split_maxima(0)
        dve.wait_ge(spare_ps, 1)
        dve.tensor_copy(m_rows[:], spare[0:PART * UNITS // 2, 0:P // 2].bitcast(BF16)).then_inc(spare_done, 1)
        for u in range(2 * LEAD):
            reduce_block(1, u)

        def body(b, last):
            for hg in range(NHG):
                for s in range(STEPS):
                    if s == STEPS - LEAD and not (last and hg == NHG - 1):
                        split_maxima(b * NHG + hg + 1)
                    for g, _, u in max_units(b, hg, s, last):
                        reduce_block(g, u)
                    for task, arg in tasks_at(b, hg, s):
                        spare_task(task_number(b, hg, task, arg), b, hg, task, arg)

        batches(dve, body)
        for task, arg in TAIL:
            spare_task(task_number(B, 0, task, arg), B, 0, task, arg)


_T = {"L0_attn_Wq": "Wq", "L0_attn_Wk": "Wk", "L0_attn_Wv": "Wv", "L0_attn_Wqa": "Wqa", "L0_attn_Wka": "Wka",
      "L0_ffn_gate_idx": "gate_idx", "L0_ffn_up_idx": "up_idx", "L0_ffn_down_idx": "down_idx",
      "L1_attn_w_qkv": "w_qkv", "L1_attn_w_o": "w_o", "L1_ffn_gate_weight": "router", "L1_ffn_gate_w": "gate_w",
      "L1_ffn_up_w": "up_w", "L1_ffn_down_w": "down_w", "L1_ffn_sh_gate_w": "sh_gate", "L1_ffn_sh_up_w": "sh_up",
      "L1_ffn_sh_down_w": "sh_down"}
_COLUMNS = {"L0_attn_bq": "bq", "L0_attn_bk": "bk", "L0_attn_bv": "bv", "L0_attn_bqa": "bqa", "L0_attn_bka": "bka",
            "L0_attn_ln_g": "ln_g", "L0_attn_ln_b": "ln_b", "L1_attn_b_qkv": "b_qkv"}
_ROWS = {"L0_ffn_lut": "lut", "L1_attn_b_qkv": "b_qkv_row", "L1_attn_b_o": "b_o"}


def lay_out(inputs):
    import numpy as _np

    laid = {"x": _np.ascontiguousarray(inputs["L0_attn_hidden_states"]).reshape(B * S, D)}
    for name, short in _T.items():
        laid[short] = _np.ascontiguousarray(_np.swapaxes(_np.asarray(inputs[name]), -1, -2))
    for name, short in _COLUMNS.items():
        laid[short] = _np.ascontiguousarray(_np.asarray(inputs[name]).reshape(-1, P).T)
    for name, short in _ROWS.items():
        laid[short] = _np.ascontiguousarray(inputs[name])
    return laid


def kernel(**inputs):
    import concourse.bacc as _bacc
    from concourse.bass_utils import run_bass_kernel_spmd as _run

    laid = lay_out(inputs)
    nc = _bacc.Bacc("TRN2", target_bir_lowering=False, num_devices=1)
    a = {n: nc.dram_tensor(f"in_{n}", v.shape, mybir.dt.from_np(v.dtype), kind="ExternalInput").ap()
         for n, v in laid.items()}
    out = nc.dram_tensor("out_0", (B, S, D), F32, kind="ExternalOutput").ap()
    build(nc, a, out)
    r = _run(nc, [{f"in_{n}": v for n, v in laid.items()}], core_ids=[0])
    return r.results[0]["out_0"]
```

```python
from contextlib import ExitStack

import concourse.bass as bass
from concourse import mybir

F32 = mybir.dt.float32
F32R = mybir.dt.float32r
BF16 = mybir.dt.bfloat16
I32 = mybir.dt.int32
ALU = mybir.AluOpType
ACT = mybir.ActivationFunctionType
AX = mybir.AxisListType

P = 128
B, S, D = 4, 1024, 256
KD = D // P
BLK = 512
NB = B * S // BLK
TT = BLK // P
NT = B * S // P
EPS = 1e-5
SCALE0 = 1.0 / D ** 0.5

F0 = 688
C0 = 6
F0C = [116] * 5 + [F0 - 5 * 116]
LUT = 16
FLAT0 = 4 * F0 + C0 * D
LC = 480
NLC = -(-FLAT0 // LC)

WQ, WK, WV, WQA, WKA = range(5)

H, HD = 16, D // 16
NX, FX, FS = 8, 176, 352
F1 = NX * FX + FS
CX = NX * FX // P
F1C = [P] * CX + [120, 120, 112]
C1 = len(F1C)
PART = 3
VW = 32
LANE = 32


def wait(eng, sem, value):
    if not isinstance(value, int) or value > 0:
        eng.wait_ge(sem, value)


def split3(pe, out, w_hi, w_lo, x_hi, x_lo, first, last):
    pe.matmul(out, w_hi, x_hi, start=first, stop=False, skip_group_check=True)
    pe.matmul(out, w_lo, x_hi, start=False, stop=False, skip_group_check=True)
    return pe.matmul(out, w_hi, x_lo, start=False, stop=last, skip_group_check=True)


def layer_norm_stats(sem, mean, var, raw, name):
    done = sem(f"{name}_stats_done")
    stats, work = raw
    steps = 6

    def run(dve):
        mean_e, mean_o = stats[:, :, 1], stats[:, :, 4]
        dve.tensor_tensor(work[:, 0, :], mean_e, mean_o, ALU.add).then_inc(done, 1)
        dve.tensor_tensor(work[:, 1, :], mean_e, mean_o, ALU.subtract).then_inc(done, 1)
        dve.tensor_tensor(work[:, 2, :], stats[:, :, 2], stats[:, :, 5], ALU.add).then_inc(done, 1)
        dve.wait_ge(done, 1)
        dve.tensor_scalar(mean[:], work[:, 0, :], 0.5, None, ALU.mult).then_inc(done, 1)
        dve.wait_ge(done, 2)
        dve.scalar_tensor_tensor(work[:, 3, :], work[:, 1, :], 0.25, work[:, 1, :], ALU.mult, ALU.mult).then_inc(done, 1)
        dve.wait_ge(done, 5)
        dve.scalar_tensor_tensor(var[:], work[:, 2, :], 1.0 / D, work[:, 3, :], ALU.mult, ALU.add).then_inc(done, 1)
        dve.wait_ge(done, steps)
    return run, (done, steps)


def build(nc, a, out, stop_after=None):
    with ExitStack() as whole:
        def persistent(name, shape, dt, ctx=whole):
            return ctx.enter_context(nc.sbuf_tensor(name, shape, dt))

        def sem(name):
            return whole.enter_context(nc.semaphore(name))

        x_sb = persistent("x_sb", [P, NT, D], F32)
        ident = persistent("ident", [P, P], F32)
        mean = persistent("mean", [P, NT], F32)
        var = persistent("var", [P, NT], F32)
        rstd = persistent("rstd", [P, NT], F32)
        shift = persistent("shift", [P, NT], F32)
        stats = persistent("stats", [P, NT, 6], F32)
        pair = persistent("stat_work", [P, 4, NT], F32)
        eps_col = persistent("eps_col", [P, 1], F32)
        x_loaded = sem("x_loaded")
        stored = sem("stored")

        ahead = ExitStack()
        raw = {n: ahead.enter_context(nc.sbuf_tensor(n, shape, F32, side="right")) for n, shape in
               (("gu_raw", [P, 2, KD, F1]), ("qkv_raw", [P, KD, 3 * D]), ("rt_raw", [P, KD, NX]))}
        raw_in = {n: sem(f"l1_{n}_loaded") for n in ("gu", "qkv")}

        def load_ahead(sp):
            qkv, rt, gu = raw["qkv_raw"], raw["rt_raw"], raw["gu_raw"]
            sp.dma_start(qkv[:], a["w_qkv"].rearrange("(k p) o -> p k o", p=P)).then_inc(raw_in["qkv"], 16)
            sp.dma_start(rt[:], a["router"].rearrange("(k p) o -> p k o", p=P)).then_inc(raw_in["qkv"], 16)
            for w, (routed_w, shared_w) in enumerate((("gate_w", "sh_gate"), ("up_w", "sh_up"))):
                for k in range(KD):
                    rows = slice(k * P, (k + 1) * P)
                    sp.dma_start(gu[:, w, k, 0:NX * FX].rearrange("p (n f) -> p n f", n=NX),
                                 a[routed_w][:, rows, :].rearrange("n p f -> p n f")).then_inc(raw_in["gu"], 16)
                    sp.dma_start(gu[:, w, k, NX * FX:F1], a[shared_w][rows, :]).then_inc(raw_in["gu"], 16)

        with ExitStack() as layer0:
            prepare_and_run_layer0(nc, a, layer0, sem, x_sb, ident, mean, var, rstd, shift, (stats, pair),
                                   eps_col, x_loaded, load_ahead)
        if stop_after != 0:
            scratch = {n: nc.dram_tensor(n, [B, PART, D, S], BF16) for n in ("q_parts", "k_parts")}
            scratch["v"] = nc.dram_tensor("v_scratch", [NT, P, H * VW], F32)
            run_layer1_ffn(nc, a, ahead, sem, x_sb, ident, mean, var, rstd, shift, (stats, pair), eps_col, scratch,
                           raw, raw_in)
        if stop_after is None:
            run_layer1_attention(nc, a, whole, sem, x_sb, ident, scratch, out)
        if stop_after in (0, 1):
            block = whole.enter_context(nc.Block())

            @block.sync
            def _(sp):
                sp.dma_start(out.rearrange("b (n p) d -> p (b n) d", p=P), x_sb[:]).then_inc(stored, 16)
                sp.wait_ge(stored, 16)


def prepare_and_run_layer0(nc, a, scope, sem, x_sb, ident, mean, var, rstd, shift, stat_raw, eps_col, x_loaded,
                           load_ahead):
    def sb(name, shape, dt, ctx=scope):
        return ctx.enter_context(nc.sbuf_tensor(name, shape, dt))

    w_hi = sb("w_hi", [P, 5, KD, D], F32R)
    w_lo = sb("w_lo", [P, 5, KD, D], F32R)
    f_hi = sb("f_hi", [P, NLC * LC], F32R)
    f_lo = sb("f_lo", [P, NLC * LC], F32R)
    bias = sb("bias", [P, 5, KD], F32)
    rstd_h = sb("rstd_h", [P, NT], F32)
    shift_h = sb("shift_h", [P, NT], F32)
    ones = sb("ones", [P, BLK], F32)

    def gate_up(t, w, k, c):
        lo = (2 * w + k) * F0 + sum(F0C[:c])
        return t[:, lo:lo + F0C[c]]

    def down(t, c):
        return t[0:F0C[c], 4 * F0 + c * D:4 * F0 + (c + 1) * D]

    with ExitStack() as ctx:
        def st(name, shape, dt):
            return sb(name, shape, dt, ctx)

        def pb(name, shape):
            return ctx.enter_context(nc.psum_tensor(name, shape, F32))

        w_raw = st("w_raw", [P, 5, KD, D], F32)
        b_raw = st("b_raw", [P, 5, KD], F32)
        ln_g, ln_b = st("ln_g", [P, KD], F32), st("ln_b", [P, KD], F32)
        idx = st("idx", [P, NLC * LC], I32)
        lut, lut_lo = st("lut", [P, LUT], F32), st("lut_lo", [P, LUT], F32R)
        lut_hi = st("lut_hi", [P, LUT], F32R)
        d_hi, d_lo = st("d_hi", [P, LUT, P], F32R), st("d_lo", [P, LUT, P], F32R)
        mask = st("mask", [P, 4, LC], F32R)
        small = st("small", [P, 4, NT], F32)
        pb_bias, pb_hi, pb_lo = pb("pb_bias", [P, 512]), pb("pb_hi", [P, 2, 512]), pb("pb_lo", [P, 2, 512])

        w_loaded, small_loaded, idx_loaded = sem("w_loaded"), sem("small_loaded"), sem("idx_loaded")
        lut_loaded, gate_loaded = sem("lut_loaded"), sem("gate_loaded")
        idx_zero, ident_ready, ident_zero = sem("idx_zero"), sem("ident_ready"), sem("ident_zero")
        lut_split, diag_hi, diag_lo, mask_ready, mask_used = (sem("lut_split"), sem("diag_hi"), sem("diag_lo"),
                                                              sem("mask_ready"), sem("mask_used"))
        weights_kept = sem("weights_kept")
        bias_ps, bias_ready, w_scaled, w_hi_ready, w_lo_ready = (sem("bias_ps"), sem("bias_ready"), sem("w_scaled"),
                                                                 sem("w_hi_ready"), sem("w_lo_ready"))
        stat_step, root_ready = sem("stat_step"), sem("root_ready")
        constants = sem("constants")
        x_rows = sem("x_rows")
        stats_of, stats_kept = layer_norm_stats(sem, mean, var, stat_raw, "ln0")

        def lut_chunks(eng, body):
            body(0, 0)
            with eng.Fori(0, (NLC - 1) // 2) as m:
                body(2 * m + 1, 1)
                body(2 * m + 2, 0)

        block = ctx.enter_context(nc.Block())

        @block.sync
        def _(sp):
            for w, name in enumerate(("gate_idx", "up_idx")):
                sp.dma_start(idx[:, 2 * w * F0:2 * (w + 1) * F0].rearrange("p (k f) -> p k f", k=KD),
                             a[name].rearrange("(k p) f -> p k f", p=P)).then_inc(idx_loaded if w else gate_loaded, 16)
            sp.wait_ge(idx_zero, 1)
            for c in range(C0):
                f = sum(F0C[:c])
                sp.dma_start(down(idx, c), a["down_idx"][f:f + F0C[c], :]).then_inc(idx_loaded, 16)
            sp.dma_start(x_sb[:], a["x"].rearrange("(n p) d -> p n d", p=P)).then_inc(x_loaded, 16)

        @block.scalar
        def _(act):
            act.dma_start(lut[:], a["lut"].rearrange("(o n) -> o n", o=1).broadcast_to([P, LUT])).then_inc(lut_loaded, 16)
            act.dma_start(ln_g[:], a["ln_g"]).then_inc(small_loaded, 16)
            act.dma_start(ln_b[:], a["ln_b"]).then_inc(small_loaded, 16)
            for i, name in enumerate(("q", "k", "v", "qa", "ka")):
                act.dma_start(w_raw[:, i, :, :], a["W" + name].rearrange("(k p) o -> p k o", p=P)).then_inc(w_loaded, 16)
                act.dma_start(b_raw[:, i, :], a["b" + name]).then_inc(small_loaded, 16)
            act.wait_ge(lut_split, 2)
            act.wait_ge(ident_ready, 1)
            for j in range(LUT):
                act.activation(d_lo[:, j, :], ident[:], ACT.Copy, scale=lut_lo[:, j:j + 1].bitcast(F32)).then_inc(diag_lo, 1)

            def keep(i, par):
                act.wait_ge(mask_used, i * LUT + 4 + LUT)
                act.activation(f_hi[:, bass.ds(i * LC, LC)], pb_hi[:, par, 0:LC], ACT.Copy).then_inc(weights_kept, 1)
                act.activation(f_lo[:, bass.ds(i * LC, LC)], pb_lo[:, par, 0:LC], ACT.Copy).then_inc(weights_kept, 1)
                if isinstance(i, int):
                    act.wait_ge(bias_ps, 3 * KD)
                    for w in (WQ, WK, WV):
                        for k in range(KD):
                            act.activation(w_raw[:, w, k, :], w_raw[:, w, k, :], ACT.Copy,
                                           scale=ln_g[:, k:k + 1]).then_inc(w_scaled, 1)
                    act.wait_ge(w_scaled, 3 * KD)
                    for w in range(5):
                        act.activation(w_hi[:, w, :, :], w_raw[:, w, :, :], ACT.Copy).then_inc(w_hi_ready, 1)

            lut_chunks(act, keep)
            act.wait_ge(*stats_kept)
            act.wait_ge(constants, 2)
            act.activation(small[:, 0, :], var[:], ACT.Sqrt, bias=eps_col[:]).then_inc(root_ready, 1)
            act.wait_ge(stat_step, 3)
            act.activation(small[:, 2, :], small[:, 1, :], ACT.Sqrt, bias=eps_col[:]).then_inc(root_ready, 1)

        @block.gpsimd
        def _(pool):
            pool.memset(ident[:], 0.0).then_inc(ident_zero, 1)
            pool.wait_ge(ident_zero, 1)
            pool.affine_select(out=ident[:], in_=ident[:], compare_op=ALU.not_equal, fill=1.0, base=0,
                               pattern=[[-1, P]], channel_multiplier=1).then_inc(ident_ready, 1)
            pool.memset(idx[:, 4 * F0:], 0).then_inc(idx_zero, 1)
            for w in range(5):
                pool.wait_ge(w_hi_ready, w + 1)
                pool.tensor_tensor(w_lo[:, w, :, :], w_raw[:, w, :, :], w_hi[:, w, :, :],
                                   ALU.subtract).then_inc(w_lo_ready, 1)
            pool.wait_ge(w_lo_ready, 5)

        @block.vector
        def _(dve):
            dve.memset(ones[:], 1.0).then_inc(constants, 1)
            dve.memset(eps_col[:], EPS).then_inc(constants, 1)
            dve.wait_ge(lut_loaded, 16)
            dve.tensor_copy(lut_hi[:], lut[:]).then_inc(lut_split, 1)
            dve.wait_ge(lut_split, 1)
            dve.tensor_tensor(lut_lo[:], lut[:], lut_hi[:], ALU.subtract).then_inc(lut_split, 1)
            dve.wait_ge(ident_ready, 1)
            dve.wait_ge(gate_loaded, 16)

            def masks(i, par):
                first = isinstance(i, int)
                for j in range(LUT):
                    if first:
                        dve.tensor_scalar(d_hi[:, j, :], ident[:], lut_hi[:, j:j + 1].bitcast(F32), None,
                                          ALU.mult).then_inc(diag_hi, 1)
                    dve.wait_ge(mask_used, i * LUT + j + 1)
                    dve.tensor_scalar(mask[:, j % 4, :], idx[:, bass.ds(i * LC, LC)], float(j), None,
                                      ALU.is_equal).then_inc(mask_ready, 1)
                    if not first and j % 4 == 3:
                        t = bass.ds((i - 1) * TT + j // 4, 1)
                        dve.bn_stats(stat_raw[0][:, t, :], x_sb[:, t, :]).then_inc(x_rows, 1)
                if first:
                    dve.wait_ge(small_loaded, 7 * 16)
                    dve.wait_ge(bias_ps, 3 * KD)
                    for w in (WQ, WK, WV):
                        dve.tensor_tensor(bias[:, w, :], pb_bias[:, w * KD:(w + 1) * KD], b_raw[:, w, :],
                                          ALU.add).then_inc(bias_ready, 1)
                    for w in (WQA, WKA):
                        dve.tensor_scalar(bias[:, w, :], b_raw[:, w, :], SCALE0, None, ALU.mult).then_inc(bias_ready, 1)
                    dve.wait_ge(idx_loaded, (1 + C0) * 16)
                    dve.wait_ge(x_loaded, 16)

            lut_chunks(dve, masks)
            dve.wait_ge(x_rows, NT)
            stats_of(dve)
            dve.wait_ge(root_ready, 1)
            dve.reciprocal(rstd[:], small[:, 0, :]).then_inc(stat_step, 1)
            dve.wait_ge(stat_step, 1)
            dve.tensor_tensor(small[:, 3, :], rstd[:], rstd[:], ALU.mult).then_inc(stat_step, 1)
            dve.wait_ge(stat_step, 2)
            dve.tensor_tensor(small[:, 1, :], var[:], small[:, 3, :], ALU.mult).then_inc(stat_step, 1)
            dve.scalar_tensor_tensor(shift[:], mean[:], -1.0, rstd[:], ALU.mult, ALU.mult).then_inc(stat_step, 1)
            dve.wait_ge(root_ready, 2)
            dve.reciprocal(small[:, 0, :], small[:, 2, :]).then_inc(stat_step, 1)
            dve.wait_ge(stat_step, 5)
            dve.tensor_tensor(rstd_h[:], rstd[:], small[:, 0, :], ALU.mult).then_inc(stat_step, 1)
            dve.tensor_tensor(shift_h[:], shift[:], small[:, 0, :], ALU.mult).then_inc(stat_step, 1)

        @block.tensor
        def _(pe):
            pe.sem_inc(mask_used, 4)
            pe.sem_inc(weights_kept, 2)

            def look_up(i, par):
                first = isinstance(i, int)
                if not first:
                    pe.wait_ge(weights_kept, i * 2)
                for j in range(LUT):
                    if first:
                        pe.wait_ge(diag_hi, j + 1)
                        pe.wait_ge(diag_lo, j + 1)
                    pe.wait_ge(mask_ready, i * LUT + j + 1)
                    pe.matmul(pb_hi[:, par, 0:LC], d_hi[:, j, :], mask[:, j % 4, :], start=(j == 0), stop=(j == LUT - 1))
                    pe.matmul(pb_lo[:, par, 0:LC], d_lo[:, j, :], mask[:, j % 4, :], start=(j == 0),
                              stop=(j == LUT - 1)).then_inc(mask_used, 1)
                if first:
                    pe.wait_ge(w_loaded, 5 * 16)
                    pe.wait_ge(small_loaded, 7 * 16)
                    for w in (WQ, WK, WV):
                        for c in range(KD):
                            for k in range(KD):
                                ins = pe.matmul(pb_bias[:, w * KD + c:w * KD + c + 1], w_raw[:, w, k, c * P:(c + 1) * P],
                                                ln_b[:, k:k + 1], start=(k == 0), stop=(k == KD - 1),
                                                skip_group_check=True)
                            ins.then_inc(bias_ps, 1)

            lut_chunks(pe, look_up)

    run_layer0(nc, scope, sem, x_sb, ident, rstd, shift, rstd_h, shift_h, ones, bias, w_hi, w_lo, f_hi, f_lo,
               gate_up, down, stat_raw[0], load_ahead)


def run_layer0(nc, scope, sem, x_sb, ident, rstd, shift, rstd_h, shift_h, ones, bias, w_hi, w_lo, f_hi, f_lo,
               gate_up, down, stats, load_ahead):
    def sb(name, shape, dt=F32):
        return scope.enter_context(nc.sbuf_tensor(name, shape, dt))

    x_tok, h_tok = sb("x_tok", [P, TT, D]), sb("h_tok", [P, TT, D])
    xt_hi, xt_lo = sb("xt_hi", [P, 2 * KD, BLK], F32R), sb("xt_lo", [P, 2 * KD, BLK], F32R)
    q_sb, e_sb, sum_sb, rc_sb = (sb(n, [P, KD, BLK]) for n in ("q_sb", "e_sb", "sum_sb", "rc_sb"))
    pool1, sum2, pool2, mixed = (sb(n, [P, KD, BLK]) for n in ("pool1", "sum2", "pool2", "mixed"))
    c_hi, c_lo = sb("c_hi", [P, KD, BLK], F32R), sb("c_lo", [P, KD, BLK], F32R)
    silu, hid = sb("silu", [P, 2, BLK]), sb("hid", [P, 2, BLK])
    hid_hi, hid_lo = sb("hid_hi", [P, 2, BLK], F32R), sb("hid_lo", [P, 2, BLK], F32R)
    ps = scope.enter_context(nc.psum_tensor("ps0", [P, 8, 512], F32))
    proj = ps[:, 0:2, :]
    ring = ps[:, 2:6, :]
    acc = ps[:, 6:8, :].rearrange("p h (j d) -> p (h j) d", d=D)

    names = ("l0_xtok l0_htok l0_xt_ps l0_xt_hi l0_xt_lo l0_proj_ps l0_q l0_chi l0_clo l0_exp l0_times l0_sum "
             "l0_recip l0_weight l0_pooled l0_mixed l0_attn l0_gu_ps l0_silu l0_hid l0_hid_hi l0_hid_lo l0_down "
             "l0_acc_ps l0_x1 l0_stat_rows").split()
    (xtok, htok, xt_ps, xt_hi_ok, xt_lo_ok, proj_ps, q_ok, chi_ok, clo_ok, exp_ok, times_ok, sum_ok,
     recip_ok, weight_ok, pooled_ok, mixed_ok, attn_ok, gu_ps, silu_ok, hid_ok, hid_hi_ok, hid_lo_ok, down_ok,
     acc_ps, x1_ok, rows_ok) = (sem(n) for n in names)
    block = scope.enter_context(nc.Block())

    @block.sync
    def _(sp):
        load_ahead(sp)

    def steps(eng, body):
        for u in range(2):
            body(u, u, False)
        with eng.Fori(1, B - 1) as b:
            for u in range(2):
                body(b * 2 + u, u, False)
        for u in range(2):
            body((B - 1) * 2 + u, u, u == 1)

    @block.tensor
    def _(pe):
        def transposes(m, first=False):
            for t in range(2 * KD):
                wait(pe, xtok if t < KD else htok, m * TT + TT)
                if not first:
                    wait(pe, hid_ok if t % 2 else silu_ok, m * C0 - 1 + t // 2)
                tok, k = (x_tok, t) if t < KD else (h_tok, t - KD)
                for j in range(TT):
                    ins = pe.transpose(ring[:, t, j * P:(j + 1) * P], tok[:, j, k * P:(k + 1) * P], ident[:])
                ins.then_inc(xt_ps, 1)

        def projection(i, first, hi, lo):
            for c in range(KD):
                for k in range(KD):
                    o = slice(c * P, (c + 1) * P)
                    ins = split3(pe, proj[:, c, :], w_hi[:, i, k, o], w_lo[:, i, k, o], hi[:, first + k, :],
                                 lo[:, first + k, :], k == 0, k == KD - 1)
                ins.then_inc(proj_ps, 1)

        def gate_and_up(n, c):
            r = 2 * (c % 2)
            if c >= 2:
                wait(pe, silu_ok, n * C0 + c - 1)
                wait(pe, hid_ok, n * C0 + c - 1)
            for w in range(2):
                for k in range(KD):
                    ins = split3(pe, ring[0:F0C[c], r + w, :], gate_up(f_hi, w, k, c), gate_up(f_lo, w, k, c),
                                 xt_hi[:, k, :], xt_lo[:, k, :], k == 0, k == KD - 1)
                ins.then_inc(gu_ps, 1)

        def down_chunk(n, c):
            wait(pe, hid_hi_ok, n * C0 + c + 1)
            wait(pe, hid_lo_ok, n * C0 + c + 1)
            if c == 0:
                wait(pe, x1_ok, n * 2)
            for j in range(TT):
                t = slice(j * P, (j + 1) * P)
                f = slice(0, F0C[c])
                pe.matmul(acc[:, j, :], hid_hi[f, c % 2, t], down(f_hi, c), start=(c == 0 and j % 2 == 0),
                          stop=False, skip_group_check=True)
                pe.matmul(acc[:, j, :], hid_lo[f, c % 2, t], down(f_hi, c), start=False, stop=False,
                          skip_group_check=True)
                ins = pe.matmul(acc[:, j, :], hid_hi[f, c % 2, t], down(f_lo, c), start=False, stop=False,
                                skip_group_check=True)
            ins.then_inc(down_ok, 1)

        def first_chunk(m):
            wait(pe, xt_hi_ok, m * 4 + 4)
            wait(pe, xt_lo_ok, m * 4 + 4)
            gate_and_up(m, 0)

        def add_attention(m):
            for j in range(TT):
                for k in range(KD):
                    ins = pe.matmul(acc[:, j, k * P:(k + 1) * P], mixed[:, k, j * P:(j + 1) * P], ident[:],
                                    start=False, stop=(k == KD - 1 and j % 2 == 1), skip_group_check=True)
                if j % 2:
                    ins.then_inc(acc_ps, 1)

        transposes(0, first=True)
        first_chunk(0)

        def body(n, u, last):
            wait(pe, attn_ok, n * KD)
            projection(WQ, KD, xt_hi, xt_lo)
            if not (isinstance(n, int) and n == 0):
                add_attention(n - 1)
            gate_and_up(n, 1)
            wait(pe, chi_ok, n * 2 * KD + KD)
            wait(pe, clo_ok, n * 2 * KD + KD)
            projection(WQA, 0, c_hi, c_lo)
            gate_and_up(n, 2)
            wait(pe, exp_ok, n * 2 * KD + KD)
            projection(WK, KD, xt_hi, xt_lo)
            down_chunk(n, 0)
            gate_and_up(n, 3)
            down_chunk(n, 1)
            gate_and_up(n, 4)
            down_chunk(n, 2)
            wait(pe, chi_ok, n * 2 * KD + 2 * KD)
            wait(pe, clo_ok, n * 2 * KD + 2 * KD)
            projection(WKA, 0, c_hi, c_lo)
            gate_and_up(n, 5)
            down_chunk(n, 3)
            wait(pe, exp_ok, n * 2 * KD + 2 * KD)
            projection(WV, KD, xt_hi, xt_lo)
            if not last:
                transposes(n + 1)
            down_chunk(n, 4)
            down_chunk(n, 5)
            if not last:
                first_chunk(n + 1)

        steps(pe, body)
        wait(pe, attn_ok, NB * KD)
        add_attention(NB - 1)

    @block.scalar
    def _(act):
        def twice_normalised(m):
            wait(act, xt_ps, m * 4)
            for j in range(TT):
                t = bass.ds(m * TT + j, 1)
                act.activation(h_tok[:, j, :], x_sb[:, t, :], ACT.Identity, scale=rstd_h[:, t],
                               bias=shift_h[:, t]).then_inc(htok, 1)

        def transposed(m):
            for t in range(2 * KD):
                wait(act, xt_ps, m * 4 + t + 1)
                act.activation(xt_hi[:, t, :], ring[:, t, :], ACT.Copy).then_inc(xt_hi_ok, 1)

        def silu_of(n, c):
            wait(act, gu_ps, n * 2 * C0 + 2 * c + 1)
            if c >= 2:
                wait(act, hid_ok, n * C0 + c - 1)
            f = slice(0, F0C[c])
            act.activation(silu[f, c % 2, :], ring[f, 2 * (c % 2), :], ACT.Silu).then_inc(silu_ok, 1)

        def hidden_high(n, c):
            wait(act, hid_ok, n * C0 + c + 1)
            if c >= 2:
                wait(act, down_ok, n * C0 + c - 1)
            f = slice(0, F0C[c])
            act.activation(hid_hi[f, c % 2, :], hid[f, c % 2, :], ACT.Copy).then_inc(hid_hi_ok, 1)

        def exponentials(n, which, i):
            for c in range(KD):
                wait(act, proj_ps, n * 5 * KD + (3 * KD if which else KD) + c + 1)
                act.activation(e_sb[:, c, :], proj[:, c, :], ACT.Exp, scale=SCALE0,
                               bias=bias[:, i, c:c + 1]).then_inc(exp_ok, 1)

        twice_normalised(0)
        transposed(0)

        def body(n, u, last):
            silu_of(n, 0)
            for c in range(KD):
                wait(act, proj_ps, n * 5 * KD + c + 1)
                act.activation(q_sb[:, c, :], proj[:, c, :], ACT.Identity, bias=bias[:, WQ, c:c + 1]).then_inc(q_ok, 1)
            if not last:
                twice_normalised(n + 1)
            hidden_high(n, 0)
            silu_of(n, 1)
            hidden_high(n, 1)
            exponentials(n, 0, WQA)
            silu_of(n, 2)
            hidden_high(n, 2)
            silu_of(n, 3)
            silu_of(n, 4)
            hidden_high(n, 3)
            for c in range(KD):
                wait(act, mixed_ok, n * KD + c + 1)
                act.activation(c_hi[:, c, :], mixed[:, c, :], ACT.Copy).then_inc(chi_ok, 1)
            hidden_high(n, 4)
            exponentials(n, 1, WKA)
            silu_of(n, 5)
            hidden_high(n, 5)
            if not last:
                transposed(n + 1)

        steps(act, body)

    @block.gpsimd
    def _(pool):
        def hidden_low(n, c):
            wait(pool, hid_hi_ok, n * C0 + c + 1)
            f = slice(0, F0C[c])
            pool.tensor_tensor(hid_lo[f, c % 2, :], hid[f, c % 2, :], hid_hi[f, c % 2, :],
                               ALU.subtract).then_inc(hid_lo_ok, 1)

        def body(n, u, last):
            hidden_low(n, 0)
            hidden_low(n, 1)
            for c in range(KD):
                wait(pool, exp_ok, n * 2 * KD + c + 1)
                pool.tensor_tensor(q_sb[:, c, :], q_sb[:, c, :], e_sb[:, c, :], ALU.mult).then_inc(times_ok, 1)
            hidden_low(n, 2)
            hidden_low(n, 3)
            hidden_low(n, 4)
            for c in range(KD):
                wait(pool, exp_ok, n * 2 * KD + KD + c + 1)
                pool.tensor_tensor(q_sb[:, c, :], mixed[:, c, :], e_sb[:, c, :], ALU.mult).then_inc(times_ok, 1)
            hidden_low(n, 5)

        steps(pool, body)

    @block.vector
    def _(dve):
        def once_normalised(m):
            wait(dve, xt_ps, m * 4)
            for j in range(TT):
                t = bass.ds(m * TT + j, 1)
                dve.tensor_scalar(x_tok[:, j, :], x_sb[:, t, :], rstd[:, t], shift[:, t], ALU.mult,
                                  ALU.add).then_inc(xtok, 1)

        def add_to_x(m):
            for h in range(TT // 2):
                wait(dve, acc_ps, m * 2 + h + 1)
                t = bass.ds(m * TT + 2 * h, 2)
                dve.tensor_tensor(x_sb[:, t, :], x_sb[:, t, :], acc[:, 2 * h:2 * h + 2, :], ALU.add).then_inc(x1_ok, 1)

        def statistics(m):
            for j in range(TT):
                t = bass.ds(m * TT + j, 1)
                dve.bn_stats(stats[:, t, :], x_sb[:, t, :]).then_inc(rows_ok, 1)

        def transposed_low(m):
            for t in range(2 * KD):
                wait(dve, xt_hi_ok, m * 4 + t + 1)
                dve.tensor_tensor(xt_lo[:, t, :], ring[:, t, :], xt_hi[:, t, :], ALU.subtract).then_inc(xt_lo_ok, 1)

        def hidden(n, c):
            wait(dve, silu_ok, n * C0 + c + 1)
            wait(dve, gu_ps, n * 2 * C0 + 2 * c + 2)
            if c >= 2:
                wait(dve, hid_lo_ok, n * C0 + c - 1)
            f = slice(0, F0C[c])
            dve.tensor_tensor(hid[f, c % 2, :], silu[f, c % 2, :], ring[f, 2 * (c % 2) + 1, :],
                              ALU.mult).then_inc(hid_ok, 1)

        def running_sum(sem_out, dst, src, waits, u):
            for c in range(KD):
                for s, v in waits:
                    wait(dve, s, v + c + 1)
                carry = dst[:, c, BLK - 1:BLK] if u else 0.0
                dve.tensor_tensor_scan(dst[:, c, :], ones[:], src[:, c, :], carry, ALU.mult, ALU.add).then_inc(sem_out, 1)

        def reciprocal(n, which, c):
            k = 2 * KD * n + KD * which + c
            wait(dve, sum_ok, k + 1)
            src = sum2 if which else sum_sb
            dve.reciprocal(rc_sb[:, c, :], src[:, c, :]).then_inc(recip_ok, 1)

        def weighted(n, which):
            for c in range(KD):
                k = 2 * KD * n + KD * which + c
                wait(dve, recip_ok, k + 1)
                wait(dve, times_ok, k + 1)
                dve.tensor_tensor(rc_sb[:, c, :], rc_sb[:, c, :], q_sb[:, c, :], ALU.mult).then_inc(weight_ok, 1)

        once_normalised(0)
        transposed_low(0)

        def body(n, u, last):
            hidden(n, 0)
            for c in range(KD):
                wait(dve, q_ok, n * KD + c + 1)
                dve.tensor_copy(c_hi[:, c, :], q_sb[:, c, :]).then_inc(chi_ok, 1)
            for c in range(KD):
                wait(dve, chi_ok, n * 2 * KD + c + 1)
                dve.tensor_tensor(c_lo[:, c, :], q_sb[:, c, :], c_hi[:, c, :], ALU.subtract).then_inc(clo_ok, 1)
            if not last:
                once_normalised(n + 1)
            if not (isinstance(n, int) and n == 0):
                add_to_x(n - 1)
            wait(dve, x1_ok, n * 2)
            hidden(n, 1)
            if not (isinstance(n, int) and n == 0):
                statistics(n - 1)
            running_sum(sum_ok, sum_sb, e_sb, [(exp_ok, n * 2 * KD)], u)
            reciprocal(n, 0, 0)
            hidden(n, 2)
            reciprocal(n, 0, 1)
            weighted(n, 0)
            hidden(n, 3)
            running_sum(pooled_ok, pool1, rc_sb, [(weight_ok, n * 2 * KD)], u)
            for c in range(KD):
                wait(dve, proj_ps, n * 5 * KD + 2 * KD + c + 1)
                wait(dve, pooled_ok, n * 2 * KD + c + 1)
                dve.scalar_tensor_tensor(mixed[:, c, :], proj[:, c, :], bias[:, WK, c:c + 1], pool1[:, c, :],
                                         ALU.add, ALU.mult).then_inc(mixed_ok, 1)
            for c in range(KD):
                wait(dve, chi_ok, n * 2 * KD + KD + c + 1)
                dve.tensor_tensor(c_lo[:, c, :], mixed[:, c, :], c_hi[:, c, :], ALU.subtract).then_inc(clo_ok, 1)
            hidden(n, 4)
            running_sum(sum_ok, sum2, e_sb, [(exp_ok, n * 2 * KD + KD)], u)
            reciprocal(n, 1, 0)
            hidden(n, 5)
            reciprocal(n, 1, 1)
            if not last:
                transposed_low(n + 1)
            weighted(n, 1)
            running_sum(pooled_ok, pool2, rc_sb, [(weight_ok, n * 2 * KD + KD)], u)
            for c in range(KD):
                wait(dve, proj_ps, n * 5 * KD + 4 * KD + c + 1)
                wait(dve, pooled_ok, n * 2 * KD + KD + c + 1)
                dve.scalar_tensor_tensor(mixed[:, c, :], proj[:, c, :], bias[:, WV, c:c + 1], pool2[:, c, :],
                                         ALU.add, ALU.mult).then_inc(attn_ok, 1)
        steps(dve, body)
        add_to_x(NB - 1)
        wait(dve, x1_ok, NB * 2)
        statistics(NB - 1)
        wait(dve, rows_ok, NT)


def run_layer1_ffn(nc, a, ahead, sem, x_sb, ident, mean, var, rstd, shift, stat_raw, eps_col, scratch, raw, raw_in):
    with ExitStack() as scope:
        def sb(name, shape, dt, ctx=scope):
            return ctx.enter_context(nc.sbuf_tensor(name, shape, dt))

        gu_hi, gu_lo = (sb(n, [P, 2, KD, F1], F32R) for n in ("gu_hi", "gu_lo"))
        dn_hi, dn_lo = (sb(n, [P, C1, D], F32R) for n in ("dn_hi", "dn_lo"))
        qkv_hi, qkv_lo = (sb(n, [P, KD, 3 * D], F32R) for n in ("qkv_hi", "qkv_lo"))
        rt_hi, rt_lo = (sb(n, [P, KD, NX], F32R) for n in ("rt_hi", "rt_lo"))
        expert_of = sb("expert_of", [3 * LANE, CX * P], BF16)
        before8 = sb("before8", [P, TT, NX, NX], BF16)
        before4 = sb("before4", [P, TT, NX // 2, NX // 2], BF16)
        w_parts = sb("w_parts", [P, TT, 3 * LANE], BF16)
        bv_row, bo_row = sb("bv_row", [P, D], F32), sb("bo_row", [P, D], F32)
        qk_bias = sb("qk_bias", [P, 3 * KD], F32)

        with ahead:
            load_layer1(nc, a, ahead, sem, mean, var, rstd, shift, stat_raw, eps_col, gu_hi, gu_lo, dn_hi, dn_lo,
                        qkv_hi, qkv_lo, rt_hi, rt_lo, expert_of, before8, before4, w_parts, bv_row, bo_row, qk_bias,
                        raw, raw_in)
        layer1_steps(nc, scope, sem, x_sb, ident, rstd, shift, scratch, gu_hi, gu_lo, dn_hi, dn_lo, qkv_hi,
                     qkv_lo, rt_hi, rt_lo, expert_of, before8, before4, w_parts, bv_row, bo_row, qk_bias)


def load_layer1(nc, a, ctx, sem, mean, var, rstd, shift, stat_raw, eps_col, gu_hi, gu_lo, dn_hi, dn_lo, qkv_hi,
                qkv_lo, rt_hi, rt_lo, expert_of, before8, before4, w_parts, bv_row, bo_row, qk_bias, raw, raw_in):
    def st(name, shape, dt=F32):
        return ctx.enter_context(nc.sbuf_tensor(name, shape, dt, side="right"))

    gu, qkv, rt = raw["gu_raw"], raw["qkv_raw"], raw["rt_raw"]
    gu_loaded, qkv_loaded = raw_in["gu"], raw_in["qkv"]
    dn, small = st("dn_raw", [P, C1, D]), st("small1", [P, NT])
    names = "l1_dn_loaded l1_rows_loaded l1_hi l1_lo_dve l1_lo_pool l1_masks l1_root l1_rstd"
    dn_loaded, rows_loaded, hi_ok, lo_dve, lo_pool, masks, root, rstd_ok = (sem(n) for n in names.split())
    dn_zero = sem("l1_dn_zero")
    stats_of, stats_kept = layer_norm_stats(sem, mean, var, stat_raw, "ln1")
    block = ctx.enter_context(nc.Block())

    @block.sync
    def _(sp):
        sp.dma_start(bv_row[:], a["b_qkv_row"][2 * D:3 * D].rearrange("(o n) -> o n", o=1)
                      .broadcast_to([P, D])).then_inc(rows_loaded, 16)
        sp.dma_start(bo_row[:], a["b_o"].rearrange("(o n) -> o n", o=1).broadcast_to([P, D])).then_inc(rows_loaded, 16)
        sp.dma_start(qk_bias[:], a["b_qkv"]).then_inc(rows_loaded, 16)
        sp.dma_start(dn[:, 0:CX, :], a["down_w"].rearrange("n f d -> (n f) d").rearrange("(c p) d -> p c d", p=P)
                      ).then_inc(dn_loaded, 16)
        wait(sp, dn_zero, 1)
        for c in range(CX, C1):
            f = sum(F1C[CX:c])
            sp.dma_start(dn[0:F1C[c], c, :], a["sh_down"][f:f + F1C[c], :]).then_inc(dn_loaded, 16)

    @block.scalar
    def _(act):
        wait(act, qkv_loaded, 32)
        act.activation(qkv_hi[:], qkv[:], ACT.Copy).then_inc(hi_ok, 1)
        act.activation(rt_hi[:], rt[:], ACT.Copy).then_inc(hi_ok, 1)
        wait(act, gu_loaded, 8 * 16)
        for w in range(2):
            for k in range(KD):
                act.activation(gu_hi[:, w, k, :], gu[:, w, k, :], ACT.Copy).then_inc(hi_ok, 1)
        wait(act, dn_loaded, (1 + C1 - CX) * 16)
        for h in range(2):
            c = slice(h * C1 // 2, (h + 1) * C1 // 2)
            act.activation(dn_hi[:, c, :], dn[:, c, :], ACT.Copy).then_inc(hi_ok, 1)
        wait(act, *stats_kept)
        act.activation(small[:], var[:], ACT.Sqrt, bias=eps_col[:]).then_inc(root, 1)
        wait(act, rows_loaded, 48)

    @block.gpsimd
    def _(pool):
        pool.memset(dn[:, CX:C1, :], 0.0).then_inc(dn_zero, 1)
        pool.memset(expert_of[:], 1.0).then_inc(masks, 1)
        pool.memset(before8[:], 1.0).then_inc(masks, 1)
        pool.memset(before4[:], 1.0).then_inc(masks, 1)
        pool.memset(w_parts[:], 0.0).then_inc(masks, 1)
        wait(pool, masks, 4)
        for t, n in ((before8, NX), (before4, NX // 2)):
            pool.affine_select(out=t[:], in_=t[:], compare_op=ALU.is_gt, fill=0.0, base=0,
                               pattern=[[0, TT], [1, n], [-1, n]], channel_multiplier=0).then_inc(masks, 1)
        for r in range(PART):
            rows = expert_of[r * LANE:(r + 1) * LANE, :]
            pool.affine_select(out=rows, in_=rows, compare_op=ALU.is_ge, fill=0.0, base=0,
                               pattern=[[1, CX * P]], channel_multiplier=-FX).then_inc(masks, 1)
            wait(pool, masks, 7 + 2 * r)
            pool.affine_select(out=rows, in_=rows, compare_op=ALU.is_ge, fill=0.0, base=FX - 1,
                               pattern=[[-1, CX * P]], channel_multiplier=FX).then_inc(masks, 1)
        wait(pool, masks, 12)
        wait(pool, hi_ok, 6)
        pool.tensor_tensor(gu_lo[:, 1, 1, :], gu[:, 1, 1, :], gu_hi[:, 1, 1, :], ALU.subtract).then_inc(lo_pool, 1)
        wait(pool, lo_pool, 1)

    @block.vector
    def _(dve):
        stats_of(dve)
        wait(dve, hi_ok, 1)
        dve.tensor_tensor(qkv_lo[:], qkv[:], qkv_hi[:], ALU.subtract).then_inc(lo_dve, 1)
        wait(dve, hi_ok, 2)
        dve.tensor_tensor(rt_lo[:], rt[:], rt_hi[:], ALU.subtract).then_inc(lo_dve, 1)
        for i, (w, k) in enumerate(((0, 0), (0, 1), (1, 0))):
            wait(dve, hi_ok, 3 + i)
            dve.tensor_tensor(gu_lo[:, w, k, :], gu[:, w, k, :], gu_hi[:, w, k, :], ALU.subtract).then_inc(lo_dve, 1)
        for h in range(2):
            c = slice(h * C1 // 2, (h + 1) * C1 // 2)
            wait(dve, hi_ok, 7 + h)
            dve.tensor_tensor(dn_lo[:, c, :], dn[:, c, :], dn_hi[:, c, :], ALU.subtract).then_inc(lo_dve, 1)
        wait(dve, root, 1)
        dve.reciprocal(rstd[:], small[:]).then_inc(rstd_ok, 1)
        wait(dve, rstd_ok, 1)
        dve.scalar_tensor_tensor(shift[:], mean[:], -1.0, rstd[:], ALU.mult, ALU.mult).then_inc(rstd_ok, 1)
        wait(dve, lo_dve, 7)
        wait(dve, rstd_ok, 2)


ORDER1 = list(range(CX, C1)) + list(range(CX))


def layer1_steps(nc, scope, sem, x_sb, ident, rstd, shift, scratch, gu_hi, gu_lo, dn_hi, dn_lo, qkv_hi, qkv_lo,
                 rt_hi, rt_lo, expert_of, before8, before4, w_parts, bv_row, bo_row, qk_bias):
    def sb(name, shape, dt=F32):
        return scope.enter_context(nc.sbuf_tensor(name, shape, dt, side="right"))

    x_tok = sb("x_tok1", [P, TT, D])
    xt_hi, xt_lo = sb("xt_hi1", [P, 2, KD, BLK], F32R), sb("xt_lo1", [P, 2, KD, BLK], F32R)
    parts = sb("parts", [P, 2 * KD, PART, BLK], BF16)
    rest = sb("rest", [P, 2 * KD, BLK])
    v_sb = sb("v_sb", [P, TT, H, VW])
    hid = sb("hid1", [P, 2, BLK])
    hid_hi, hid_lo = sb("hid_hi1", [P, 2, BLK], F32R), sb("hid_lo1", [P, 2, BLK], F32R)
    w_turned = sb("w_turned", [3 * LANE, BLK], BF16)
    ident_bf = sb("ident_bf", [P, P], BF16)
    top, total = sb("top", [P, TT]), sb("total", [P, TT])
    logit, score, kept = sb("logit", [P, TT, NX]), sb("score", [P, TT, NX]), sb("kept_score", [P, TT, NX])
    group, g_rank = sb("group", [P, TT, NX // 2]), sb("g_rank", [P, TT, NX // 2])
    rank, w_rest = sb("rank", [P, TT, NX]), sb("w_rest", [P, TT, NX])
    above, equal = sb("above", [P, TT, NX, NX], BF16), sb("equal", [P, TT, NX, NX], BF16)
    ps = scope.enter_context(nc.psum_tensor("ps1", [P, 8, 512], F32))
    ring, spread, misc = ps[:, 0:4, :], ps[:, 4, :], ps[:, 5, :]
    acc = ps[:, 6:8, :].rearrange("p h (j d) -> p (h j) d", d=D)
    logits = misc[:, 0:TT * NX].rearrange("p (t e) -> p t e", t=TT)
    turned = misc[0:3 * LANE, 128:128 + BLK // 2].bitcast(BF16)

    names = ("l1_xtok l1_xt_ps l1_xt_hi l1_xt_lo l1_logits l1_route l1_exp l1_w_ready l1_turned_ps l1_w_turned l1_qk_ps l1_part1 "
             "l1_rest l1_part2 l1_part3 l1_v_ps l1_v l1_gu_ps l1_silu l1_prod l1_spread_ps l1_weighted "
             "l1_hid_hi l1_hid_lo l1_down l1_x2 l1_out l1_ones l1_ident_bf").split()
    (xtok, xt_ps, xt_hi_ok, xt_lo_ok, logits_ok, route, exp_ok, w_ready, turned_ps, w_turned_ok, qk_ps, part1, rest_ok, part2,
     part3, v_ps, v_ok, gu_ps, silu_ok, prod_ok, spread_ps, weighted_ok, hid_hi_ok, hid_lo_ok, down_ok,
     x2_ok, out_ok, ones_ok, ident_bf_ok) = (sem(n) for n in names)
    v_out = sem("l1_v_out")
    NQK = 2 * KD
    parts_out = [sem(f"l1_parts_out{c}") for c in range(NQK)]
    TURN_AT = (6, 9)
    block = scope.enter_context(nc.Block())

    def steps(eng, body):
        body(0, 0, False)
        with eng.Fori(0, NB // 2 - 1) as m:
            body(2 * m + 1, 1, False)
            body(2 * m + 2, 0, False)
        body(NB - 1, (NB - 1) % 2, True)

    def banks(i):
        return 2 * ((i + 1) % 2)

    def finished(n, i):
        if i < C1 - CX:
            return prod_ok, n * C1 + i + 1
        return weighted_ok, n * CX + i - (C1 - CX) + 1

    @block.tensor
    def _(pe):
        def transposes(m, k):
            if k == 0:
                wait(pe, xtok, m * TT + TT)
                wait(pe, w_turned_ok, m)
            else:
                wait(pe, xt_hi_ok, m * KD + k)
                wait(pe, xt_lo_ok, m * KD + k)
            for j in range(TT):
                ins = pe.transpose(misc[:, j * P:(j + 1) * P], x_tok[:, j, k * P:(k + 1) * P], ident[:])
            ins.then_inc(xt_ps, 1)

        def router(m, par):
            wait(pe, xt_hi_ok, m * KD + KD)
            wait(pe, xt_lo_ok, m * KD + KD)
            for j in range(TT):
                t = slice(j * P, (j + 1) * P)
                for k in range(KD):
                    pe.matmul(logits[:, j, :], xt_hi[:, par, k, t], rt_hi[:, k, :], start=(j == 0 and k == 0),
                              stop=False, skip_group_check=True)
                    pe.matmul(logits[:, j, :], xt_lo[:, par, k, t], rt_hi[:, k, :], start=False, stop=False,
                              skip_group_check=True)
                    ins = pe.matmul(logits[:, j, :], xt_hi[:, par, k, t], rt_lo[:, k, :], start=False,
                                    stop=(k == KD - 1), skip_group_check=True)
            ins.then_inc(logits_ok, 1)

        def gate_and_up(n, par, i):
            c, r = ORDER1[i], banks(i)
            f = slice(sum(F1C[:c]), sum(F1C[:c + 1]))
            if i == 0:
                wait(pe, rest_ok, n * NQK + NQK)
            elif i == 1:
                wait(pe, v_ok, n * 2 + 2)
            else:
                wait(pe, silu_ok, n * C1 + i - 1)
                wait(pe, prod_ok, n * C1 + i - 1)
            for w in range(2):
                for k in range(KD):
                    ins = split3(pe, ring[0:F1C[c], r + w, :], gu_hi[:, w, k, f], gu_lo[:, w, k, f],
                                 xt_hi[:, par, k, :], xt_lo[:, par, k, :], k == 0, k == KD - 1)
                ins.then_inc(gu_ps, 1)

        def spread_weights(n, c):
            wait(pe, w_turned_ok, n + 1)
            wait(pe, weighted_ok, n * CX + c)
            pe.matmul(spread[:, :], expert_of[:, c * P:(c + 1) * P], w_turned[:], start=True,
                      stop=True).then_inc(spread_ps, 1)

        def down_chunk(n, i):
            c = ORDER1[i]
            wait(pe, hid_hi_ok, n * C1 + i + 1)
            wait(pe, hid_lo_ok, n * C1 + i + 1)
            if i == 0:
                wait(pe, x2_ok, n * 2)
            f = slice(0, F1C[c])
            for j in range(TT):
                t = slice(j * P, (j + 1) * P)
                pe.matmul(acc[:, j, :], hid_hi[f, i % 2, t], dn_hi[f, c, :], start=(i == 0 and j % 2 == 0), stop=False,
                          skip_group_check=True)
                pe.matmul(acc[:, j, :], hid_lo[f, i % 2, t], dn_hi[f, c, :], start=False, stop=False,
                          skip_group_check=True)
                ins = pe.matmul(acc[:, j, :], hid_hi[f, i % 2, t], dn_lo[f, c, :], start=False, stop=(i == C1 - 1),
                                skip_group_check=True)
            ins.then_inc(down_ok, 1)

        wait(pe, ident_bf_ok, 1)
        for k in range(KD):
            transposes(0, k)
        router(0, 0)

        def body(n, par, last):
            wait(pe, silu_ok, n * C1)
            wait(pe, prod_ok, n * C1)
            for c in range(NQK):
                o = slice(c * P, (c + 1) * P)
                for k in range(KD):
                    ins = split3(pe, ring[:, c, :], qkv_hi[:, k, o], qkv_lo[:, k, o], xt_hi[:, par, k, :],
                                 xt_lo[:, par, k, :], k == 0, k == KD - 1)
                ins.then_inc(qk_ps, 1)
            for h in range(2):
                wait(pe, rest_ok, n * NQK + h + 1)
                o = slice(2 * D, 3 * D)
                for jj in range(2):
                    j = 2 * h + jj
                    t, dst = slice(j * P, (j + 1) * P), ring[:, h, jj * D:(jj + 1) * D]
                    for k in range(KD):
                        pe.matmul(dst, xt_hi[:, par, k, t], qkv_hi[:, k, o], start=(jj == 0 and k == 0), stop=False,
                                  skip_group_check=True)
                        pe.matmul(dst, xt_lo[:, par, k, t], qkv_hi[:, k, o], start=False, stop=False,
                                  skip_group_check=True)
                        ins = pe.matmul(dst, xt_hi[:, par, k, t], qkv_lo[:, k, o], start=False, stop=(k == KD - 1),
                                        skip_group_check=True)
                ins.then_inc(v_ps, 1)
            for i in range(C1):
                gate_and_up(n, par, i)
                if i == C1 - CX:
                    wait(pe, w_ready, n + 1)
                    for j in range(TT):
                        ins = pe.transpose(turned[:, j * P:(j + 1) * P], w_parts[:, j, :], ident_bf[:])
                    ins.then_inc(turned_ps, 1)
                if i >= 2:
                    down_chunk(n, i - 2)
                if ORDER1[i] < CX:
                    spread_weights(n, ORDER1[i])
                if i in TURN_AT and not last:
                    transposes(n + 1, TURN_AT.index(i))
            down_chunk(n, C1 - 2)
            if not last:
                router(n + 1, 1 - par)
            down_chunk(n, C1 - 1)

        steps(pe, body)

    @block.scalar
    def _(act):
        def transposed(m, par, k):
            wait(act, xt_ps, m * KD + k + 1)
            act.activation(xt_hi[:, par, k, :], misc, ACT.Copy).then_inc(xt_hi_ok, 1)

        def first_part(n, c):
            wait(act, qk_ps, n * NQK + c + 1)
            wait(act, parts_out[c], n * 16)
            act.activation(parts[:, c, 0, :], ring[:, c, :], ACT.Identity, bias=qk_bias[:, c:c + 1]).then_inc(part1, 1)

        def second_part(n, c):
            wait(act, rest_ok, n * NQK + c + 1)
            act.activation(parts[:, c, 1, :], rest[:, c, :], ACT.Copy).then_inc(part2, 1)

        def silu_of(n, i):
            wait(act, gu_ps, n * 2 * C1 + 2 * i + 1)
            if i >= 2:
                wait(act, hid_hi_ok, n * C1 + i - 1)
                wait(act, hid_lo_ok, n * C1 + i - 1)
            else:
                wait(act, hid_hi_ok, n * C1)
                wait(act, hid_lo_ok, n * C1)
            f = slice(0, F1C[ORDER1[i]])
            act.activation(hid[f, i % 2, :], ring[f, banks(i), :], ACT.Silu).then_inc(silu_ok, 1)

        def hidden_high(n, i):
            wait(act, *finished(n, i))
            if i >= 2:
                wait(act, down_ok, n * C1 + i - 1)
            else:
                wait(act, down_ok, n * C1)
            f = slice(0, F1C[ORDER1[i]])
            act.activation(hid_hi[f, i % 2, :], hid[f, i % 2, :], ACT.Copy).then_inc(hid_hi_ok, 1)

        for k in range(KD):
            transposed(0, 0, k)

        def body(n, par, last):
            first_part(n, 0)
            first_part(n, 1)
            for c in range(2, NQK):
                second_part(n, c - 2)
                first_part(n, c)
            second_part(n, NQK - 2)
            second_part(n, NQK - 1)
            wait(act, route, n + 1)
            act.activation(score[:], logit[:], ACT.Exp).then_inc(exp_ok, 1)
            silu_of(n, 0)
            for i in range(1, C1):
                silu_of(n, i)
                hidden_high(n, i - 1)
                if i - 1 in TURN_AT and not last:
                    transposed(n + 1, 1 - par, TURN_AT.index(i - 1))
            hidden_high(n, C1 - 1)

        steps(act, body)

    @block.gpsimd
    def _(pool):
        pool.memset(v_sb[:], 0.0).then_inc(ones_ok, 1)
        wait(pool, ones_ok, 1)
        pool.memset(v_sb[:, :, :, HD:HD + 1], 1.0).then_inc(ones_ok, 1)
        wait(pool, ones_ok, 2)

        def hidden_low(n, i):
            wait(pool, hid_hi_ok, n * C1 + i + 1)
            f = slice(0, F1C[ORDER1[i]])
            pool.tensor_tensor(hid_lo[f, i % 2, :], hid[f, i % 2, :], hid_hi[f, i % 2, :],
                               ALU.subtract).then_inc(hid_lo_ok, 1)

        def body(n, par, last):
            for c in range(NQK):
                wait(pool, part2, n * NQK + c + 1)
                pool.tensor_tensor(parts[:, c, 2, :], rest[:, c, :], parts[:, c, 1, :],
                                   ALU.subtract).then_inc(part3, 1)
            for i in range(C1):
                hidden_low(n, i)
            for h in range(TT // 2):
                wait(pool, x2_ok, n * 2 + h + 1)
                t = bass.ds(n * TT + 2 * h, 2)
                pool.tensor_tensor(x_sb[:, t, :], x_sb[:, t, :],
                                   bo_row[:].rearrange("p (o d) -> p o d", o=1).broadcast_to([P, 2, D]),
                                   ALU.add).then_inc(out_ok, 1)

        steps(pool, body)
        wait(pool, out_ok, 2 * NB)

    @block.sync
    def _(sp):
        def store(b, u, base):
            for c in range(NQK):
                wait(sp, part3, base * NQK + c + 1)
                dram = scratch["q_parts" if c < KD else "k_parts"]
                rows = slice((c % KD) * P, (c % KD + 1) * P)
                dst = dram[bass.ds(b, 1), :, rows, u * BLK:(u + 1) * BLK]
                sp.dma_start(dst.rearrange("b r p t -> p (b r) t"), parts[:, c, :, :]).then_inc(parts_out[c], 16)
            wait(sp, v_ok, base * 2 + 2)
            sp.dma_start(scratch["v"][bass.ds(base * TT, TT), :, :].rearrange("n p f -> p n f"),
                         v_sb[:].rearrange("p n h w -> p n (h w)")).then_inc(v_out, 16)

        with sp.Fori(0, B) as b:
            for u in range(S // BLK):
                store(b, u, b * (S // BLK) + u)
        wait(sp, v_out, NB * 16)
        for p in parts_out:
            wait(sp, p, NB * 16)

    @block.vector
    def _(dve):
        dve.tensor_copy(ident_bf[:], ident[:]).then_inc(ident_bf_ok, 1)

        def normalised(m):
            wait(dve, xt_ps, m * KD)
            for j in range(TT):
                t = bass.ds(m * TT + j, 1)
                dve.tensor_scalar(x_tok[:, j, :], x_sb[:, t, :], rstd[:, t], shift[:, t], ALU.mult,
                                  ALU.add).then_inc(xtok, 1)

        def transposed_low(m, par, k):
            wait(dve, xt_hi_ok, m * KD + k + 1)
            dve.tensor_tensor(xt_lo[:, par, k, :], misc, xt_hi[:, par, k, :], ALU.subtract).then_inc(xt_lo_ok, 1)

        def product(n, i):
            wait(dve, silu_ok, n * C1 + i + 1)
            wait(dve, gu_ps, n * 2 * C1 + 2 * i + 2)
            f = slice(0, F1C[ORDER1[i]])
            dve.tensor_tensor(hid[f, i % 2, :], hid[f, i % 2, :], ring[f, banks(i) + 1, :],
                              ALU.mult).then_inc(prod_ok, 1)

        def weigh(n, i):
            wait(dve, prod_ok, n * C1 + i + 1)
            wait(dve, spread_ps, n * CX + ORDER1[i] + 1)
            dve.tensor_tensor(hid[:, i % 2, :], hid[:, i % 2, :], spread[:, :], ALU.mult).then_inc(weighted_ok, 1)

        def ranks(chain, out_rank, values, before, n, g):
            shape = [P, TT, g, g]
            other = values[:].rearrange("p t (a j) -> p t a j", a=1).broadcast_to(shape)
            own = values[:].rearrange("p t (i a) -> p t i a", a=1).broadcast_to(shape)
            ab, eq = above[:, :, 0:g, 0:g], equal[:, :, 0:g, 0:g]
            chain(dve.tensor_tensor(ab, other, own, ALU.is_gt), needed=False)
            chain(dve.tensor_tensor(eq, other, own, ALU.is_equal))
            chain(dve.tensor_tensor(eq, eq, before[:], ALU.mult))
            chain(dve.tensor_tensor(ab, ab, eq, ALU.add))
            chain(dve.tensor_reduce(out_rank[:], ab, AX.X, ALU.add))

        ROUTE_STEPS = 22
        chained = sem("l1_route_chain")

        done = [0]

        def chain_of(n):
            def chain(ins, needed=True):
                ins.then_inc(chained, 1)
                done[0] += 1
                if needed:
                    wait(dve, chained, n * ROUTE_STEPS + done[0])
            return chain

        def wide(t):
            return t[:].rearrange("p (t a) -> p t a", a=1).broadcast_to([P, TT, NX])

        def route_groups(n):
            chain = chain_of(n)
            wait(dve, exp_ok, n + 1)
            chain(dve.tensor_reduce(total[:], score[:], AX.X, ALU.add))
            chain(dve.reciprocal(total[:], total[:]))
            chain(dve.tensor_tensor(score[:], score[:], wide(total), ALU.mult))
            pairs = score[:].rearrange("p t (g e) -> p t g e", e=2)
            chain(dve.tensor_tensor(group[:], pairs[:, :, :, 0], pairs[:, :, :, 1], ALU.max))
            ranks(chain, g_rank, group, before4, n, NX // 2)

        def route_experts(n):
            chain = chain_of(n)
            chain(dve.tensor_scalar(g_rank[:], g_rank[:], 2.0, None, ALU.is_lt))
            chain(dve.tensor_tensor(kept[:].rearrange("p t (g e) -> p t g e", e=2),
                                    score[:].rearrange("p t (g e) -> p t g e", e=2),
                                    g_rank[:].rearrange("p t (g a) -> p t g a", a=1).broadcast_to([P, TT, NX // 2, 2]),
                                    ALU.mult))
            ranks(chain, rank, kept, before8, n, NX)

        def route_weights(n):
            chain = chain_of(n)
            chain(dve.scalar_tensor_tensor(w_rest[:], rank[:], 2.0, kept[:], ALU.is_lt, ALU.mult))
            wait(dve, turned_ps, n)
            for r in range(PART):
                part = w_parts[:, :, r * LANE:r * LANE + NX]
                if r < PART - 1:
                    chain(dve.tensor_copy(part, w_rest[:]))
                    chain(dve.tensor_tensor(w_rest[:], w_rest[:], part, ALU.subtract))
                else:
                    dve.tensor_copy(part, w_rest[:]).then_inc(w_ready, 1)
            assert done[0] == ROUTE_STEPS, done[0]

        normalised(0)
        for k in range(KD):
            transposed_low(0, 0, k)

        def body(n, par, last):
            done[0] = 1
            wait(dve, logits_ok, n + 1)
            dve.tensor_reduce(top[:], logits, AX.X, ALU.max).then_inc(chained, 1)
            wait(dve, chained, n * ROUTE_STEPS + 1)
            dve.tensor_tensor(logit[:], logits, top[:].rearrange("p (t a) -> p t a", a=1).broadcast_to([P, TT, NX]),
                              ALU.subtract).then_inc(route, 1)
            for c in range(NQK):
                wait(dve, part1, n * NQK + c + 1)
                wait(dve, part3, (n - 1) * NQK + c + 1)
                dve.scalar_tensor_tensor(rest[:, c, :], ring[:, c, :], qk_bias[:, c:c + 1], parts[:, c, 0, :],
                                         ALU.add, ALU.subtract).then_inc(rest_ok, 1)
            for h in range(2):
                wait(dve, v_ps, n * 2 + h + 1)
                src = ring[:, h, :].rearrange("p (t h d) -> p t h d", t=2, h=H)
                if h == 0:
                    wait(dve, ones_ok, 2)
                    wait(dve, v_out, n * 16)
                dve.tensor_tensor(v_sb[:, 2 * h:2 * h + 2, :, 0:HD], src,
                                  bv_row[:].rearrange("p (o h d) -> p o h d", o=1, h=H).broadcast_to([P, 2, H, HD]),
                                  ALU.add).then_inc(v_ok, 1)
            route_groups(n)
            for i in range(C1):
                product(n, i)
                if i == 0:
                    route_experts(n)
                if i == 1:
                    route_weights(n)
                if i == C1 - CX:
                    wait(dve, turned_ps, n + 1)
                    wait(dve, spread_ps, n * CX)
                    dve.tensor_copy(w_turned[:], turned).then_inc(w_turned_ok, 1)
                if ORDER1[i] < CX:
                    weigh(n, i)
                if i == TURN_AT[0] - 2 and not last:
                    normalised(n + 1)
                if i in TURN_AT and not last:
                    transposed_low(n + 1, 1 - par, TURN_AT.index(i))
            for h in range(TT // 2):
                wait(dve, down_ok, n * C1 + C1)
                t = bass.ds(n * TT + 2 * h, 2)
                dve.tensor_tensor(x_sb[:, t, :], x_sb[:, t, :], acc[:, 2 * h:2 * h + 2, :], ALU.add).then_inc(x2_ok, 1)

        steps(dve, body)
        wait(dve, x2_ok, 2 * NB)


HG = 4
NHG = H // HG
NG = B * NHG
KT = S // P
HALF = S // 2
STEPS = 2 * KT
UNITS = HG * KT * 2
HU = UNITS // 2
HM = HU // 2
PER_STEP = UNITS // STEPS
LEAD = 3
ROWS = 6 * HD
SLOTS = ((0, 0), (1, 0), (2, 0), (0, 1), (1, 1), (0, 2))
TASKS = {hg: [(0, "turn", 1), (KT - LEAD, "maxima", 1), (8, "turn", 0), (STEPS - LEAD, "maxima", 0)]
         for hg in range(NHG)}
TASKS[0] += [(1, "features", (1, 0)), (2, "features", (1, 1)), (3, "project", (1, 0)), (4, "project", (1, 1))]
TASKS[NHG - 1] += [(9, "features", (0, 0)), (10, "features", (0, 1)), (11, "project", (0, 0)), (12, "project", (0, 1))]
for tasks in TASKS.values():
    tasks.sort()
CARRIED = 5
PER_BATCH = sum(len(t) for t in TASKS.values())


def task_number(b, hg, task, arg):
    before = sum(len(TASKS[g]) for g in range(hg)) + [t[1:] for t in TASKS[hg]].index((task, arg))
    return b * PER_BATCH + before + 1 - CARRIED - (1 if isinstance(b, int) and b == B else 0)


def run_layer1_attention(nc, a, scope, sem, x_sb, ident, scratch, out):
    def sb(name, shape, dt=F32):
        return scope.enter_context(nc.sbuf_tensor(name, shape, dt))

    q_stack, k_stack = (sb(n, [P, NHG, HG, S], BF16) for n in ("q_stack", "k_stack"))
    v_cur = sb("v_cur", [P, NHG, KT, HG * VW])
    probs = sb("probs", [P, 2, HG, HALF])
    o_sb = sb("o_sb", [P, HALF])
    att = sb("att", [P, KT, D])
    at_hi, at_lo = sb("at_hi", [P, KD, HALF], F32R), sb("at_lo", [P, KD, HALF], F32R)
    wo, wo_hi, wo_lo = sb("wo", [P, KD, D]), sb("wo_hi", [P, KD, D], F32R), sb("wo_lo", [P, KD, D], F32R)
    inv = sb("inv", [P, 4, HG])
    half_max, neg_max, m_rest = sb("half_max", [P, 2, HU]), sb("neg_max", [P, HM]), sb("m_rest", [P, 2, HM])
    zeros, zeros_ok = sb("zeros", [P, HM]), sem("at_zeros")
    m_parts = sb("m_parts", [P, PART, HM], BF16)
    m_rows = sb("m_rows", [PART * HG, HALF], BF16)
    ident_b = sb("ident_b", [P, P], BF16)
    ps = scope.enter_context(nc.psum_tensor("ps2", [P, 8, 512], F32))
    scores = ps[:, 0:4, :].rearrange("p (u j) n -> p u j n", u=2)
    maxima, o_ps, spare = ps[:, 4:6, :], ps[:, 6, :], ps[:, 7, :]
    m_turned = spare[0:PART * HG, 0:HALF // 2].bitcast(BF16)

    qk_in = [sem(f"at_qk_in{i}") for i in range(NHG)]
    v_in = [sem(f"at_v_in{i}") for i in range(NHG)]
    names = ("at_wo_in at_wo_hi at_wo_lo at_ones at_ident at_scores_ps at_exp at_pv at_max_ps at_reduced at_min at_o_out "
             "at_spare_ps at_spare_done at_split at_m_in at_inv at_high at_out").split()
    (wo_in, wo_hi_ok, wo_lo_ok, ones_ok, ident_ok, scores_ps, exp_ok, pv_ok, max_ps, reduced, min_ok, o_out, spare_ps,
     spare_done, split_ok, m_in, inv_ok, high_ok, out_done) = (sem(n) for n in names)
    TAIL = [(task, arg) for _, task, arg in TASKS[0][:CARRIED]]
    block = scope.enter_context(nc.Block())

    def batches(eng, body):
        body(0, False)
        with eng.Fori(1, B - 1) as b:
            body(b, False)
        body(B - 1, True)

    def tasks_at(b, hg, s):
        for i, (at, task, arg) in enumerate(TASKS[hg]):
            carried = isinstance(b, int) and b == 0 and hg == 0 and i < CARRIED
            ended = isinstance(b, int) and b == B - 1 and hg == NHG - 1 and (task, arg) == ("maxima", 0)
            if at == s and not carried and not ended:
                yield task, arg

    def max_units(b, hg, s, last):
        ahead, u = divmod(PER_STEP * (s + LEAD + KT), UNITS)
        if last and hg + ahead >= NHG:
            return []
        return [(b * NHG + hg + ahead, (hg + ahead) % NHG, u + i) for i in range(PER_STEP)]

    def unit(u):
        return u % HU // KT, u // HU * (KT // 2) + u // 2 % (KT // 2), u % 2

    @block.sync
    def _(sp):
        def load_qk(b, hg):
            for i, parts in enumerate(SLOTS):
                for name, stack, part in zip(("q_parts", "k_parts"), (q_stack, k_stack), parts):
                    src = scratch[name][bass.ds(b, 1), part, hg * HG * HD:(hg + 1) * HG * HD, :]
                    sp.dma_start(stack[i * HD:(i + 1) * HD, hg, :, :],
                                 src.rearrange("b (h d) t -> d (b h) t", h=HG)).then_inc(qk_in[hg], 16)

        def load_v(b, hg):
            src = scratch["v"][bass.ds(b * KT, KT), :, hg * HG * VW:(hg + 1) * HG * VW]
            sp.dma_start(v_cur[:, hg, :, :], src.rearrange("n p f -> p n f")).then_inc(v_in[hg], 16)

        def turn_maxima(number, hg, half):
            sp.wait_ge(spare_done, number + 1)
            sp.dma_start(q_stack[ROWS:ROWS + PART, hg, :, half * HALF:(half + 1) * HALF], m_rows[:]).then_inc(m_in, 16)

        load_qk(0, 0)
        sp.dma_start(wo[:], a["w_o"].rearrange("(k p) o -> p k o", p=P)).then_inc(wo_in, 16)
        load_v(0, 0)
        load_qk(0, 1)
        turn_maxima(0, 0, 0)

        def store(b, hg, half, o):
            sp.wait_ge(spare_done, task_number(b, hg, "project", (half, o)) + 1)
            t = bass.ds(b * KT + (2 * o if half == 0 else 2 * o - 4), 2)
            sp.dma_start(out.rearrange("b (n p) d -> p (b n) d", p=P)[:, t, :], x_sb[:, t, :]).then_inc(out_done, 16)

        def body(b, last):
            for hg in range(NHG):
                g = b * NHG + hg
                if not (last and hg >= NHG - 2):
                    wait(sp, scores_ps, (g - 1) * STEPS * 2)
                    load_qk(b + (hg + 2) // NHG, (hg + 2) % NHG)
                if not (last and hg == NHG - 1):
                    wait(sp, pv_ok, (g - 2) * STEPS)
                    load_v(b + (hg + 1) // NHG, (hg + 1) % NHG)
                for s in range(STEPS):
                    for task, arg in tasks_at(b, hg, s):
                        if task == "project":
                            store(b, hg, *arg)
                        if task == "maxima":
                            turn_maxima(task_number(b, hg, task, arg), hg if arg else (hg + 1) % NHG, arg)

        batches(sp, body)
        for o in range(2):
            store(B, 0, 1, o)
        sp.wait_ge(out_done, 4 * B * 16)

    @block.gpsimd
    def _(pool):
        pool.memset(k_stack[ROWS:P, :, :, :], 1.0).then_inc(ones_ok, 1)
        pool.wait_ge(ones_ok, 1)
        pool.memset(zeros[:], 0.0).then_inc(zeros_ok, 1)
        pool.wait_ge(zeros_ok, 1)
        in_split = sem("at_in_split")

        def split_maxima(h):
            if not (isinstance(h, int) and h == 0):
                pool.wait_ge(scores_ps, (h - 1) * STEPS + 1)
            pool.wait_ge(min_ok, h + 1)
            pool.tensor_tensor(m_parts[:, 0, :], neg_max[:], zeros[:], ALU.add).then_inc(in_split, 1)
            pool.wait_ge(in_split, h * 4 + 1)
            pool.tensor_tensor(m_rest[:, 0, :], neg_max[:], m_parts[:, 0, :], ALU.subtract).then_inc(in_split, 1)
            pool.wait_ge(in_split, h * 4 + 2)
            pool.tensor_tensor(m_parts[:, 1, :], m_rest[:, 0, :], zeros[:], ALU.add).then_inc(in_split, 1)
            pool.wait_ge(in_split, h * 4 + 3)
            pool.tensor_tensor(m_rest[:, 1, :], m_rest[:, 0, :], m_parts[:, 1, :], ALU.subtract).then_inc(in_split, 1)
            pool.wait_ge(in_split, h * 4 + 4)
            pool.tensor_tensor(m_parts[:, 2, :], m_rest[:, 1, :], zeros[:], ALU.add).then_inc(split_ok, 1)

        def body(b, last):
            for hg in range(NHG):
                g = b * NHG + hg
                split_maxima(2 * g + 1)
                if not (last and hg == NHG - 1):
                    split_maxima(2 * g + 2)

        split_maxima(0)
        batches(pool, body)

    @block.tensor
    def _(pe):
        def score_block(b, hg, t, s, pair):
            if s == 0 and pair == 0:
                pe.wait_ge(qk_in[hg], (b + 1) * 2 * len(SLOTS) * 16)
            if s % KT == 0 and pair == 0:
                pe.wait_ge(m_in, ((b * NHG + hg) * 2 + s // KT + 1) * 16)
            wait(pe, exp_ok, 2 * t + pair - 1)
            half, kt = s // KT, s % KT
            for jj in range(2):
                j = 2 * pair + jj
                ins = pe.matmul(scores[:, pair, jj, :], k_stack[0:ROWS + PART, hg, j, kt * P:(kt + 1) * P],
                                q_stack[0:ROWS + PART, hg, j, half * HALF:(half + 1) * HALF], start=True, stop=True)
            ins.then_inc(scores_ps, 1)

        def max_block(g, hg, u):
            j, qt, kh = unit(u)
            wait(pe, reduced, g * UNITS + u - 1)
            pe.matmul(maxima[:, u % 2, :], q_stack[0:ROWS, hg, j, qt * P:(qt + 1) * P],
                      k_stack[0:ROWS, hg, j, kh * HALF:(kh + 1) * HALF], start=True, stop=True).then_inc(max_ps, 1)

        def weighted_values(b, hg, t, s):
            half, kt = s // KT, s % KT
            if s == 0:
                pe.wait_ge(v_in[hg], (b + 1) * 16)
            if kt == 0:
                wait(pe, o_out, (b * NHG + hg) * 2 + half)
            pe.wait_ge(exp_ok, 2 * t + 2)
            for j in range(HG):
                ins = pe.matmul(o_ps[32 * j:32 * j + VW, :], v_cur[:, hg, kt, j * VW:(j + 1) * VW],
                                probs[:, s % 2, j, :], start=(kt == 0), stop=(kt == KT - 1))
            ins.then_inc(pv_ok, 1)

        def turned_maxima():
            columns = m_parts[:].rearrange("p r (j q) -> p (r j) q", j=HG)
            for q in range(KT // 2):
                ins = pe.transpose(m_turned[:, q * P:(q + 1) * P], columns[:, :, q], ident_b[:])
            return ins

        def spare_task(n, b, hg, task, arg):
            wait(pe, spare_done, n)
            if task == "turn":
                done = (b * NHG + hg) * 2 + (1 if arg == 0 else 0)
                pe.wait_ge(o_out, done)
                for t in range(4):
                    ins = pe.transpose(spare[:, t * P:(t + 1) * P], o_sb[:, t * P:(t + 1) * P], ident[:])
            elif task == "maxima":
                pe.wait_ge(split_ok, (b * NHG + hg) * 2 + (2 if arg else 3))
                ins = turned_maxima()
            elif task == "features":
                half, k = arg
                for t in range(4):
                    ins = pe.transpose(spare[:, t * P:(t + 1) * P], att[:, 4 * half + t, k * P:(k + 1) * P], ident[:])
            else:
                half, o = arg
                for tt in range(2):
                    t, dst = slice((2 * o + tt) * P, (2 * o + tt + 1) * P), spare[:, tt * D:(tt + 1) * D]
                    for k in range(KD):
                        pe.matmul(dst, at_hi[:, k, t], wo_hi[:, k, :], start=(tt == 0 and k == 0), stop=False,
                                  skip_group_check=True)
                        pe.matmul(dst, at_lo[:, k, t], wo_hi[:, k, :], start=False, stop=False, skip_group_check=True)
                        ins = pe.matmul(dst, at_hi[:, k, t], wo_lo[:, k, :], start=False, stop=(k == KD - 1),
                                        skip_group_check=True)
            ins.then_inc(spare_ps, 1)

        pe.wait_ge(ident_ok, 1)
        pe.wait_ge(qk_in[0], 2 * len(SLOTS) * 16)
        for u in range(HU):
            max_block(0, 0, u)
        pe.wait_ge(split_ok, 1)
        turned_maxima().then_inc(spare_ps, 1)
        for u in range(HU, HU + PER_STEP * LEAD):
            max_block(0, 0, u)
        pe.wait_ge(wo_lo_ok, 1)
        pe.wait_ge(ones_ok, 1)
        for pair in range(2):
            score_block(0, 0, 0, 0, pair)

        def body(b, last):
            for hg in range(NHG):
                g = b * NHG + hg
                for s in range(STEPS):
                    t = g * STEPS + s
                    units = max_units(b, hg, s, last)

                    def next_scores(pair):
                        if s < STEPS - 1:
                            score_block(b, hg, t + 1, s + 1, pair)
                        elif not (last and hg == NHG - 1):
                            score_block(b + (hg + 1) // NHG, (hg + 1) % NHG, t + 1, 0, pair)

                    def next_maxima(i):
                        if units:
                            max_block(*units[i])

                    if units and units[0][2] == 0:
                        pe.wait_ge(qk_in[units[0][1]], (b + (hg + 1) // NHG + 1) * 2 * len(SLOTS) * 16)
                    for pair in range(2):
                        next_scores(pair)
                    for i in range(PER_STEP // 2):
                        next_maxima(i)
                    weighted_values(b, hg, t, s)
                    for i in range(PER_STEP // 2, PER_STEP):
                        next_maxima(i)
                    for task, arg in tasks_at(b, hg, s):
                        spare_task(task_number(b, hg, task, arg), b, hg, task, arg)

        batches(pe, body)
        for task, arg in TAIL:
            spare_task(task_number(B, 0, task, arg), B, 0, task, arg)

    @block.scalar
    def _(act):
        act.wait_ge(wo_in, 16)
        act.activation(wo_hi[:], wo[:], ACT.Copy).then_inc(wo_hi_ok, 1)

        def exponentials(t, s):
            for pair in range(2):
                act.wait_ge(scores_ps, 2 * t + pair + 1)
                wait(act, pv_ok, t - 1)
                act.activation(probs[:, s % 2, 2 * pair:2 * pair + 2, :], scores[:, pair, :, :], ACT.Exp,
                               scale=1.0 / HD ** 0.5).then_inc(exp_ok, 1)

        def take_out(b, hg, half):
            h = (b * NHG + hg) * 2 + (0 if half == 0 else -1)
            act.wait_ge(pv_ok, (h + 1) * KT)
            if half == 0:
                if not (isinstance(b, int) and b == 0 and hg == 0):
                    act.wait_ge(spare_ps, task_number(b, hg, "turn", 1) + 1)
            else:
                before = (b, hg - 1) if hg else (b - 1, NHG - 1)
                act.wait_ge(spare_ps, task_number(*before, "turn", 0) + 1)
            act.activation(o_sb[:], o_ps[:], ACT.Copy).then_inc(o_out, 1)

        def high(n, arg):
            act.wait_ge(spare_ps, n + 1)
            act.activation(at_hi[:, arg[1], :], spare[:, :], ACT.Copy).then_inc(high_ok, 1)

        def maxima_out(h, n):
            act.wait_ge(spare_ps, n + 1)
            wait(act, m_in, h * 16)
            act.activation(m_rows[:], m_turned, ACT.Copy).then_inc(spare_done, 1)

        maxima_out(0, 0)

        def body(b, last):
            for hg in range(NHG):
                g = b * NHG + hg
                for s in range(STEPS):
                    exponentials(g * STEPS + s, s)
                    if s == KT:
                        take_out(b, hg, 0)
                    if s == 0 and not (isinstance(b, int) and b == 0 and hg == 0):
                        take_out(b, hg, 1)
                    for task, arg in tasks_at(b, hg, s - 1):
                        if task == "features":
                            high(task_number(b, hg, task, arg), arg)
                        if task == "maxima":
                            maxima_out(2 * g + (1 if arg else 2), task_number(b, hg, task, arg))

        batches(act, body)
        take_out(B, 0, 1)
        for task, arg in TAIL:
            if task == "features":
                high(task_number(B, 0, task, arg), arg)

    @block.vector
    def _(dve):
        dve.tensor_copy(ident_b[:], ident[:]).then_inc(ident_ok, 1)

        def reduce_block(g, _, u):
            dve.wait_ge(max_ps, g * UNITS + u + 1)
            dve.tensor_reduce(half_max[:, u // HU, u % HU:u % HU + 1], maxima[:, u % 2, :], AX.X, ALU.max, negate=True).then_inc(reduced, 1)

        def spare_task(n, b, hg, task, arg):
            dve.wait_ge(spare_ps, n + 1)
            if task == "turn":
                h = (b * NHG + hg) * 2 + (0 if arg == 0 else -1)
                src = spare[:, :].rearrange("p (t j w) -> p t j w", t=4, j=HG)
                dve.reciprocal(inv[:], src[:, :, :, HD]).then_inc(inv_ok, 1)
                dve.wait_ge(inv_ok, h + 1)
                g = hg if arg == 0 else (hg - 1) % NHG
                half = arg
                dst = att[:, 4 * half:4 * half + 4, g * HG * HD:(g + 1) * HG * HD]
                dve.tensor_tensor(dst.rearrange("p t (j d) -> p t j d", j=HG), src[:, :, :, 0:HD],
                                  inv[:].rearrange("p t (j o) -> p t j o", o=1).broadcast_to([P, 4, HG, HD]),
                                  ALU.mult).then_inc(spare_done, 1)
            elif task == "features":
                half, k = arg
                dve.wait_ge(high_ok, 4 * b + 2 * half + k + 1 - (4 if half else 0))
                dve.tensor_tensor(at_lo[:, k, :], spare[:, :], at_hi[:, k, :], ALU.subtract).then_inc(spare_done, 1)
            else:
                half, o = arg
                tile = bass.ds(b * KT + 4 * half - (KT if half else 0) + 2 * o, 2)
                dve.tensor_tensor(x_sb[:, tile, :], x_sb[:, tile, :],
                                  spare[:, :].rearrange("p (t d) -> p t d", t=2), ALU.add).then_inc(spare_done, 1)

        def whole_maxima(h, parity):
            halves = half_max[:, parity, :].rearrange("p (n k) -> p n k", k=2)
            wait(dve, split_ok, h)
            dve.wait_ge(reduced, (h + 1) * HU)
            dve.tensor_tensor(neg_max[:], halves[:, :, 0], halves[:, :, 1], ALU.min).then_inc(min_ok, 1)

        for u in range(HU):
            reduce_block(0, 0, u)
        whole_maxima(0, 0)
        dve.wait_ge(wo_hi_ok, 1)
        dve.tensor_tensor(wo_lo[:], wo[:], wo_hi[:], ALU.subtract).then_inc(wo_lo_ok, 1)
        for u in range(HU, HU + PER_STEP * LEAD):
            reduce_block(0, 0, u)

        def body(b, last):
            for hg in range(NHG):
                g = b * NHG + hg
                for s in range(STEPS):
                    if s == KT - LEAD:
                        whole_maxima(2 * g + 1, 1)
                    if s == STEPS - LEAD and not (last and hg == NHG - 1):
                        whole_maxima(2 * g + 2, 0)
                    for unit_of in max_units(b, hg, s, last):
                        reduce_block(*unit_of)
                    for task, arg in tasks_at(b, hg, s):
                        if task != "maxima":
                            spare_task(task_number(b, hg, task, arg), b, hg, task, arg)

        batches(dve, body)
        for task, arg in TAIL:
            spare_task(task_number(B, 0, task, arg), B, 0, task, arg)


_T = {"L0_attn_Wq": "Wq", "L0_attn_Wk": "Wk", "L0_attn_Wv": "Wv", "L0_attn_Wqa": "Wqa", "L0_attn_Wka": "Wka",
      "L0_ffn_gate_idx": "gate_idx", "L0_ffn_up_idx": "up_idx", "L0_ffn_down_idx": "down_idx",
      "L1_attn_w_qkv": "w_qkv", "L1_attn_w_o": "w_o", "L1_ffn_gate_weight": "router", "L1_ffn_gate_w": "gate_w",
      "L1_ffn_up_w": "up_w", "L1_ffn_down_w": "down_w", "L1_ffn_sh_gate_w": "sh_gate", "L1_ffn_sh_up_w": "sh_up",
      "L1_ffn_sh_down_w": "sh_down"}
_COLUMNS = {"L0_attn_bq": "bq", "L0_attn_bk": "bk", "L0_attn_bv": "bv", "L0_attn_bqa": "bqa", "L0_attn_bka": "bka",
            "L0_attn_ln_g": "ln_g", "L0_attn_ln_b": "ln_b", "L1_attn_b_qkv": "b_qkv"}
_ROWS = {"L0_ffn_lut": "lut", "L1_attn_b_qkv": "b_qkv_row", "L1_attn_b_o": "b_o"}


def lay_out(inputs):
    import numpy as _np

    laid = {"x": _np.ascontiguousarray(inputs["L0_attn_hidden_states"]).reshape(B * S, D)}
    for name, short in _T.items():
        laid[short] = _np.ascontiguousarray(_np.swapaxes(_np.asarray(inputs[name]), -1, -2))
    for name, short in _COLUMNS.items():
        laid[short] = _np.ascontiguousarray(_np.asarray(inputs[name]).reshape(-1, P).T)
    for name, short in _ROWS.items():
        laid[short] = _np.ascontiguousarray(inputs[name])
    return laid


def kernel(**inputs):
    import concourse.bacc as _bacc
    from concourse.bass_utils import run_bass_kernel_spmd as _run

    laid = lay_out(inputs)
    nc = _bacc.Bacc("TRN2", target_bir_lowering=False, num_devices=1)
    a = {n: nc.dram_tensor(f"in_{n}", v.shape, mybir.dt.from_np(v.dtype), kind="ExternalInput").ap()
         for n, v in laid.items()}
    out = nc.dram_tensor("out_0", (B, S, D), F32, kind="ExternalOutput").ap()
    build(nc, a, out)
    r = _run(nc, [{f"in_{n}": v for n, v in laid.items()}], core_ids=[0])
    return r.results[0]["out_0"]
```

```python
from contextlib import ExitStack

import concourse.bass as bass
from concourse import mybir

F32 = mybir.dt.float32
F32R = mybir.dt.float32r
BF16 = mybir.dt.bfloat16
I32 = mybir.dt.int32
ALU = mybir.AluOpType
ACT = mybir.ActivationFunctionType
AX = mybir.AxisListType

P = 128
B, S, D = 4, 1024, 256
KD = D // P
BLK = 512
NB = B * S // BLK
TT = BLK // P
NT = B * S // P
EPS = 1e-5
SCALE0 = 1.0 / D ** 0.5

F0 = 688
C0 = 6
F0C = [116] * 5 + [F0 - 5 * 116]
LUT = 16
FLAT0 = 4 * F0 + C0 * D
LC = 480
NLC = -(-FLAT0 // LC)

WQ, WK, WV, WQA, WKA = range(5)

H, HD = 16, D // 16
NX, FX, FS = 8, 176, 352
F1 = NX * FX + FS
CX = NX * FX // P
F1C = [P] * CX + [120, 120, 112]
C1 = len(F1C)
PART = 3
VW = 32
LANE = 32


def wait(eng, sem, value):
    if not isinstance(value, int) or value > 0:
        eng.wait_ge(sem, value)


def split3(pe, out, w_hi, w_lo, x_hi, x_lo, first, last):
    pe.matmul(out, w_hi, x_hi, start=first, stop=False, skip_group_check=True)
    pe.matmul(out, w_lo, x_hi, start=False, stop=False, skip_group_check=True)
    return pe.matmul(out, w_hi, x_lo, start=False, stop=last, skip_group_check=True)


def layer_norm_stats(sem, mean, var, raw, name):
    done = sem(f"{name}_stats_done")
    stats, work = raw
    steps = 6

    def run(dve):
        mean_e, mean_o = stats[:, :, 1], stats[:, :, 4]
        dve.tensor_tensor(work[:, 0, :], mean_e, mean_o, ALU.add).then_inc(done, 1)
        dve.tensor_tensor(work[:, 1, :], mean_e, mean_o, ALU.subtract).then_inc(done, 1)
        dve.tensor_tensor(work[:, 2, :], stats[:, :, 2], stats[:, :, 5], ALU.add).then_inc(done, 1)
        dve.wait_ge(done, 1)
        dve.tensor_scalar(mean[:], work[:, 0, :], 0.5, None, ALU.mult).then_inc(done, 1)
        dve.wait_ge(done, 2)
        dve.scalar_tensor_tensor(work[:, 3, :], work[:, 1, :], 0.25, work[:, 1, :], ALU.mult, ALU.mult).then_inc(done, 1)
        dve.wait_ge(done, 5)
        dve.scalar_tensor_tensor(var[:], work[:, 2, :], 1.0 / D, work[:, 3, :], ALU.mult, ALU.add).then_inc(done, 1)
        dve.wait_ge(done, steps)
    return run, (done, steps)


def build(nc, a, out, stop_after=None):
    with ExitStack() as whole:
        def persistent(name, shape, dt, ctx=whole):
            return ctx.enter_context(nc.sbuf_tensor(name, shape, dt))

        def sem(name):
            return whole.enter_context(nc.semaphore(name))

        x_sb = persistent("x_sb", [P, NT, D], F32)
        ident = persistent("ident", [P, P], F32)
        mean = persistent("mean", [P, NT], F32)
        var = persistent("var", [P, NT], F32)
        rstd = persistent("rstd", [P, NT], F32)
        shift = persistent("shift", [P, NT], F32)
        stats = persistent("stats", [P, NT, 6], F32)
        pair = persistent("stat_work", [P, 4, NT], F32)
        eps_col = persistent("eps_col", [P, 1], F32)
        half_max = persistent("half_max", [P, 2, HU], F32)
        x_loaded = sem("x_loaded")
        stored = sem("stored")

        ahead = ExitStack()
        raw = {n: ahead.enter_context(nc.sbuf_tensor(n, shape, F32, side="right")) for n, shape in
               (("gu_raw", [P, 2, KD, F1]), ("qkv_raw", [P, KD, 3 * D]), ("rt_raw", [P, KD, NX]))}
        raw_in = {n: sem(f"l1_{n}_loaded") for n in ("gu", "qkv")}

        def load_ahead(sp):
            qkv, rt, gu = raw["qkv_raw"], raw["rt_raw"], raw["gu_raw"]
            sp.dma_start(qkv[:], a["w_qkv"].rearrange("(k p) o -> p k o", p=P)).then_inc(raw_in["qkv"], 16)
            sp.dma_start(rt[:], a["router"].rearrange("(k p) o -> p k o", p=P)).then_inc(raw_in["qkv"], 16)
            for w, (routed_w, shared_w) in enumerate((("gate_w", "sh_gate"), ("up_w", "sh_up"))):
                for k in range(KD):
                    rows = slice(k * P, (k + 1) * P)
                    sp.dma_start(gu[:, w, k, 0:NX * FX].rearrange("p (n f) -> p n f", n=NX),
                                 a[routed_w][:, rows, :].rearrange("n p f -> p n f")).then_inc(raw_in["gu"], 16)
                    sp.dma_start(gu[:, w, k, NX * FX:F1], a[shared_w][rows, :]).then_inc(raw_in["gu"], 16)

        with ExitStack() as layer0:
            prepare_and_run_layer0(nc, a, layer0, sem, x_sb, ident, mean, var, rstd, shift, (stats, pair),
                                   eps_col, x_loaded, load_ahead)
        if stop_after != 0:
            scratch = {n: nc.dram_tensor(n, [B, PART, D, S], BF16) for n in ("q_parts", "k_parts")}
            scratch["v"] = nc.dram_tensor("v_scratch", [NT, P, H * VW], F32)
            run_layer1_ffn(nc, a, ahead, sem, x_sb, ident, mean, var, rstd, shift, (stats, pair), eps_col, scratch,
                           raw, raw_in, half_max)
        if stop_after is None:
            run_layer1_attention(nc, a, whole, sem, x_sb, ident, scratch, half_max, out)
        if stop_after in (0, 1):
            block = whole.enter_context(nc.Block())

            @block.sync
            def _(sp):
                sp.dma_start(out.rearrange("b (n p) d -> p (b n) d", p=P), x_sb[:]).then_inc(stored, 16)
                sp.wait_ge(stored, 16)


def prepare_and_run_layer0(nc, a, scope, sem, x_sb, ident, mean, var, rstd, shift, stat_raw, eps_col, x_loaded,
                           load_ahead):
    def sb(name, shape, dt, ctx=scope):
        return ctx.enter_context(nc.sbuf_tensor(name, shape, dt))

    w_hi = sb("w_hi", [P, 5, KD, D], F32R)
    w_lo = sb("w_lo", [P, 5, KD, D], F32R)
    f_hi = sb("f_hi", [P, NLC * LC], F32R)
    f_lo = sb("f_lo", [P, NLC * LC], F32R)
    bias = sb("bias", [P, 5, KD], F32)
    rstd_h = sb("rstd_h", [P, NT], F32)
    shift_h = sb("shift_h", [P, NT], F32)
    ones = sb("ones", [P, BLK], F32)

    def gate_up(t, w, k, c):
        lo = (2 * w + k) * F0 + sum(F0C[:c])
        return t[:, lo:lo + F0C[c]]

    def down(t, c):
        return t[0:F0C[c], 4 * F0 + c * D:4 * F0 + (c + 1) * D]

    with ExitStack() as ctx:
        def st(name, shape, dt):
            return sb(name, shape, dt, ctx)

        def pb(name, shape):
            return ctx.enter_context(nc.psum_tensor(name, shape, F32))

        w_raw = st("w_raw", [P, 5, KD, D], F32)
        b_raw = st("b_raw", [P, 5, KD], F32)
        ln_g, ln_b = st("ln_g", [P, KD], F32), st("ln_b", [P, KD], F32)
        idx = st("idx", [P, NLC * LC], I32)
        lut, lut_lo = st("lut", [P, LUT], F32), st("lut_lo", [P, LUT], F32R)
        lut_hi = st("lut_hi", [P, LUT], F32R)
        d_hi, d_lo = st("d_hi", [P, LUT, P], F32R), st("d_lo", [P, LUT, P], F32R)
        mask = st("mask", [P, 4, LC], F32R)
        small = st("small", [P, 4, NT], F32)
        pb_bias, pb_hi, pb_lo = pb("pb_bias", [P, 512]), pb("pb_hi", [P, 2, 512]), pb("pb_lo", [P, 2, 512])

        w_loaded, small_loaded, idx_loaded = sem("w_loaded"), sem("small_loaded"), sem("idx_loaded")
        lut_loaded, gate_loaded = sem("lut_loaded"), sem("gate_loaded")
        idx_zero, ident_ready, ident_zero = sem("idx_zero"), sem("ident_ready"), sem("ident_zero")
        lut_split, diag_hi, diag_lo, mask_ready, mask_used = (sem("lut_split"), sem("diag_hi"), sem("diag_lo"),
                                                              sem("mask_ready"), sem("mask_used"))
        weights_kept = sem("weights_kept")
        bias_ps, bias_ready, w_scaled, w_hi_ready, w_lo_ready = (sem("bias_ps"), sem("bias_ready"), sem("w_scaled"),
                                                                 sem("w_hi_ready"), sem("w_lo_ready"))
        stat_step, root_ready = sem("stat_step"), sem("root_ready")
        constants = sem("constants")
        x_rows = sem("x_rows")
        stats_of, stats_kept = layer_norm_stats(sem, mean, var, stat_raw, "ln0")

        def lut_chunks(eng, body):
            for i in range(3):
                body(i, i % 2)
            with eng.Fori(0, (NLC - 3) // 2) as m:
                body(2 * m + 3, 1)
                body(2 * m + 4, 0)

        def is_chunk(i, number):
            return isinstance(i, int) and i == number

        block = ctx.enter_context(nc.Block())

        @block.sync
        def _(sp):
            for w, name in enumerate(("gate_idx", "up_idx")):
                sp.dma_start(idx[:, 2 * w * F0:2 * (w + 1) * F0].rearrange("p (k f) -> p k f", k=KD),
                             a[name].rearrange("(k p) f -> p k f", p=P)).then_inc(idx_loaded if w else gate_loaded, 16)
            sp.dma_start(ln_g[:], a["ln_g"]).then_inc(small_loaded, 16)
            sp.dma_start(ln_b[:], a["ln_b"]).then_inc(small_loaded, 16)
            for i, name in enumerate(("q", "k", "v", "qa", "ka")):
                sp.dma_start(w_raw[:, i, :, :], a["W" + name].rearrange("(k p) o -> p k o", p=P)).then_inc(w_loaded, 16)
                sp.dma_start(b_raw[:, i, :], a["b" + name]).then_inc(small_loaded, 16)
            sp.wait_ge(idx_zero, 1)
            for c in range(C0):
                f = sum(F0C[:c])
                sp.dma_start(down(idx, c), a["down_idx"][f:f + F0C[c], :]).then_inc(idx_loaded, 16)
            sp.dma_start(x_sb[:], a["x"].rearrange("(n p) d -> p n d", p=P)).then_inc(x_loaded, 16)

        @block.scalar
        def _(act):
            act.dma_start(lut[:], a["lut"].rearrange("(o n) -> o n", o=1).broadcast_to([P, LUT])).then_inc(lut_loaded, 16)
            act.wait_ge(lut_split, 2)
            act.wait_ge(ident_ready, 1)
            for j in range(LUT):
                act.activation(d_lo[:, j, :], ident[:], ACT.Copy,
                               scale=lut_lo[:, j:j + 1].bitcast(F32)).then_inc(diag_lo, 1)

            def keep(i, par):
                act.wait_ge(mask_used, i * LUT + 4 + LUT)
                act.activation(f_hi[:, bass.ds(i * LC, LC)], pb_hi[:, par, 0:LC], ACT.Copy).then_inc(weights_kept, 1)
                act.activation(f_lo[:, bass.ds(i * LC, LC)], pb_lo[:, par, 0:LC], ACT.Copy).then_inc(weights_kept, 1)
                if is_chunk(i, 2):
                    act.wait_ge(bias_ps, 3 * KD)
                    for w in (WQ, WK, WV):
                        for k in range(KD):
                            act.activation(w_raw[:, w, k, :], w_raw[:, w, k, :], ACT.Copy,
                                           scale=ln_g[:, k:k + 1]).then_inc(w_scaled, 1)
                    act.wait_ge(w_scaled, 3 * KD)
                    for w in range(5):
                        act.activation(w_hi[:, w, :, :], w_raw[:, w, :, :], ACT.Copy).then_inc(w_hi_ready, 1)

            lut_chunks(act, keep)
            act.wait_ge(*stats_kept)
            act.wait_ge(constants, 2)
            act.activation(small[:, 0, :], var[:], ACT.Sqrt, bias=eps_col[:]).then_inc(root_ready, 1)
            act.wait_ge(stat_step, 3)
            act.activation(small[:, 2, :], small[:, 1, :], ACT.Sqrt, bias=eps_col[:]).then_inc(root_ready, 1)

        @block.gpsimd
        def _(pool):
            pool.memset(ident[:], 0.0).then_inc(ident_zero, 1)
            pool.wait_ge(ident_zero, 1)
            pool.affine_select(out=ident[:], in_=ident[:], compare_op=ALU.not_equal, fill=1.0, base=0,
                               pattern=[[-1, P]], channel_multiplier=1).then_inc(ident_ready, 1)
            pool.memset(idx[:, 4 * F0:], 0).then_inc(idx_zero, 1)
            for w in range(5):
                pool.wait_ge(w_hi_ready, w + 1)
                pool.tensor_tensor(w_lo[:, w, :, :], w_raw[:, w, :, :], w_hi[:, w, :, :],
                                   ALU.subtract).then_inc(w_lo_ready, 1)
            pool.wait_ge(w_lo_ready, 5)

        @block.vector
        def _(dve):
            dve.memset(ones[:], 1.0).then_inc(constants, 1)
            dve.memset(eps_col[:], EPS).then_inc(constants, 1)
            dve.wait_ge(lut_loaded, 16)
            dve.tensor_copy(lut_hi[:], lut[:]).then_inc(lut_split, 1)
            dve.wait_ge(lut_split, 1)
            dve.tensor_tensor(lut_lo[:], lut[:], lut_hi[:], ALU.subtract).then_inc(lut_split, 1)
            dve.wait_ge(ident_ready, 1)
            dve.wait_ge(gate_loaded, 16)

            def masks(i, par):
                def statistics_of_tile(j, i=i):
                    t = bass.ds((i - 1) * TT + j, 1)
                    dve.bn_stats(stat_raw[0][:, t, :], x_sb[:, t, :]).then_inc(x_rows, 1)

                if is_chunk(i, 2):
                    dve.wait_ge(idx_loaded, (1 + C0) * 16)
                for j in range(LUT):
                    if is_chunk(i, 0):
                        dve.tensor_scalar(d_hi[:, j, :], ident[:], lut_hi[:, j:j + 1].bitcast(F32), None,
                                          ALU.mult).then_inc(diag_hi, 1)
                    dve.wait_ge(mask_used, i * LUT + j + 1)
                    dve.tensor_scalar(mask[:, j % 4, :], idx[:, bass.ds(i * LC, LC)], float(j), None,
                                      ALU.is_equal).then_inc(mask_ready, 1)
                    if j % 4 == 3 and not isinstance(i, int):
                        statistics_of_tile(j // 4)
                if is_chunk(i, 2):
                    dve.wait_ge(x_loaded, 16)
                    for j in range(2 * TT):
                        statistics_of_tile(j, 1)

            lut_chunks(dve, masks)
            dve.wait_ge(small_loaded, 7 * 16)
            dve.wait_ge(bias_ps, 3 * KD)
            for w in (WQ, WK, WV):
                dve.tensor_tensor(bias[:, w, :], pb_bias[:, w * KD:(w + 1) * KD], b_raw[:, w, :],
                                  ALU.add).then_inc(bias_ready, 1)
            for w in (WQA, WKA):
                dve.tensor_scalar(bias[:, w, :], b_raw[:, w, :], SCALE0, None, ALU.mult).then_inc(bias_ready, 1)
            dve.wait_ge(x_rows, NT)
            stats_of(dve)
            dve.wait_ge(root_ready, 1)
            dve.reciprocal(rstd[:], small[:, 0, :]).then_inc(stat_step, 1)
            dve.wait_ge(stat_step, 1)
            dve.tensor_tensor(small[:, 3, :], rstd[:], rstd[:], ALU.mult).then_inc(stat_step, 1)
            dve.wait_ge(stat_step, 2)
            dve.tensor_tensor(small[:, 1, :], var[:], small[:, 3, :], ALU.mult).then_inc(stat_step, 1)
            dve.scalar_tensor_tensor(shift[:], mean[:], -1.0, rstd[:], ALU.mult, ALU.mult).then_inc(stat_step, 1)
            dve.wait_ge(root_ready, 2)
            dve.reciprocal(small[:, 0, :], small[:, 2, :]).then_inc(stat_step, 1)
            dve.wait_ge(stat_step, 5)
            dve.tensor_tensor(rstd_h[:], rstd[:], small[:, 0, :], ALU.mult).then_inc(stat_step, 1)
            dve.tensor_tensor(shift_h[:], shift[:], small[:, 0, :], ALU.mult).then_inc(stat_step, 1)

        @block.tensor
        def _(pe):
            pe.sem_inc(mask_used, 4)
            pe.sem_inc(weights_kept, 2)

            def look_up(i, par):
                if not is_chunk(i, 0):
                    pe.wait_ge(weights_kept, i * 2)
                for j in range(LUT):
                    if is_chunk(i, 0):
                        pe.wait_ge(diag_hi, j + 1)
                        pe.wait_ge(diag_lo, j + 1)
                    pe.wait_ge(mask_ready, i * LUT + j + 1)
                    pe.matmul(pb_hi[:, par, 0:LC], d_hi[:, j, :], mask[:, j % 4, :], start=(j == 0), stop=(j == LUT - 1))
                    pe.matmul(pb_lo[:, par, 0:LC], d_lo[:, j, :], mask[:, j % 4, :], start=(j == 0),
                              stop=(j == LUT - 1)).then_inc(mask_used, 1)
                if is_chunk(i, 2):
                    pe.wait_ge(w_loaded, 5 * 16)
                    pe.wait_ge(small_loaded, 7 * 16)
                    for w in (WQ, WK, WV):
                        for c in range(KD):
                            for k in range(KD):
                                ins = pe.matmul(pb_bias[:, w * KD + c:w * KD + c + 1], w_raw[:, w, k, c * P:(c + 1) * P],
                                                ln_b[:, k:k + 1], start=(k == 0), stop=(k == KD - 1),
                                                skip_group_check=True)
                            ins.then_inc(bias_ps, 1)

            lut_chunks(pe, look_up)

    run_layer0(nc, scope, sem, x_sb, ident, rstd, shift, rstd_h, shift_h, ones, bias, w_hi, w_lo, f_hi, f_lo,
               gate_up, down, stat_raw[0], load_ahead)


def run_layer0(nc, scope, sem, x_sb, ident, rstd, shift, rstd_h, shift_h, ones, bias, w_hi, w_lo, f_hi, f_lo,
               gate_up, down, stats, load_ahead):
    def sb(name, shape, dt=F32):
        return scope.enter_context(nc.sbuf_tensor(name, shape, dt))

    x_tok, h_tok = sb("x_tok", [P, TT, D]), sb("h_tok", [P, TT, D])
    xt_hi, xt_lo = sb("xt_hi", [P, 2 * KD, BLK], F32R), sb("xt_lo", [P, 2 * KD, BLK], F32R)
    q_sb, e_sb, sum_sb, rc_sb = (sb(n, [P, KD, BLK]) for n in ("q_sb", "e_sb", "sum_sb", "rc_sb"))
    pool1, sum2, pool2, mixed = (sb(n, [P, KD, BLK]) for n in ("pool1", "sum2", "pool2", "mixed"))
    c_hi, c_lo = sb("c_hi", [P, KD, BLK], F32R), sb("c_lo", [P, KD, BLK], F32R)
    silu, hid = sb("silu", [P, 2, BLK]), sb("hid", [P, 2, BLK])
    hid_hi, hid_lo = sb("hid_hi", [P, 2, BLK], F32R), sb("hid_lo", [P, 2, BLK], F32R)
    ps = scope.enter_context(nc.psum_tensor("ps0", [P, 8, 512], F32))
    proj = ps[:, 0:2, :]
    ring = ps[:, 2:6, :]
    acc = ps[:, 6:8, :].rearrange("p h (j d) -> p (h j) d", d=D)

    names = ("l0_xtok l0_htok l0_xt_ps l0_xt_hi l0_xt_lo l0_proj_ps l0_q l0_chi l0_clo l0_exp l0_times l0_sum "
             "l0_recip l0_weight l0_weight0 l0_pooled l0_mixed l0_attn l0_gu_ps l0_silu l0_hid l0_hid_hi l0_hid_lo l0_down "
             "l0_acc_ps l0_x1 l0_stat_rows").split()
    (xtok, htok, xt_ps, xt_hi_ok, xt_lo_ok, proj_ps, q_ok, chi_ok, clo_ok, exp_ok, times_ok, sum_ok,
     recip_ok, weight_ok, weight0_ok, pooled_ok, mixed_ok, attn_ok, gu_ps, silu_ok, hid_ok, hid_hi_ok, hid_lo_ok, down_ok,
     acc_ps, x1_ok, rows_ok) = (sem(n) for n in names)
    block = scope.enter_context(nc.Block())

    @block.sync
    def _(sp):
        load_ahead(sp)

    def steps(eng, body):
        for u in range(2):
            body(u, u, False)
        with eng.Fori(1, B - 1) as b:
            for u in range(2):
                body(b * 2 + u, u, False)
        for u in range(2):
            body((B - 1) * 2 + u, u, u == 1)

    @block.tensor
    def _(pe):
        def transposes(m, first=False):
            for t in range(2 * KD):
                wait(pe, xtok if t < KD else htok, m * TT + TT)
                if not first:
                    wait(pe, hid_ok if t % 2 else silu_ok, m * C0 - 1 + t // 2)
                tok, k = (x_tok, t) if t < KD else (h_tok, t - KD)
                for j in range(TT):
                    ins = pe.transpose(ring[:, t, j * P:(j + 1) * P], tok[:, j, k * P:(k + 1) * P], ident[:])
                ins.then_inc(xt_ps, 1)

        def projection(i, first, hi, lo):
            for c in range(KD):
                for k in range(KD):
                    o = slice(c * P, (c + 1) * P)
                    ins = split3(pe, proj[:, c, :], w_hi[:, i, k, o], w_lo[:, i, k, o], hi[:, first + k, :],
                                 lo[:, first + k, :], k == 0, k == KD - 1)
                ins.then_inc(proj_ps, 1)

        def gate_and_up(n, c):
            r = 2 * (c % 2)
            if c >= 2:
                wait(pe, silu_ok, n * C0 + c - 1)
                wait(pe, hid_ok, n * C0 + c - 1)
            for w in range(2):
                for k in range(KD):
                    ins = split3(pe, ring[0:F0C[c], r + w, :], gate_up(f_hi, w, k, c), gate_up(f_lo, w, k, c),
                                 xt_hi[:, k, :], xt_lo[:, k, :], k == 0, k == KD - 1)
                ins.then_inc(gu_ps, 1)

        def down_chunk(n, c):
            wait(pe, hid_hi_ok, n * C0 + c + 1)
            wait(pe, hid_lo_ok, n * C0 + c + 1)
            if c == 0:
                wait(pe, x1_ok, n * 2)
            for j in range(TT):
                t = slice(j * P, (j + 1) * P)
                f = slice(0, F0C[c])
                pe.matmul(acc[:, j, :], hid_hi[f, c % 2, t], down(f_hi, c), start=(c == 0 and j % 2 == 0),
                          stop=False, skip_group_check=True)
                pe.matmul(acc[:, j, :], hid_lo[f, c % 2, t], down(f_hi, c), start=False, stop=False,
                          skip_group_check=True)
                ins = pe.matmul(acc[:, j, :], hid_hi[f, c % 2, t], down(f_lo, c), start=False, stop=False,
                                skip_group_check=True)
            ins.then_inc(down_ok, 1)

        def first_chunk(m):
            wait(pe, xt_hi_ok, m * 4 + 4)
            wait(pe, xt_lo_ok, m * 4 + 4)
            gate_and_up(m, 0)

        def add_attention():
            for j in range(TT):
                for k in range(KD):
                    ins = pe.matmul(acc[:, j, k * P:(k + 1) * P], mixed[:, k, j * P:(j + 1) * P], ident[:],
                                    start=False, stop=(k == KD - 1 and j % 2 == 1), skip_group_check=True)
                if j % 2:
                    ins.then_inc(acc_ps, 1)

        transposes(0, first=True)
        first_chunk(0)

        def body(n, u, last):
            wait(pe, attn_ok, n * KD)
            projection(WQ, KD, xt_hi, xt_lo)
            if not (isinstance(n, int) and n == 0):
                add_attention()
            gate_and_up(n, 1)
            wait(pe, chi_ok, n * 2 * KD + KD)
            wait(pe, clo_ok, n * 2 * KD + KD)
            projection(WQA, 0, c_hi, c_lo)
            gate_and_up(n, 2)
            wait(pe, exp_ok, n * 2 * KD + KD)
            projection(WK, KD, xt_hi, xt_lo)
            down_chunk(n, 0)
            gate_and_up(n, 3)
            down_chunk(n, 1)
            gate_and_up(n, 4)
            down_chunk(n, 2)
            wait(pe, chi_ok, n * 2 * KD + 2 * KD)
            wait(pe, clo_ok, n * 2 * KD + 2 * KD)
            projection(WKA, 0, c_hi, c_lo)
            gate_and_up(n, 5)
            down_chunk(n, 3)
            wait(pe, exp_ok, n * 2 * KD + 2 * KD)
            projection(WV, KD, xt_hi, xt_lo)
            if not last:
                transposes(n + 1)
            down_chunk(n, 4)
            down_chunk(n, 5)
            if not last:
                first_chunk(n + 1)

        steps(pe, body)
        wait(pe, attn_ok, NB * KD)
        add_attention()

    @block.scalar
    def _(act):
        def twice_normalised(m):
            wait(act, xt_ps, m * 4)
            for j in range(TT):
                t = bass.ds(m * TT + j, 1)
                act.activation(h_tok[:, j, :], x_sb[:, t, :], ACT.Identity, scale=rstd_h[:, t],
                               bias=shift_h[:, t]).then_inc(htok, 1)

        def transposed(m):
            for t in range(2 * KD):
                wait(act, xt_ps, m * 4 + t + 1)
                act.activation(xt_hi[:, t, :], ring[:, t, :], ACT.Copy).then_inc(xt_hi_ok, 1)

        def silu_of(n, c):
            wait(act, gu_ps, n * 2 * C0 + 2 * c + 1)
            if c >= 2:
                wait(act, hid_ok, n * C0 + c - 1)
            f = slice(0, F0C[c])
            act.activation(silu[f, c % 2, :], ring[f, 2 * (c % 2), :], ACT.Silu).then_inc(silu_ok, 1)

        def hidden_high(n, c):
            wait(act, hid_ok, n * C0 + c + 1)
            if c >= 2:
                wait(act, down_ok, n * C0 + c - 1)
            f = slice(0, F0C[c])
            act.activation(hid_hi[f, c % 2, :], hid[f, c % 2, :], ACT.Copy).then_inc(hid_hi_ok, 1)

        def exponentials(n, which, i):
            for c in range(KD):
                wait(act, proj_ps, n * 5 * KD + (3 * KD if which else KD) + c + 1)
                act.activation(e_sb[:, c, :], proj[:, c, :], ACT.Exp, scale=SCALE0,
                               bias=bias[:, i, c:c + 1]).then_inc(exp_ok, 1)

        twice_normalised(0)
        transposed(0)

        def body(n, u, last):
            silu_of(n, 0)
            for c in range(KD):
                wait(act, proj_ps, n * 5 * KD + c + 1)
                act.activation(q_sb[:, c, :], proj[:, c, :], ACT.Identity, bias=bias[:, WQ, c:c + 1]).then_inc(q_ok, 1)
            if not last:
                twice_normalised(n + 1)
            hidden_high(n, 0)
            silu_of(n, 1)
            hidden_high(n, 1)
            exponentials(n, 0, WQA)
            silu_of(n, 2)
            hidden_high(n, 2)
            silu_of(n, 3)
            silu_of(n, 4)
            hidden_high(n, 3)
            for c in range(KD):
                wait(act, mixed_ok, n * KD + c + 1)
                act.activation(c_hi[:, c, :], mixed[:, c, :], ACT.Copy).then_inc(chi_ok, 1)
            hidden_high(n, 4)
            exponentials(n, 1, WKA)
            silu_of(n, 5)
            hidden_high(n, 5)
            if not last:
                transposed(n + 1)

        steps(act, body)

    @block.gpsimd
    def _(pool):
        def hidden_low(n, c):
            wait(pool, hid_hi_ok, n * C0 + c + 1)
            f = slice(0, F0C[c])
            pool.tensor_tensor(hid_lo[f, c % 2, :], hid[f, c % 2, :], hid_hi[f, c % 2, :],
                               ALU.subtract).then_inc(hid_lo_ok, 1)

        def weighted(n, which):
            k = 2 * KD * n + KD * which
            wait(pool, recip_ok, k + 1)
            wait(pool, times_ok, k + 1)
            pool.tensor_tensor(rc_sb[:, 0, :], rc_sb[:, 0, :], q_sb[:, 0, :], ALU.mult).then_inc(weight0_ok, 1)

        def body(n, u, last):
            hidden_low(n, 0)
            hidden_low(n, 1)
            for c in range(KD):
                wait(pool, exp_ok, n * 2 * KD + c + 1)
                pool.tensor_tensor(q_sb[:, c, :], q_sb[:, c, :], e_sb[:, c, :], ALU.mult).then_inc(times_ok, 1)
            weighted(n, 0)
            hidden_low(n, 2)
            hidden_low(n, 3)
            hidden_low(n, 4)
            for c in range(KD):
                wait(pool, exp_ok, n * 2 * KD + KD + c + 1)
                pool.tensor_tensor(q_sb[:, c, :], mixed[:, c, :], e_sb[:, c, :], ALU.mult).then_inc(times_ok, 1)
            weighted(n, 1)
            hidden_low(n, 5)

        steps(pool, body)

    @block.vector
    def _(dve):
        def once_normalised(m):
            wait(dve, xt_ps, m * 4)
            for j in range(TT):
                t = bass.ds(m * TT + j, 1)
                dve.tensor_scalar(x_tok[:, j, :], x_sb[:, t, :], rstd[:, t], shift[:, t], ALU.mult,
                                  ALU.add).then_inc(xtok, 1)

        def add_to_x(m):
            for h in range(TT // 2):
                wait(dve, acc_ps, m * 2 + h + 1)
                t = bass.ds(m * TT + 2 * h, 2)
                dve.tensor_tensor(x_sb[:, t, :], x_sb[:, t, :], acc[:, 2 * h:2 * h + 2, :], ALU.add).then_inc(x1_ok, 1)

        def statistics(m):
            for j in range(TT):
                t = bass.ds(m * TT + j, 1)
                dve.bn_stats(stats[:, t, :], x_sb[:, t, :]).then_inc(rows_ok, 1)

        def transposed_low(m):
            for t in range(2 * KD):
                wait(dve, xt_hi_ok, m * 4 + t + 1)
                dve.tensor_tensor(xt_lo[:, t, :], ring[:, t, :], xt_hi[:, t, :], ALU.subtract).then_inc(xt_lo_ok, 1)

        def hidden(n, c):
            wait(dve, silu_ok, n * C0 + c + 1)
            wait(dve, gu_ps, n * 2 * C0 + 2 * c + 2)
            if c >= 2:
                wait(dve, hid_lo_ok, n * C0 + c - 1)
            f = slice(0, F0C[c])
            dve.tensor_tensor(hid[f, c % 2, :], silu[f, c % 2, :], ring[f, 2 * (c % 2) + 1, :],
                              ALU.mult).then_inc(hid_ok, 1)

        def running_sum(sem_out, dst, src, waits, u, weights=None):
            for c in range(KD):
                if weights is not None:
                    wait(dve, weight_ok if c else weight0_ok, weights)
                for s, v in waits:
                    wait(dve, s, v + c + 1)
                carry = dst[:, c, BLK - 1:BLK] if u else 0.0
                dve.tensor_tensor_scan(dst[:, c, :], ones[:], src[:, c, :], carry, ALU.mult, ALU.add).then_inc(sem_out, 1)

        def reciprocal(n, which, c):
            k = 2 * KD * n + KD * which + c
            wait(dve, sum_ok, k + 1)
            src = sum2 if which else sum_sb
            dve.reciprocal(rc_sb[:, c, :], src[:, c, :]).then_inc(recip_ok, 1)

        def weighted(n, which):
            k = 2 * KD * n + KD * which + 1
            wait(dve, recip_ok, k + 1)
            wait(dve, times_ok, k + 1)
            dve.tensor_tensor(rc_sb[:, 1, :], rc_sb[:, 1, :], q_sb[:, 1, :], ALU.mult).then_inc(weight_ok, 1)

        once_normalised(0)
        transposed_low(0)

        def body(n, u, last):
            hidden(n, 0)
            for c in range(KD):
                wait(dve, q_ok, n * KD + c + 1)
                dve.tensor_copy(c_hi[:, c, :], q_sb[:, c, :]).then_inc(chi_ok, 1)
            for c in range(KD):
                wait(dve, chi_ok, n * 2 * KD + c + 1)
                dve.tensor_tensor(c_lo[:, c, :], q_sb[:, c, :], c_hi[:, c, :], ALU.subtract).then_inc(clo_ok, 1)
            if not last:
                once_normalised(n + 1)
            if not (isinstance(n, int) and n == 0):
                add_to_x(n - 1)
            wait(dve, x1_ok, n * 2)
            hidden(n, 1)
            if not (isinstance(n, int) and n == 0):
                statistics(n - 1)
            running_sum(sum_ok, sum_sb, e_sb, [(exp_ok, n * 2 * KD)], u)
            reciprocal(n, 0, 0)
            hidden(n, 2)
            reciprocal(n, 0, 1)
            weighted(n, 0)
            hidden(n, 3)
            running_sum(pooled_ok, pool1, rc_sb, [], u, 2 * n + 1)
            for c in range(KD):
                wait(dve, proj_ps, n * 5 * KD + 2 * KD + c + 1)
                wait(dve, pooled_ok, n * 2 * KD + c + 1)
                dve.scalar_tensor_tensor(mixed[:, c, :], proj[:, c, :], bias[:, WK, c:c + 1], pool1[:, c, :],
                                         ALU.add, ALU.mult).then_inc(mixed_ok, 1)
            for c in range(KD):
                wait(dve, chi_ok, n * 2 * KD + KD + c + 1)
                dve.tensor_tensor(c_lo[:, c, :], mixed[:, c, :], c_hi[:, c, :], ALU.subtract).then_inc(clo_ok, 1)
            hidden(n, 4)
            running_sum(sum_ok, sum2, e_sb, [(exp_ok, n * 2 * KD + KD)], u)
            reciprocal(n, 1, 0)
            hidden(n, 5)
            reciprocal(n, 1, 1)
            if not last:
                transposed_low(n + 1)
            weighted(n, 1)
            running_sum(pooled_ok, pool2, rc_sb, [], u, 2 * n + 2)
            for c in range(KD):
                wait(dve, proj_ps, n * 5 * KD + 4 * KD + c + 1)
                wait(dve, pooled_ok, n * 2 * KD + KD + c + 1)
                dve.scalar_tensor_tensor(mixed[:, c, :], proj[:, c, :], bias[:, WV, c:c + 1], pool2[:, c, :],
                                         ALU.add, ALU.mult).then_inc(attn_ok, 1)
        steps(dve, body)
        add_to_x(NB - 1)
        wait(dve, x1_ok, NB * 2)
        statistics(NB - 1)
        wait(dve, rows_ok, NT)


def run_layer1_ffn(nc, a, ahead, sem, x_sb, ident, mean, var, rstd, shift, stat_raw, eps_col, scratch, raw, raw_in,
                   half_max):
    with ExitStack() as scope:
        def sb(name, shape, dt, ctx=scope):
            return ctx.enter_context(nc.sbuf_tensor(name, shape, dt))

        gu_hi, gu_lo = (sb(n, [P, 2, KD, F1], F32R) for n in ("gu_hi", "gu_lo"))
        dn_hi, dn_lo = (sb(n, [P, C1, D], F32R) for n in ("dn_hi", "dn_lo"))
        qkv_hi, qkv_lo = (sb(n, [P, KD, 3 * D], F32R) for n in ("qkv_hi", "qkv_lo"))
        rt_hi, rt_lo = (sb(n, [P, KD, NX], F32R) for n in ("rt_hi", "rt_lo"))
        expert_of = sb("expert_of", [3 * LANE, CX * P], BF16)
        before8 = sb("before8", [P, TT, NX, NX], BF16)
        before4 = sb("before4", [P, TT, NX // 2, NX // 2], BF16)
        w_parts = sb("w_parts", [P, TT, 3 * LANE], BF16)
        bv_row, bo_row = sb("bv_row", [P, D], F32), sb("bo_row", [P, D], F32)
        qk_bias = sb("qk_bias", [P, 3 * KD], F32)

        x_tok = sb("x_tok1", [P, TT, D], F32)
        xt_hi, xt_lo = sb("xt_hi1", [P, 2, KD, BLK], F32R), sb("xt_lo1", [P, 2, KD, BLK], F32R)
        ps = scope.enter_context(nc.psum_tensor("ps1", [P, 8, 512], F32))
        ring, misc = ps[:, 0:4, :], ps[:, 5, :]
        logits = misc[:, 0:TT * NX].rearrange("p (t e) -> p t e", t=TT)

        def router(pe, par):
            for j in range(TT):
                t = slice(j * P, (j + 1) * P)
                for k in range(KD):
                    pe.matmul(logits[:, j, :], xt_hi[:, par, k, t], rt_hi[:, k, :], start=(j == 0 and k == 0),
                              stop=False, skip_group_check=True)
                    pe.matmul(logits[:, j, :], xt_lo[:, par, k, t], rt_hi[:, k, :], start=False, stop=False,
                              skip_group_check=True)
                    ins = pe.matmul(logits[:, j, :], xt_hi[:, par, k, t], rt_lo[:, k, :], start=False,
                                    stop=(k == KD - 1), skip_group_check=True)
            return ins

        with ahead:
            load_layer1(nc, a, ahead, sem, x_sb, ident, x_tok, xt_hi, xt_lo, ring, router, mean, var, rstd, shift,
                        stat_raw, eps_col, gu_hi, gu_lo, dn_hi, dn_lo, qkv_hi, qkv_lo, rt_hi, rt_lo, expert_of,
                        before8, before4, w_parts, bv_row, bo_row, qk_bias,
                        raw, raw_in)
        layer1_steps(nc, scope, sem, x_sb, ident, x_tok, xt_hi, xt_lo, ps, logits, router, rstd, shift, scratch,
                     gu_hi, gu_lo, dn_hi, dn_lo, qkv_hi, qkv_lo, expert_of, before8, before4, w_parts, bv_row, bo_row,
                     qk_bias, half_max)


def load_layer1(nc, a, ctx, sem, x_sb, ident, x_tok, xt_hi, xt_lo, ring, router, mean, var, rstd, shift, stat_raw,
                eps_col, gu_hi, gu_lo, dn_hi, dn_lo, qkv_hi, qkv_lo, rt_hi, rt_lo, expert_of, before8, before4, w_parts,
                bv_row, bo_row, qk_bias, raw, raw_in):
    def st(name, shape, dt=F32):
        return ctx.enter_context(nc.sbuf_tensor(name, shape, dt, side="right"))

    gu, qkv, rt = raw["gu_raw"], raw["qkv_raw"], raw["rt_raw"]
    gu_loaded, qkv_loaded = raw_in["gu"], raw_in["qkv"]
    dn, small = st("dn_raw", [P, C1, D]), st("small1", [P, NT])
    names = "l1_dn_loaded l1_rows_loaded l1_hi l1_lo_dve l1_lo_pool l1_masks l1_root l1_rstd"
    dn_loaded, rows_loaded, hi_ok, lo_dve, lo_pool, masks, root, rstd_ok = (sem(n) for n in names.split())
    dn_zero = sem("l1_dn_zero")
    first_x, first_turned, first_hi, first_lo = (sem(f"l1_first_{n}") for n in ("x", "turned", "hi", "lo"))
    stats_of, stats_kept = layer_norm_stats(sem, mean, var, stat_raw, "ln1")
    block = ctx.enter_context(nc.Block())

    @block.sync
    def _(sp):
        sp.dma_start(bv_row[:], a["b_qkv_row"][2 * D:3 * D].rearrange("(o n) -> o n", o=1)
                      .broadcast_to([P, D])).then_inc(rows_loaded, 16)
        sp.dma_start(bo_row[:], a["b_o"].rearrange("(o n) -> o n", o=1).broadcast_to([P, D])).then_inc(rows_loaded, 16)
        sp.dma_start(qk_bias[:], a["b_qkv"]).then_inc(rows_loaded, 16)
        sp.dma_start(dn[:, 0:CX, :], a["down_w"].rearrange("n f d -> (n f) d").rearrange("(c p) d -> p c d", p=P)
                      ).then_inc(dn_loaded, 16)
        wait(sp, dn_zero, 1)
        for c in range(CX, C1):
            f = sum(F1C[CX:c])
            sp.dma_start(dn[0:F1C[c], c, :], a["sh_down"][f:f + F1C[c], :]).then_inc(dn_loaded, 16)

    @block.tensor
    def _(pe):
        pe.wait_ge(first_x, TT)
        for k in range(KD):
            for j in range(TT):
                ins = pe.transpose(ring[:, k, j * P:(j + 1) * P], x_tok[:, j, k * P:(k + 1) * P], ident[:])
            ins.then_inc(first_turned, 1)
        pe.wait_ge(hi_ok, 2)
        pe.wait_ge(lo_dve, 2)
        pe.wait_ge(first_hi, KD)
        pe.wait_ge(first_lo, KD)
        router(pe, 0)

    @block.scalar
    def _(act):
        wait(act, *stats_kept)
        act.activation(small[:], var[:], ACT.Sqrt, bias=eps_col[:]).then_inc(root, 1)
        wait(act, qkv_loaded, 32)
        act.activation(qkv_hi[:], qkv[:], ACT.Copy).then_inc(hi_ok, 1)
        act.activation(rt_hi[:], rt[:], ACT.Copy).then_inc(hi_ok, 1)
        wait(act, gu_loaded, 8 * 16)
        for w in range(2):
            for k in range(KD):
                act.activation(gu_hi[:, w, k, :], gu[:, w, k, :], ACT.Copy).then_inc(hi_ok, 1)
                if w == 0:
                    wait(act, first_turned, k + 1)
                    act.activation(xt_hi[:, 0, k, :], ring[:, k, :], ACT.Copy).then_inc(first_hi, 1)
        wait(act, dn_loaded, (1 + C1 - CX) * 16)
        for h in range(2):
            c = slice(h * C1 // 2, (h + 1) * C1 // 2)
            act.activation(dn_hi[:, c, :], dn[:, c, :], ACT.Copy).then_inc(hi_ok, 1)
        wait(act, rows_loaded, 48)

    @block.gpsimd
    def _(pool):
        pool.memset(dn[:, CX:C1, :], 0.0).then_inc(dn_zero, 1)
        pool.memset(expert_of[:], 1.0).then_inc(masks, 1)
        pool.memset(before8[:], 1.0).then_inc(masks, 1)
        pool.memset(before4[:], 1.0).then_inc(masks, 1)
        pool.memset(w_parts[:], 0.0).then_inc(masks, 1)
        wait(pool, masks, 4)
        for t, n in ((before8, NX), (before4, NX // 2)):
            pool.affine_select(out=t[:], in_=t[:], compare_op=ALU.is_gt, fill=0.0, base=0,
                               pattern=[[0, TT], [1, n], [-1, n]], channel_multiplier=0).then_inc(masks, 1)
        for r in range(PART):
            rows = expert_of[r * LANE:(r + 1) * LANE, :]
            pool.affine_select(out=rows, in_=rows, compare_op=ALU.is_ge, fill=0.0, base=0,
                               pattern=[[1, CX * P]], channel_multiplier=-FX).then_inc(masks, 1)
            wait(pool, masks, 7 + 2 * r)
            pool.affine_select(out=rows, in_=rows, compare_op=ALU.is_ge, fill=0.0, base=FX - 1,
                               pattern=[[-1, CX * P]], channel_multiplier=FX).then_inc(masks, 1)
        wait(pool, masks, 12)
        wait(pool, hi_ok, 6)
        pool.tensor_tensor(gu_lo[:, 1, 1, :], gu[:, 1, 1, :], gu_hi[:, 1, 1, :], ALU.subtract).then_inc(lo_pool, 1)
        wait(pool, lo_pool, 1)

    @block.vector
    def _(dve):
        stats_of(dve)
        wait(dve, root, 1)
        dve.reciprocal(rstd[:], small[:]).then_inc(rstd_ok, 1)
        wait(dve, rstd_ok, 1)
        dve.scalar_tensor_tensor(shift[:], mean[:], -1.0, rstd[:], ALU.mult, ALU.mult).then_inc(rstd_ok, 1)
        wait(dve, rstd_ok, 2)
        for j in range(TT):
            dve.tensor_scalar(x_tok[:, j, :], x_sb[:, j, :], rstd[:, j:j + 1], shift[:, j:j + 1], ALU.mult,
                              ALU.add).then_inc(first_x, 1)
        wait(dve, hi_ok, 1)
        dve.tensor_tensor(qkv_lo[:], qkv[:], qkv_hi[:], ALU.subtract).then_inc(lo_dve, 1)
        wait(dve, hi_ok, 2)
        dve.tensor_tensor(rt_lo[:], rt[:], rt_hi[:], ALU.subtract).then_inc(lo_dve, 1)
        for i, (w, k) in enumerate(((0, 0), (0, 1), (1, 0))):
            wait(dve, hi_ok, 3 + i)
            dve.tensor_tensor(gu_lo[:, w, k, :], gu[:, w, k, :], gu_hi[:, w, k, :], ALU.subtract).then_inc(lo_dve, 1)
            if i < KD:
                wait(dve, first_hi, i + 1)
                dve.tensor_tensor(xt_lo[:, 0, i, :], ring[:, i, :], xt_hi[:, 0, i, :], ALU.subtract).then_inc(first_lo, 1)
        for h in range(2):
            c = slice(h * C1 // 2, (h + 1) * C1 // 2)
            wait(dve, hi_ok, 7 + h)
            dve.tensor_tensor(dn_lo[:, c, :], dn[:, c, :], dn_hi[:, c, :], ALU.subtract).then_inc(lo_dve, 1)
        wait(dve, lo_dve, 7)


ORDER1 = list(range(CX, C1)) + list(range(CX))


def layer1_steps(nc, scope, sem, x_sb, ident, x_tok, xt_hi, xt_lo, ps, logits, router, rstd, shift, scratch,
                 gu_hi, gu_lo, dn_hi, dn_lo, qkv_hi, qkv_lo, expert_of, before8, before4, w_parts, bv_row, bo_row,
                 qk_bias, half_max):
    def sb(name, shape, dt=F32):
        return scope.enter_context(nc.sbuf_tensor(name, shape, dt, side="right"))

    parts = sb("parts", [P, 2 * KD, PART, BLK], BF16)
    rest = sb("rest", [P, 2, BLK])
    first_q, first_k = sb("first_q", [P, HG, HALF], BF16), sb("first_k", [P, HG, S], BF16)
    v_sb = sb("v_sb", [P, TT, H, VW])
    hid = sb("hid1", [P, 2, BLK])
    hid_hi, hid_lo = sb("hid_hi1", [P, 2, BLK], F32R), sb("hid_lo1", [P, 2, BLK], F32R)
    w_turned = sb("w_turned", [3 * LANE, BLK], BF16)
    ident_bf = sb("ident_bf", [P, P], BF16)
    top, total = sb("top", [P, TT]), sb("total", [P, TT])
    logit, score, kept = sb("logit", [P, TT, NX]), sb("score", [P, TT, NX]), sb("kept_score", [P, TT, NX])
    group, g_rank = sb("group", [P, TT, NX // 2]), sb("g_rank", [P, TT, NX // 2])
    rank, w_rest = sb("rank", [P, TT, NX]), sb("w_rest", [P, TT, NX])
    above, equal = sb("above", [P, TT, NX, NX], BF16), sb("equal", [P, TT, NX, NX], BF16)
    ring, spread, misc = ps[:, 0:4, :], ps[:, 4, :], ps[:, 5, :]
    acc = ps[:, 6:8, :].rearrange("p h (j d) -> p (h j) d", d=D)
    turned = misc[0:3 * LANE, 128:128 + BLK // 2].bitcast(BF16)

    names = ("l1_xtok l1_xt_ps l1_xt_hi l1_xt_lo l1_logits l1_route l1_exp l1_w_ready l1_turned_ps l1_w_turned l1_qk_ps l1_part1 "
             "l1_rest l1_part2 l1_part3 l1_v_ps l1_v l1_gu_ps l1_silu l1_prod l1_spread_ps l1_weighted "
             "l1_hid_hi l1_hid_lo l1_down l1_x2 l1_out l1_ones l1_ident_bf").split()
    (xtok, xt_ps, xt_hi_ok, xt_lo_ok, logits_ok, route, exp_ok, w_ready, turned_ps, w_turned_ok, qk_ps, part1, rest_ok, part2,
     part3, v_ps, v_ok, gu_ps, silu_ok, prod_ok, spread_ps, weighted_ok, hid_hi_ok, hid_lo_ok, down_ok,
     x2_ok, out_ok, ones_ok, ident_bf_ok) = (sem(n) for n in names)
    v_out = sem("l1_v_out")
    first_in, first_ps, first_reduced = sem("l1_first_in"), sem("l1_first_ps"), sem("l1_first_reduced")
    NQK = 2 * KD
    parts_out = [sem(f"l1_parts_out{c}") for c in range(NQK)]
    TURN_AT = (6, 9)
    block = scope.enter_context(nc.Block())

    def steps(eng, body):
        body(0, 0, False)
        with eng.Fori(0, NB // 2 - 1) as m:
            body(2 * m + 1, 1, False)
            body(2 * m + 2, 0, False)
        body(NB - 1, (NB - 1) % 2, True)

    def banks(i):
        return 2 * ((i + 1) % 2)

    def first_maxima(i, place):
        u = 3 * (i - (C1 - CX) - 1) + place
        return [u] if i > C1 - CX and u < HU else []

    def finished(n, i):
        if i < C1 - CX:
            return prod_ok, n * C1 + i + 1
        return weighted_ok, n * CX + i - (C1 - CX) + 1

    @block.tensor
    def _(pe):
        def transposes(m, k):
            if k == 0:
                wait(pe, xtok, m * TT + TT)
                wait(pe, w_turned_ok, m)
            else:
                wait(pe, xt_hi_ok, m * KD + k)
                wait(pe, xt_lo_ok, m * KD + k)
            for j in range(TT):
                ins = pe.transpose(misc[:, j * P:(j + 1) * P], x_tok[:, j, k * P:(k + 1) * P], ident[:])
            ins.then_inc(xt_ps, 1)

        def next_router(m, par):
            wait(pe, xt_hi_ok, m * KD + KD)
            wait(pe, xt_lo_ok, m * KD + KD)
            router(pe, par).then_inc(logits_ok, 1)

        def first_maximum(u):
            j, q, kh = unit(u)
            if u == 0:
                wait(pe, first_in, 2 * len(SLOTS) * 16)
            wait(pe, first_reduced, u)
            pe.matmul(misc, first_q[0:ROWS, j, q * P:(q + 1) * P], first_k[0:ROWS, j, kh * HALF:(kh + 1) * HALF],
                      start=True, stop=True).then_inc(first_ps, 1)

        def gate_and_up(n, par, i, last):
            c, r = ORDER1[i], banks(i)
            f = slice(sum(F1C[:c]), sum(F1C[:c + 1]))
            if i == 0:
                wait(pe, rest_ok, n * NQK + NQK)
            elif i == 1:
                wait(pe, v_ok, n * 2 + 2)
            else:
                wait(pe, silu_ok, n * C1 + i - 1)
                wait(pe, prod_ok, n * C1 + i - 1)
            for w in range(2):
                for k in range(KD):
                    ins = split3(pe, ring[0:F1C[c], r + w, :], gu_hi[:, w, k, f], gu_lo[:, w, k, f],
                                 xt_hi[:, par, k, :], xt_lo[:, par, k, :], k == 0, k == KD - 1)
                ins.then_inc(gu_ps, 1)
                for u in first_maxima(i, w) if last else ():
                    first_maximum(u)

        def spread_weights(n, c):
            wait(pe, w_turned_ok, n + 1)
            wait(pe, weighted_ok, n * CX + c)
            pe.matmul(spread[:, :], expert_of[:, c * P:(c + 1) * P], w_turned[:], start=True,
                      stop=True).then_inc(spread_ps, 1)

        def down_chunk(n, i):
            c = ORDER1[i]
            wait(pe, hid_hi_ok, n * C1 + i + 1)
            wait(pe, hid_lo_ok, n * C1 + i + 1)
            if i == 0:
                wait(pe, x2_ok, n * 2)
            f = slice(0, F1C[c])
            for j in range(TT):
                t = slice(j * P, (j + 1) * P)
                pe.matmul(acc[:, j, :], hid_hi[f, i % 2, t], dn_hi[f, c, :], start=(i == 0 and j % 2 == 0), stop=False,
                          skip_group_check=True)
                pe.matmul(acc[:, j, :], hid_lo[f, i % 2, t], dn_hi[f, c, :], start=False, stop=False,
                          skip_group_check=True)
                ins = pe.matmul(acc[:, j, :], hid_hi[f, i % 2, t], dn_lo[f, c, :], start=False, stop=(i == C1 - 1),
                                skip_group_check=True)
            ins.then_inc(down_ok, 1)

        wait(pe, ident_bf_ok, 1)
        pe.sem_inc(xt_ps, KD)
        pe.sem_inc(logits_ok, 1)

        def body(n, par, last):
            wait(pe, silu_ok, n * C1)
            wait(pe, prod_ok, n * C1)
            for c in range(NQK):
                o = slice(c * P, (c + 1) * P)
                for k in range(KD):
                    ins = split3(pe, ring[:, c, :], qkv_hi[:, k, o], qkv_lo[:, k, o], xt_hi[:, par, k, :],
                                 xt_lo[:, par, k, :], k == 0, k == KD - 1)
                ins.then_inc(qk_ps, 1)
            for h in range(2):
                wait(pe, rest_ok, n * NQK + h + 1)
                o = slice(2 * D, 3 * D)
                for jj in range(2):
                    j = 2 * h + jj
                    t, dst = slice(j * P, (j + 1) * P), ring[:, h, jj * D:(jj + 1) * D]
                    for k in range(KD):
                        pe.matmul(dst, xt_hi[:, par, k, t], qkv_hi[:, k, o], start=(jj == 0 and k == 0), stop=False,
                                  skip_group_check=True)
                        pe.matmul(dst, xt_lo[:, par, k, t], qkv_hi[:, k, o], start=False, stop=False,
                                  skip_group_check=True)
                        ins = pe.matmul(dst, xt_hi[:, par, k, t], qkv_lo[:, k, o], start=False, stop=(k == KD - 1),
                                        skip_group_check=True)
                ins.then_inc(v_ps, 1)
            for i in range(C1):
                gate_and_up(n, par, i, last)
                if i == C1 - CX:
                    wait(pe, w_ready, n + 1)
                    for j in range(TT):
                        ins = pe.transpose(turned[:, j * P:(j + 1) * P], w_parts[:, j, :], ident_bf[:])
                    ins.then_inc(turned_ps, 1)
                if i >= 2:
                    down_chunk(n, i - 2)
                for u in first_maxima(i, 2) if last else ():
                    first_maximum(u)
                if ORDER1[i] < CX:
                    spread_weights(n, ORDER1[i])
                if i in TURN_AT and not last:
                    transposes(n + 1, TURN_AT.index(i))
            down_chunk(n, C1 - 2)
            if not last:
                next_router(n + 1, 1 - par)
            else:
                first_maximum(HU - 2)
            down_chunk(n, C1 - 1)
            if last:
                first_maximum(HU - 1)

        steps(pe, body)

    @block.scalar
    def _(act):
        def transposed(m, par, k):
            wait(act, xt_ps, m * KD + k + 1)
            act.activation(xt_hi[:, par, k, :], misc, ACT.Copy).then_inc(xt_hi_ok, 1)

        def first_part(n, c):
            wait(act, qk_ps, n * NQK + c + 1)
            wait(act, parts_out[c], n * 16)
            act.activation(parts[:, c, 0, :], ring[:, c, :], ACT.Identity, bias=qk_bias[:, c:c + 1]).then_inc(part1, 1)

        def second_part(n, c):
            wait(act, rest_ok, n * NQK + c + 1)
            act.activation(parts[:, c, 1, :], rest[:, c % 2, :], ACT.Copy).then_inc(part2, 1)

        def silu_of(n, i):
            wait(act, gu_ps, n * 2 * C1 + 2 * i + 1)
            if i >= 2:
                wait(act, hid_hi_ok, n * C1 + i - 1)
                wait(act, hid_lo_ok, n * C1 + i - 1)
            else:
                wait(act, hid_hi_ok, n * C1)
                wait(act, hid_lo_ok, n * C1)
            f = slice(0, F1C[ORDER1[i]])
            act.activation(hid[f, i % 2, :], ring[f, banks(i), :], ACT.Silu).then_inc(silu_ok, 1)

        def hidden_high(n, i):
            wait(act, *finished(n, i))
            if i >= 2:
                wait(act, down_ok, n * C1 + i - 1)
            else:
                wait(act, down_ok, n * C1)
            f = slice(0, F1C[ORDER1[i]])
            act.activation(hid_hi[f, i % 2, :], hid[f, i % 2, :], ACT.Copy).then_inc(hid_hi_ok, 1)

        act.sem_inc(xt_hi_ok, KD)

        def body(n, par, last):
            first_part(n, 0)
            first_part(n, 1)
            for c in range(2, NQK):
                second_part(n, c - 2)
                first_part(n, c)
            second_part(n, NQK - 2)
            second_part(n, NQK - 1)
            wait(act, route, n + 1)
            act.activation(score[:], logit[:], ACT.Exp).then_inc(exp_ok, 1)
            silu_of(n, 0)
            for i in range(1, C1):
                silu_of(n, i)
                hidden_high(n, i - 1)
                if i - 1 in TURN_AT and not last:
                    transposed(n + 1, 1 - par, TURN_AT.index(i - 1))
            hidden_high(n, C1 - 1)

        steps(act, body)

    @block.gpsimd
    def _(pool):
        pool.memset(v_sb[:], 0.0).then_inc(ones_ok, 1)
        wait(pool, ones_ok, 1)
        pool.memset(v_sb[:, :, :, HD:HD + 1], 1.0).then_inc(ones_ok, 1)
        wait(pool, ones_ok, 2)

        def hidden_low(n, i):
            wait(pool, hid_hi_ok, n * C1 + i + 1)
            f = slice(0, F1C[ORDER1[i]])
            pool.tensor_tensor(hid_lo[f, i % 2, :], hid[f, i % 2, :], hid_hi[f, i % 2, :],
                               ALU.subtract).then_inc(hid_lo_ok, 1)

        def add_output_bias(n):
            wait(pool, xtok, n * TT + TT)
            for h in range(TT // 2):
                t = bass.ds(n * TT + 2 * h, 2)
                pool.tensor_tensor(x_sb[:, t, :], x_sb[:, t, :],
                                   bo_row[:].rearrange("p (o d) -> p o d", o=1).broadcast_to([P, 2, D]),
                                   ALU.add).then_inc(out_ok, 1)

        def body(n, par, last):
            for c in range(NQK):
                wait(pool, part2, n * NQK + c + 1)
                pool.tensor_tensor(parts[:, c, 2, :], rest[:, c % 2, :], parts[:, c, 1, :],
                                   ALU.subtract).then_inc(part3, 1)
            for i in range(C1):
                hidden_low(n, i)
                if i == 0:
                    add_output_bias(n)

        steps(pool, body)
        wait(pool, out_ok, 2 * NB)

    @block.sync
    def _(sp):
        def store(b, u, base):
            for c in range(NQK):
                wait(sp, part3, base * NQK + c + 1)
                dram = scratch["q_parts" if c < KD else "k_parts"]
                rows = slice((c % KD) * P, (c % KD + 1) * P)
                dst = dram[bass.ds(b, 1), :, rows, u * BLK:(u + 1) * BLK]
                sp.dma_start(dst.rearrange("b r p t -> p (b r) t"), parts[:, c, :, :]).then_inc(parts_out[c], 16)
            wait(sp, v_ok, base * 2 + 2)
            sp.dma_start(scratch["v"][bass.ds(base * TT, TT), :, :].rearrange("n p f -> p n f"),
                         v_sb[:].rearrange("p n h w -> p n (h w)")).then_inc(v_out, 16)

        with sp.Fori(0, B - 1) as b:
            for u in range(S // BLK):
                store(b, u, b * (S // BLK) + u)
        for p in parts_out:
            wait(sp, p, S // BLK * 16)
        for i, (q_part, k_part) in enumerate(SLOTS):
            for name, stack, part, n in (("q_parts", first_q, q_part, HALF), ("k_parts", first_k, k_part, S)):
                src = scratch[name][0, part, 0:HG * HD, 0:n].rearrange("(h d) t -> d h t", h=HG)
                sp.dma_start(stack[i * HD:(i + 1) * HD, :, :], src).then_inc(first_in, 16)
        for u in range(S // BLK):
            store(B - 1, u, NB - S // BLK + u)
        wait(sp, v_out, NB * 16)
        for p in parts_out:
            wait(sp, p, NB * 16)

    @block.vector
    def _(dve):
        dve.tensor_copy(ident_bf[:], ident[:]).then_inc(ident_bf_ok, 1)

        def normalised(m):
            wait(dve, xt_ps, m * KD)
            for j in range(TT):
                t = bass.ds(m * TT + j, 1)
                dve.tensor_scalar(x_tok[:, j, :], x_sb[:, t, :], rstd[:, t], shift[:, t], ALU.mult,
                                  ALU.add).then_inc(xtok, 1)

        def transposed_low(m, par, k):
            wait(dve, xt_hi_ok, m * KD + k + 1)
            dve.tensor_tensor(xt_lo[:, par, k, :], misc, xt_hi[:, par, k, :], ALU.subtract).then_inc(xt_lo_ok, 1)

        def reduce_first(u):
            wait(dve, first_ps, u + 1)
            dve.tensor_reduce(half_max[:, 0, u:u + 1], misc, AX.X, ALU.max, negate=True).then_inc(first_reduced, 1)

        def product(n, i):
            wait(dve, silu_ok, n * C1 + i + 1)
            wait(dve, gu_ps, n * 2 * C1 + 2 * i + 2)
            f = slice(0, F1C[ORDER1[i]])
            dve.tensor_tensor(hid[f, i % 2, :], hid[f, i % 2, :], ring[f, banks(i) + 1, :],
                              ALU.mult).then_inc(prod_ok, 1)

        def weigh(n, i):
            wait(dve, prod_ok, n * C1 + i + 1)
            wait(dve, spread_ps, n * CX + ORDER1[i] + 1)
            dve.tensor_tensor(hid[:, i % 2, :], hid[:, i % 2, :], spread[:, :], ALU.mult).then_inc(weighted_ok, 1)

        def ranks(chain, out_rank, values, before, n, g):
            shape = [P, TT, g, g]
            other = values[:].rearrange("p t (a j) -> p t a j", a=1).broadcast_to(shape)
            own = values[:].rearrange("p t (i a) -> p t i a", a=1).broadcast_to(shape)
            ab, eq = above[:, :, 0:g, 0:g], equal[:, :, 0:g, 0:g]
            chain(dve.tensor_tensor(ab, other, own, ALU.is_gt), needed=False)
            chain(dve.tensor_tensor(eq, other, own, ALU.is_equal))
            chain(dve.tensor_tensor(eq, eq, before[:], ALU.mult))
            chain(dve.tensor_tensor(ab, ab, eq, ALU.add))
            chain(dve.tensor_reduce(out_rank[:], ab, AX.X, ALU.add))

        ROUTE_STEPS = 22
        chained = sem("l1_route_chain")

        done = [0]

        def chain_of(n):
            def chain(ins, needed=True):
                ins.then_inc(chained, 1)
                done[0] += 1
                if needed:
                    wait(dve, chained, n * ROUTE_STEPS + done[0])
            return chain

        def wide(t):
            return t[:].rearrange("p (t a) -> p t a", a=1).broadcast_to([P, TT, NX])

        def route_groups(n):
            chain = chain_of(n)
            wait(dve, exp_ok, n + 1)
            chain(dve.tensor_reduce(total[:], score[:], AX.X, ALU.add))
            chain(dve.reciprocal(total[:], total[:]))
            chain(dve.tensor_tensor(score[:], score[:], wide(total), ALU.mult))
            pairs = score[:].rearrange("p t (g e) -> p t g e", e=2)
            chain(dve.tensor_tensor(group[:], pairs[:, :, :, 0], pairs[:, :, :, 1], ALU.max))
            ranks(chain, g_rank, group, before4, n, NX // 2)

        def route_experts(n):
            chain = chain_of(n)
            chain(dve.tensor_scalar(g_rank[:], g_rank[:], 2.0, None, ALU.is_lt))
            chain(dve.tensor_tensor(kept[:].rearrange("p t (g e) -> p t g e", e=2),
                                    score[:].rearrange("p t (g e) -> p t g e", e=2),
                                    g_rank[:].rearrange("p t (g a) -> p t g a", a=1).broadcast_to([P, TT, NX // 2, 2]),
                                    ALU.mult))
            ranks(chain, rank, kept, before8, n, NX)

        def route_weights(n):
            chain = chain_of(n)
            chain(dve.scalar_tensor_tensor(w_rest[:], rank[:], 2.0, kept[:], ALU.is_lt, ALU.mult))
            wait(dve, turned_ps, n)
            for r in range(PART):
                part = w_parts[:, :, r * LANE:r * LANE + NX]
                if r < PART - 1:
                    chain(dve.tensor_copy(part, w_rest[:]))
                    chain(dve.tensor_tensor(w_rest[:], w_rest[:], part, ALU.subtract))
                else:
                    dve.tensor_copy(part, w_rest[:]).then_inc(w_ready, 1)
            assert done[0] == ROUTE_STEPS, done[0]

        dve.sem_inc(xtok, TT)
        dve.sem_inc(xt_lo_ok, KD)

        def body(n, par, last):
            done[0] = 1
            wait(dve, logits_ok, n + 1)
            dve.tensor_reduce(top[:], logits, AX.X, ALU.max).then_inc(chained, 1)
            wait(dve, chained, n * ROUTE_STEPS + 1)
            dve.tensor_tensor(logit[:], logits, top[:].rearrange("p (t a) -> p t a", a=1).broadcast_to([P, TT, NX]),
                              ALU.subtract).then_inc(route, 1)
            for c in range(NQK):
                wait(dve, part1, n * NQK + c + 1)
                wait(dve, part3, n * NQK + c - 1)
                dve.scalar_tensor_tensor(rest[:, c % 2, :], ring[:, c, :], qk_bias[:, c:c + 1], parts[:, c, 0, :],
                                         ALU.add, ALU.subtract).then_inc(rest_ok, 1)
            for h in range(2):
                wait(dve, v_ps, n * 2 + h + 1)
                src = ring[:, h, :].rearrange("p (t h d) -> p t h d", t=2, h=H)
                if h == 0:
                    wait(dve, ones_ok, 2)
                    wait(dve, v_out, n * 16)
                dve.tensor_tensor(v_sb[:, 2 * h:2 * h + 2, :, 0:HD], src,
                                  bv_row[:].rearrange("p (o h d) -> p o h d", o=1, h=H).broadcast_to([P, 2, H, HD]),
                                  ALU.add).then_inc(v_ok, 1)
            route_groups(n)
            for i in range(C1):
                for u in first_maxima(i, 0) if last else ():
                    reduce_first(u)
                product(n, i)
                for place in (1, 2):
                    for u in first_maxima(i, place) if last else ():
                        reduce_first(u)
                if i == 0:
                    route_experts(n)
                if i == 1:
                    route_weights(n)
                if i == C1 - CX:
                    wait(dve, turned_ps, n + 1)
                    wait(dve, spread_ps, n * CX)
                    dve.tensor_copy(w_turned[:], turned).then_inc(w_turned_ok, 1)
                if ORDER1[i] < CX:
                    weigh(n, i)
                if i == TURN_AT[0] - 2 and not last:
                    normalised(n + 1)
                if i in TURN_AT and not last:
                    transposed_low(n + 1, 1 - par, TURN_AT.index(i))
            if last:
                reduce_first(HU - 2)
                reduce_first(HU - 1)
            for h in range(TT // 2):
                wait(dve, out_ok, n * 2 + 2)
                wait(dve, down_ok, n * C1 + C1)
                t = bass.ds(n * TT + 2 * h, 2)
                dve.tensor_tensor(x_sb[:, t, :], x_sb[:, t, :], acc[:, 2 * h:2 * h + 2, :], ALU.add).then_inc(x2_ok, 1)

        steps(dve, body)
        wait(dve, x2_ok, 2 * NB)


HG = 4
NHG = H // HG
NG = B * NHG
KT = S // P
HALF = S // 2
STEPS = 2 * KT
UNITS = HG * KT * 2
HU = UNITS // 2
HM = HU // 2
PER_STEP = UNITS // STEPS
LEAD = 3
ROWS = 6 * HD
SLOTS = ((0, 0), (1, 0), (2, 0), (0, 1), (1, 1), (0, 2))
TASKS = {hg: [(0, "turn", 1), (KT - LEAD, "maxima", 1), (8, "turn", 0), (STEPS - LEAD, "maxima", 0)]
         for hg in range(NHG)}
TASKS[0] += [(1, "features", (1, 0)), (2, "features", (1, 1)), (3, "project", (1, 0)), (4, "project", (1, 1))]
TASKS[NHG - 1] += [(9, "features", (0, 0)), (10, "features", (0, 1)), (11, "project", (0, 0)), (12, "project", (0, 1))]
for tasks in TASKS.values():
    tasks.sort()
CARRIED = 5
PER_BATCH = sum(len(t) for t in TASKS.values())


def unit(u):
    return u % HU // KT, u // HU * (KT // 2) + u // 2 % (KT // 2), u % 2


def bank(hg, i):
    return (hg * UNITS + i) % 3


def before(hg, i):
    at = hg * UNITS + i
    return 3 if at >= 3 else at + (NHG * UNITS - 1 - at) % 3 + 1


def task_number(b, hg, task, arg):
    before = sum(len(TASKS[g]) for g in range(hg)) + [t[1:] for t in TASKS[hg]].index((task, arg))
    return b * PER_BATCH + before + 1 - CARRIED - (1 if isinstance(b, int) and b == B else 0)


def run_layer1_attention(nc, a, scope, sem, x_sb, ident, scratch, half_max, out):
    def sb(name, shape, dt=F32):
        return scope.enter_context(nc.sbuf_tensor(name, shape, dt))

    q_stack, k_stack = (sb(n, [P, NHG, HG, S], BF16) for n in ("q_stack", "k_stack"))
    v_cur = sb("v_cur", [P, NHG, KT, HG * VW])
    probs = sb("probs", [P, 2, HG, HALF])
    o_sb = sb("o_sb", [P, HALF])
    att = sb("att", [P, KT, D])
    at_hi, at_lo = sb("at_hi", [P, KD, HALF], F32R), sb("at_lo", [P, KD, HALF], F32R)
    wo, wo_hi, wo_lo = sb("wo", [P, KD, D]), sb("wo_hi", [P, KD, D], F32R), sb("wo_lo", [P, KD, D], F32R)
    inv = sb("inv", [P, 4, HG])
    neg_max, m_rest = sb("neg_max", [P, HM]), sb("m_rest", [P, 2, HM])
    zeros, zeros_ok = sb("zeros", [P, HM]), sem("at_zeros")
    m_parts = sb("m_parts", [P, PART, HM], BF16)
    m_rows = sb("m_rows", [PART * HG, HALF], BF16)
    ident_b = sb("ident_b", [P, P], BF16)
    ps = scope.enter_context(nc.psum_tensor("ps2", [P, 8, 512], F32))
    scores, maxima, o_ps, spare = ps[:, 0:3, :], ps[:, 3:6, :], ps[:, 6, :], ps[:, 7, :]
    m_turned = spare[0:PART * HG, 0:HALF // 2].bitcast(BF16)

    qk_in = [sem(f"at_qk_in{i}") for i in range(NHG)]
    v_in = [sem(f"at_v_in{i}") for i in range(NHG)]
    names = ("at_wo_in at_wo_hi at_wo_lo at_ones at_ident at_scores_ps at_exp at_pv at_max_ps at_reduced at_min at_o_out "
             "at_spare_ps at_spare_done at_split at_m_in at_inv at_high at_out").split()
    (wo_in, wo_hi_ok, wo_lo_ok, ones_ok, ident_ok, scores_ps, exp_ok, pv_ok, max_ps, reduced, min_ok, o_out, spare_ps,
     spare_done, split_ok, m_in, inv_ok, high_ok, out_done) = (sem(n) for n in names)
    TAIL = [(task, arg) for _, task, arg in TASKS[0][:CARRIED]]
    block = scope.enter_context(nc.Block())

    def batches(eng, body):
        body(0, False)
        with eng.Fori(1, B - 1) as b:
            body(b, False)
        body(B - 1, True)

    def tasks_at(b, hg, s):
        for i, (at, task, arg) in enumerate(TASKS[hg]):
            carried = isinstance(b, int) and b == 0 and hg == 0 and i < CARRIED
            ended = isinstance(b, int) and b == B - 1 and hg == NHG - 1 and (task, arg) == ("maxima", 0)
            if at == s and not carried and not ended:
                yield task, arg

    def max_units(b, hg, s, last):
        ahead, u = divmod(PER_STEP * (s + LEAD + KT), UNITS)
        if last and hg + ahead >= NHG:
            return []
        return [(b * NHG + hg + ahead, (hg + ahead) % NHG, u + i) for i in range(PER_STEP)]

    @block.sync
    def _(sp):
        def load_qk(b, hg):
            for i, parts in enumerate(SLOTS):
                for name, stack, part in zip(("q_parts", "k_parts"), (q_stack, k_stack), parts):
                    src = scratch[name][bass.ds(b, 1), part, hg * HG * HD:(hg + 1) * HG * HD, :]
                    sp.dma_start(stack[i * HD:(i + 1) * HD, hg, :, :],
                                 src.rearrange("b (h d) t -> d (b h) t", h=HG)).then_inc(qk_in[hg], 16)

        def load_v(b, hg):
            src = scratch["v"][bass.ds(b * KT, KT), :, hg * HG * VW:(hg + 1) * HG * VW]
            sp.dma_start(v_cur[:, hg, :, :], src.rearrange("n p f -> p n f")).then_inc(v_in[hg], 16)

        def turn_maxima(number, hg, half):
            sp.wait_ge(spare_done, number + 1)
            sp.dma_start(q_stack[ROWS:ROWS + PART, hg, :, half * HALF:(half + 1) * HALF], m_rows[:]).then_inc(m_in, 16)

        load_qk(0, 0)
        turn_maxima(0, 0, 0)
        load_v(0, 0)
        load_qk(0, 1)
        sp.dma_start(wo[:], a["w_o"].rearrange("(k p) o -> p k o", p=P)).then_inc(wo_in, 16)

        def store(b, hg, half, o):
            sp.wait_ge(spare_done, task_number(b, hg, "project", (half, o)) + 1)
            t = bass.ds(b * KT + (2 * o if half == 0 else 2 * o - 4), 2)
            sp.dma_start(out.rearrange("b (n p) d -> p (b n) d", p=P)[:, t, :], x_sb[:, t, :]).then_inc(out_done, 16)

        def body(b, last):
            for hg in range(NHG):
                g = b * NHG + hg
                if not (last and hg >= NHG - 2):
                    wait(sp, scores_ps, (g - 1) * STEPS * HG)
                    load_qk(b + (hg + 2) // NHG, (hg + 2) % NHG)
                if not (last and hg == NHG - 1):
                    wait(sp, pv_ok, (g - 2) * STEPS)
                    load_v(b + (hg + 1) // NHG, (hg + 1) % NHG)
                for s in range(STEPS):
                    for task, arg in tasks_at(b, hg, s):
                        if task == "project":
                            store(b, hg, *arg)
                        if task == "maxima":
                            turn_maxima(task_number(b, hg, task, arg), hg if arg else (hg + 1) % NHG, arg)

        batches(sp, body)
        for o in range(2):
            store(B, 0, 1, o)
        sp.wait_ge(out_done, 4 * B * 16)

    @block.gpsimd
    def _(pool):
        pool.memset(zeros[:], 0.0).then_inc(zeros_ok, 1)
        pool.wait_ge(zeros_ok, 1)
        in_split = sem("at_in_split")

        def split_maxima(h):
            if not (isinstance(h, int) and h == 0):
                pool.wait_ge(scores_ps, (h - 1) * KT * HG + 1)
            pool.wait_ge(min_ok, h + 1)
            pool.tensor_tensor(m_parts[:, 0, :], neg_max[:], zeros[:], ALU.add).then_inc(in_split, 1)
            pool.wait_ge(in_split, h * 4 + 1)
            pool.tensor_tensor(m_rest[:, 0, :], neg_max[:], m_parts[:, 0, :], ALU.subtract).then_inc(in_split, 1)
            pool.wait_ge(in_split, h * 4 + 2)
            pool.tensor_tensor(m_parts[:, 1, :], m_rest[:, 0, :], zeros[:], ALU.add).then_inc(in_split, 1)
            pool.wait_ge(in_split, h * 4 + 3)
            pool.tensor_tensor(m_rest[:, 1, :], m_rest[:, 0, :], m_parts[:, 1, :], ALU.subtract).then_inc(in_split, 1)
            pool.wait_ge(in_split, h * 4 + 4)
            pool.tensor_tensor(m_parts[:, 2, :], m_rest[:, 1, :], zeros[:], ALU.add).then_inc(split_ok, 1)

        def body(b, last):
            for hg in range(NHG):
                g = b * NHG + hg
                split_maxima(2 * g + 1)
                if not (last and hg == NHG - 1):
                    split_maxima(2 * g + 2)

        split_maxima(0)
        pool.wait_ge(split_ok, 1)
        pool.memset(k_stack[ROWS:P, 1:NHG, :, :], 1.0).then_inc(ones_ok, 1)
        pool.wait_ge(ones_ok, 2)
        batches(pool, body)

    @block.tensor
    def _(pe):
        def score_block(b, hg, t, s, j):
            if s == 0 and j == 0:
                pe.wait_ge(qk_in[hg], (b + 1) * 2 * len(SLOTS) * 16)
            if s % KT == 0 and j == 0:
                pe.wait_ge(m_in, ((b * NHG + hg) * 2 + s // KT + 1) * 16)
            i = s * HG + j
            wait(pe, exp_ok, HG * t + j - before(hg, i) + 1)
            half, kt = s // KT, s % KT
            pe.matmul(scores[:, bank(hg, i), :], k_stack[0:ROWS + PART, hg, j, kt * P:(kt + 1) * P],
                      q_stack[0:ROWS + PART, hg, j, half * HALF:(half + 1) * HALF], start=True,
                      stop=True).then_inc(scores_ps, 1)

        def max_block(g, hg, u):
            j, qt, kh = unit(u)
            wait(pe, reduced, g * UNITS + u - before(hg, u) + 1)
            pe.matmul(maxima[:, bank(hg, u), :], q_stack[0:ROWS, hg, j, qt * P:(qt + 1) * P],
                      k_stack[0:ROWS, hg, j, kh * HALF:(kh + 1) * HALF], start=True, stop=True).then_inc(max_ps, 1)

        def weighted_values(b, hg, t, s):
            half, kt = s // KT, s % KT
            if s == 0:
                pe.wait_ge(v_in[hg], (b + 1) * 16)
            if kt == 0:
                wait(pe, o_out, (b * NHG + hg) * 2 + half)
            pe.wait_ge(exp_ok, HG * (t + 1))
            for j in range(HG):
                ins = pe.matmul(o_ps[32 * j:32 * j + VW, :], v_cur[:, hg, kt, j * VW:(j + 1) * VW],
                                probs[:, s % 2, j, :], start=(kt == 0), stop=(kt == KT - 1))
            ins.then_inc(pv_ok, 1)

        def turned_maxima():
            columns = m_parts[:].rearrange("p r (j q) -> p (r j) q", j=HG)
            for q in range(KT // 2):
                ins = pe.transpose(m_turned[:, q * P:(q + 1) * P], columns[:, :, q], ident_b[:])
            return ins

        def spare_task(n, b, hg, task, arg):
            wait(pe, spare_done, n)
            if task == "turn":
                done = (b * NHG + hg) * 2 + (1 if arg == 0 else 0)
                pe.wait_ge(o_out, done)
                for t in range(4):
                    ins = pe.transpose(spare[:, t * P:(t + 1) * P], o_sb[:, t * P:(t + 1) * P], ident[:])
            elif task == "maxima":
                pe.wait_ge(split_ok, (b * NHG + hg) * 2 + (2 if arg else 3))
                ins = turned_maxima()
            elif task == "features":
                half, k = arg
                for t in range(4):
                    ins = pe.transpose(spare[:, t * P:(t + 1) * P], att[:, 4 * half + t, k * P:(k + 1) * P], ident[:])
            else:
                half, o = arg
                pe.wait_ge(wo_lo_ok, 1)
                for tt in range(2):
                    t, dst = slice((2 * o + tt) * P, (2 * o + tt + 1) * P), spare[:, tt * D:(tt + 1) * D]
                    for k in range(KD):
                        pe.matmul(dst, at_hi[:, k, t], wo_hi[:, k, :], start=(tt == 0 and k == 0), stop=False,
                                  skip_group_check=True)
                        pe.matmul(dst, at_lo[:, k, t], wo_hi[:, k, :], start=False, stop=False, skip_group_check=True)
                        ins = pe.matmul(dst, at_hi[:, k, t], wo_lo[:, k, :], start=False, stop=(k == KD - 1),
                                        skip_group_check=True)
            ins.then_inc(spare_ps, 1)

        pe.wait_ge(ident_ok, 1)
        pe.sem_inc(max_ps, HU)
        pe.wait_ge(split_ok, 1)
        turned_maxima().then_inc(spare_ps, 1)
        pe.wait_ge(qk_in[0], 2 * len(SLOTS) * 16)
        for u in range(HU, HU + PER_STEP * (LEAD - 1)):
            max_block(0, 0, u)
        pe.wait_ge(ones_ok, 2)
        for j in range(HG):
            score_block(0, 0, 0, 0, j)
            max_block(0, 0, HU + PER_STEP * (LEAD - 1) + j)

        def body(b, last):
            for hg in range(NHG):
                g = b * NHG + hg
                for s in range(STEPS):
                    t = g * STEPS + s
                    units = max_units(b, hg, s, last)

                    if units and units[0][2] == 0:
                        pe.wait_ge(qk_in[units[0][1]], (b + (hg + 1) // NHG + 1) * 2 * len(SLOTS) * 16)
                    for j in range(HG):
                        if s < STEPS - 1:
                            score_block(b, hg, t + 1, s + 1, j)
                        elif not (last and hg == NHG - 1):
                            score_block(b + (hg + 1) // NHG, (hg + 1) % NHG, t + 1, 0, j)
                        if units:
                            max_block(*units[j])
                    weighted_values(b, hg, t, s)
                    for task, arg in tasks_at(b, hg, s):
                        spare_task(task_number(b, hg, task, arg), b, hg, task, arg)

        batches(pe, body)
        for task, arg in TAIL:
            spare_task(task_number(B, 0, task, arg), B, 0, task, arg)

    @block.scalar
    def _(act):
        def exponentials(hg, t, s):
            for j in range(HG):
                act.wait_ge(scores_ps, HG * t + j + 1)
                wait(act, pv_ok, t - 1)
                act.activation(probs[:, s % 2, j, :], scores[:, bank(hg, s * HG + j), :], ACT.Exp,
                               scale=1.0 / HD ** 0.5).then_inc(exp_ok, 1)

        def take_out(b, hg, half):
            h = (b * NHG + hg) * 2 + (0 if half == 0 else -1)
            act.wait_ge(pv_ok, (h + 1) * KT)
            if half == 0:
                if not (isinstance(b, int) and b == 0 and hg == 0):
                    act.wait_ge(spare_ps, task_number(b, hg, "turn", 1) + 1)
            else:
                before = (b, hg - 1) if hg else (b - 1, NHG - 1)
                act.wait_ge(spare_ps, task_number(*before, "turn", 0) + 1)
            act.activation(o_sb[:], o_ps[:], ACT.Copy).then_inc(o_out, 1)

        def high(n, arg):
            act.wait_ge(spare_ps, n + 1)
            act.activation(at_hi[:, arg[1], :], spare[:, :], ACT.Copy).then_inc(high_ok, 1)

        def maxima_out(h, n):
            act.wait_ge(spare_ps, n + 1)
            wait(act, m_in, h * 16)
            act.activation(m_rows[:], m_turned, ACT.Copy).then_inc(spare_done, 1)

        maxima_out(0, 0)

        def body(b, last):
            for hg in range(NHG):
                g = b * NHG + hg
                for s in range(STEPS):
                    exponentials(hg, g * STEPS + s, s)
                    if isinstance(b, int) and (b, hg, s) == (0, 0, 1):
                        act.wait_ge(wo_in, 16)
                        act.activation(wo_hi[:], wo[:], ACT.Copy).then_inc(wo_hi_ok, 1)
                    if s == KT:
                        take_out(b, hg, 0)
                    if s == 0 and not (isinstance(b, int) and b == 0 and hg == 0):
                        take_out(b, hg, 1)
                    for task, arg in tasks_at(b, hg, s - 1):
                        if task == "features":
                            high(task_number(b, hg, task, arg), arg)
                        if task == "maxima":
                            maxima_out(2 * g + (1 if arg else 2), task_number(b, hg, task, arg))

        batches(act, body)
        take_out(B, 0, 1)
        for task, arg in TAIL:
            if task == "features":
                high(task_number(B, 0, task, arg), arg)

    @block.vector
    def _(dve):
        dve.tensor_copy(ident_b[:], ident[:]).then_inc(ident_ok, 1)

        def reduce_block(g, hg, u):
            dve.wait_ge(max_ps, g * UNITS + u + 1)
            dve.tensor_reduce(half_max[:, u // HU, u % HU:u % HU + 1], maxima[:, bank(hg, u), :], AX.X, ALU.max,
                              negate=True).then_inc(reduced, 1)

        def spare_task(n, b, hg, task, arg):
            dve.wait_ge(spare_ps, n + 1)
            if task == "turn":
                h = (b * NHG + hg) * 2 + (0 if arg == 0 else -1)
                src = spare[:, :].rearrange("p (t j w) -> p t j w", t=4, j=HG)
                dve.reciprocal(inv[:], src[:, :, :, HD]).then_inc(inv_ok, 1)
                dve.wait_ge(inv_ok, h + 1)
                g = hg if arg == 0 else (hg - 1) % NHG
                half = arg
                dst = att[:, 4 * half:4 * half + 4, g * HG * HD:(g + 1) * HG * HD]
                dve.tensor_tensor(dst.rearrange("p t (j d) -> p t j d", j=HG), src[:, :, :, 0:HD],
                                  inv[:].rearrange("p t (j o) -> p t j o", o=1).broadcast_to([P, 4, HG, HD]),
                                  ALU.mult).then_inc(spare_done, 1)
            elif task == "features":
                half, k = arg
                dve.wait_ge(high_ok, 4 * b + 2 * half + k + 1 - (4 if half else 0))
                dve.tensor_tensor(at_lo[:, k, :], spare[:, :], at_hi[:, k, :], ALU.subtract).then_inc(spare_done, 1)
            else:
                half, o = arg
                tile = bass.ds(b * KT + 4 * half - (KT if half else 0) + 2 * o, 2)
                dve.tensor_tensor(x_sb[:, tile, :], x_sb[:, tile, :],
                                  spare[:, :].rearrange("p (t d) -> p t d", t=2), ALU.add).then_inc(spare_done, 1)

        def whole_maxima(h, parity):
            halves = half_max[:, parity, :].rearrange("p (n k) -> p n k", k=2)
            wait(dve, split_ok, h)
            dve.wait_ge(reduced, (h + 1) * HU)
            dve.tensor_tensor(neg_max[:], halves[:, :, 0], halves[:, :, 1], ALU.min).then_inc(min_ok, 1)

        dve.sem_inc(reduced, HU)
        whole_maxima(0, 0)
        dve.memset(k_stack[ROWS:P, 0, :, :], 1.0).then_inc(ones_ok, 1)
        for u in range(HU, HU + PER_STEP * LEAD):
            reduce_block(0, 0, u)

        def body(b, last):
            for hg in range(NHG):
                g = b * NHG + hg
                for s in range(STEPS):
                    if isinstance(b, int) and (b, hg, s) == (0, 0, 4):
                        dve.wait_ge(wo_hi_ok, 1)
                        dve.tensor_tensor(wo_lo[:], wo[:], wo_hi[:], ALU.subtract).then_inc(wo_lo_ok, 1)
                    if s == KT - LEAD:
                        whole_maxima(2 * g + 1, 1)
                    if s == STEPS - LEAD and not (last and hg == NHG - 1):
                        whole_maxima(2 * g + 2, 0)
                    for unit_of in max_units(b, hg, s, last):
                        reduce_block(*unit_of)
                    for task, arg in tasks_at(b, hg, s):
                        if task != "maxima":
                            spare_task(task_number(b, hg, task, arg), b, hg, task, arg)

        batches(dve, body)
        for task, arg in TAIL:
            spare_task(task_number(B, 0, task, arg), B, 0, task, arg)


_T = {"L0_attn_Wq": "Wq", "L0_attn_Wk": "Wk", "L0_attn_Wv": "Wv", "L0_attn_Wqa": "Wqa", "L0_attn_Wka": "Wka",
      "L0_ffn_gate_idx": "gate_idx", "L0_ffn_up_idx": "up_idx", "L0_ffn_down_idx": "down_idx",
      "L1_attn_w_qkv": "w_qkv", "L1_attn_w_o": "w_o", "L1_ffn_gate_weight": "router", "L1_ffn_gate_w": "gate_w",
      "L1_ffn_up_w": "up_w", "L1_ffn_down_w": "down_w", "L1_ffn_sh_gate_w": "sh_gate", "L1_ffn_sh_up_w": "sh_up",
      "L1_ffn_sh_down_w": "sh_down"}
_COLUMNS = {"L0_attn_bq": "bq", "L0_attn_bk": "bk", "L0_attn_bv": "bv", "L0_attn_bqa": "bqa", "L0_attn_bka": "bka",
            "L0_attn_ln_g": "ln_g", "L0_attn_ln_b": "ln_b", "L1_attn_b_qkv": "b_qkv"}
_ROWS = {"L0_ffn_lut": "lut", "L1_attn_b_qkv": "b_qkv_row", "L1_attn_b_o": "b_o"}


def lay_out(inputs):
    import numpy as _np

    laid = {"x": _np.ascontiguousarray(inputs["L0_attn_hidden_states"]).reshape(B * S, D)}
    for name, short in _T.items():
        laid[short] = _np.ascontiguousarray(_np.swapaxes(_np.asarray(inputs[name]), -1, -2))
    for name, short in _COLUMNS.items():
        laid[short] = _np.ascontiguousarray(_np.asarray(inputs[name]).reshape(-1, P).T)
    for name, short in _ROWS.items():
        laid[short] = _np.ascontiguousarray(inputs[name])
    return laid


def kernel(**inputs):
    import concourse.bacc as _bacc
    from concourse.bass_utils import run_bass_kernel_spmd as _run

    laid = lay_out(inputs)
    nc = _bacc.Bacc("TRN2", target_bir_lowering=False, num_devices=1)
    a = {n: nc.dram_tensor(f"in_{n}", v.shape, mybir.dt.from_np(v.dtype), kind="ExternalInput").ap()
         for n, v in laid.items()}
    out = nc.dram_tensor("out_0", (B, S, D), F32, kind="ExternalOutput").ap()
    build(nc, a, out)
    r = _run(nc, [{f"in_{n}": v for n, v in laid.items()}], core_ids=[0])
    return r.results[0]["out_0"]
```
